# Optimizing a Trainium2 kernel written in Bass

```python
import numpy as np
import jax
import jax.numpy as jnp

def _softmax(x, axis=-1):
    return jax.nn.softmax(x, axis=axis)

def _gelu(x):
    return jax.nn.gelu(x, approximate=True)

def _silu(x):
    return jax.nn.silu(x)

def _sigmoid(x):
    return jax.nn.sigmoid(x)

def _layernorm(x, axis=-1, eps=1e-05):
    m = jnp.mean(x, axis=axis, keepdims=True)
    v = jnp.var(x, axis=axis, keepdims=True)
    return (x - m) / jnp.sqrt(v + eps)

def _scatter_add(tgt, idx, src, axis=0):
    return tgt.at[idx].add(src)

def _segment_sum(src, seg, n):
    return jax.ops.segment_sum(src, seg, n)
kernel_name = 'mk_xattn_ffn_d2_seqx_r8_87b434'

def setup_inputs(seed: int=0):
    np.random.seed(seed)
    _w = jnp.asarray

    def _rec_inputs():
        import jax
        import jax.numpy as jnp
        _rk = jax.random.key(seed)
        x = -0.0003929 + 0.9999 * jax.random.normal(jax.random.fold_in(_rk, 1), (32, 64, 512), jnp.float32)
        _lenS = 64 - jax.random.randint(jax.random.fold_in(_rk, 7), (32,), 0, max(1, 64 // 4) + 1, jnp.int32)
        _lenS2 = 64 - jax.random.randint(jax.random.fold_in(_rk, 8), (32,), 0, max(1, 64 // 4) + 1, jnp.int32)
        _ctx_4096P = jax.random.normal(jax.random.fold_in(_rk, 11), (32, 16, 512), jnp.float32)
        _ctx_4096c = jax.random.dirichlet(jax.random.fold_in(_rk, 511), 0.3 * jnp.ones((16,), jnp.float32), (32, 64))
        _ctx_4096t = jnp.einsum('bsk,bkd->bsd', _ctx_4096c, _ctx_4096P)
        _ctx_4096t = _ctx_4096t * jax.lax.rsqrt(jnp.mean(jnp.square(_ctx_4096t)) + 1e-12) * 0.953939
        ctx_4096 = 2.81802e-05 + 1.00001 * (_ctx_4096t + 0.3 * jax.random.normal(jax.random.fold_in(_rk, 611), (32, 64, 512), jnp.float32))
        return (x, ctx_4096)
    x, ctx_4096 = _rec_inputs()

    def _L0_xattn_setup():
        import jax, jax.numpy as jnp
        import numpy as np
        HID = 512
        NHEAD = 32
        NKV = 8
        HDIM = 128
        G = NHEAD // NKV
        key = jax.random.key(seed)
        ks = jax.random.split(key, 6)
        s = 0.02
        B, L = (2, 256)
        return {'query': jax.random.normal(ks[0], (B, L, HID), jnp.float32), 'kv': jax.random.normal(ks[1], (B, L, HID), jnp.float32), 'Wq': jax.random.normal(ks[2], (HID, NHEAD * HDIM), jnp.float32) * s, 'bq': jnp.zeros((NHEAD * HDIM,), jnp.float32), 'Wkv': jax.random.normal(ks[3], (HID, 2 * NKV * HDIM), jnp.float32) * s, 'bkv': jnp.zeros((2 * NKV * HDIM,), jnp.float32), 'Wo': jax.random.normal(ks[4], (NHEAD * HDIM, HID), jnp.float32) * s, 'bo': jnp.zeros((HID,), jnp.float32)}
    _L0_xattn_all = _L0_xattn_setup()
    _L0_xattn_in = {k: v for k, v in _L0_xattn_all.items() if k in ('Wq', 'bq', 'Wkv', 'bkv', 'Wo', 'bo')}
    del _L0_xattn_all

    def _L0_ffn_setup():
        import jax, jax.numpy as jnp
        import numpy as np
        HID, INT, LAT, NE, K = (512, 1024, 256, 8, 2)
        LN_EPS = 1e-05

        def _layernorm(x, gamma, beta):
            mu = jnp.mean(x, axis=-1, keepdims=True)
            var = jnp.var(x, axis=-1, keepdims=True)
            return (x - mu) * jax.lax.rsqrt(var + LN_EPS) * gamma + beta
        key = jax.random.key(seed)
        ks = jax.random.split(key, 8)
        s = lambda d: 1.0 / np.sqrt(d)
        return {'hidden_states': jax.random.normal(ks[0], (4, 256, HID), jnp.float32), 'gate_w': jax.random.normal(ks[1], (HID, NE), jnp.float32) * s(HID), 'up_w': jax.random.normal(ks[2], (HID, INT), jnp.float32) * s(HID), 'down_w': jax.random.normal(ks[3], (INT, HID), jnp.float32) * s(INT), 'fc1_w': jax.random.normal(ks[4], (HID, LAT), jnp.float32) * s(HID), 'fc2_w': jax.random.normal(ks[5], (LAT, HID), jnp.float32) * s(LAT), 'expert_w': jax.random.normal(ks[6], (LAT, LAT), jnp.float32), 'ln_gamma': jnp.ones((HID,), jnp.float32), 'ln_beta': jnp.zeros((HID,), jnp.float32)}
    _L0_ffn_all = _L0_ffn_setup()
    _L0_ffn_in = {k: v for k, v in _L0_ffn_all.items() if k in ('gate_w', 'up_w', 'down_w', 'fc1_w', 'fc2_w', 'expert_w', 'ln_gamma', 'ln_beta')}
    del _L0_ffn_all

    def _L1_xattn_setup():
        import jax, jax.numpy as jnp
        import numpy as np
        HIDDEN = 512
        N_HEADS = 32
        N_KV_HEADS = 8
        HEAD_DIM = HIDDEN // N_HEADS
        N_REP = N_HEADS // N_KV_HEADS
        EPS = 1e-05

        def _rmsnorm(x, w):
            xf = x.astype(jnp.float32)
            var = jnp.mean(xf * xf, axis=-1, keepdims=True)
            return (xf * jax.lax.rsqrt(var + EPS)).astype(x.dtype) * w
        key = jax.random.key(seed)
        ks = jax.random.split(key, 7)
        B, Q, K = (2, 128, 256)
        scale = 0.02
        return {'hidden_states': jax.random.normal(ks[0], (B, Q, HIDDEN), jnp.float32), 'encoder_hidden_states': jax.random.normal(ks[1], (B, K, HIDDEN), jnp.float32), 'wq': jax.random.normal(ks[2], (N_HEADS * HEAD_DIM, HIDDEN), jnp.float32) * scale, 'wk': jax.random.normal(ks[3], (N_KV_HEADS * HEAD_DIM, HIDDEN), jnp.float32) * scale, 'wv': jax.random.normal(ks[4], (N_KV_HEADS * HEAD_DIM, HIDDEN), jnp.float32) * scale, 'wo': jax.random.normal(ks[5], (HIDDEN, N_HEADS * HEAD_DIM), jnp.float32) * scale, 'ln_w': jnp.ones((HIDDEN,), jnp.float32)}
    _L1_xattn_all = _L1_xattn_setup()
    _L1_xattn_in = {k: v for k, v in _L1_xattn_all.items() if k in ('wq', 'wk', 'wv', 'wo', 'ln_w')}
    del _L1_xattn_all

    def _L1_ffn_setup():
        import jax, jax.numpy as jnp
        import numpy as np
        TOP_K = 2
        key = jax.random.key(seed)
        k0, k1, k2 = jax.random.split(key, 3)
        B, S, D, H, E = (4, 256, 512, 512, 8)
        sc = 1.0 / np.sqrt(D).astype(np.float32)
        x = jax.random.normal(k0, (B, S, D), dtype=jnp.float32)
        W_gate = jax.random.normal(k1, (D, E), dtype=jnp.float32) * sc
        b_gate = jnp.zeros((E,), dtype=jnp.float32)
        W_e = jax.random.normal(k2, (E, D, H), dtype=jnp.float32) * sc
        b_e = jnp.zeros((E, H), dtype=jnp.float32)
        return {'x': x, 'W_gate': W_gate, 'b_gate': b_gate, 'W_e': W_e, 'b_e': b_e}
    _L1_ffn_all = _L1_ffn_setup()
    _L1_ffn_in = {k: v for k, v in _L1_ffn_all.items() if k in ('W_gate', 'b_gate', 'W_e', 'b_e')}
    del _L1_ffn_all
    return {'x': x, 'ctx_4096': ctx_4096, 'L0_xattn_Wq': _L0_xattn_in['Wq'], 'L0_xattn_bq': _L0_xattn_in['bq'], 'L0_xattn_Wkv': _L0_xattn_in['Wkv'], 'L0_xattn_bkv': _L0_xattn_in['bkv'], 'L0_xattn_Wo': _L0_xattn_in['Wo'], 'L0_xattn_bo': _L0_xattn_in['bo'], 'L0_ffn_gate_w': _L0_ffn_in['gate_w'], 'L0_ffn_up_w': _L0_ffn_in['up_w'], 'L0_ffn_down_w': _L0_ffn_in['down_w'], 'L0_ffn_fc1_w': _L0_ffn_in['fc1_w'], 'L0_ffn_fc2_w': _L0_ffn_in['fc2_w'], 'L0_ffn_expert_w': _L0_ffn_in['expert_w'], 'L0_ffn_ln_gamma': _L0_ffn_in['ln_gamma'], 'L0_ffn_ln_beta': _L0_ffn_in['ln_beta'], 'L1_xattn_wq': _L1_xattn_in['wq'], 'L1_xattn_wk': _L1_xattn_in['wk'], 'L1_xattn_wv': _L1_xattn_in['wv'], 'L1_xattn_wo': _L1_xattn_in['wo'], 'L1_xattn_ln_w': _L1_xattn_in['ln_w'], 'L1_ffn_W_gate': _L1_ffn_in['W_gate'], 'L1_ffn_b_gate': _L1_ffn_in['b_gate'], 'L1_ffn_W_e': _L1_ffn_in['W_e'], 'L1_ffn_b_e': _L1_ffn_in['b_e']}

def reference(x, ctx_4096, L0_xattn_Wq, L0_xattn_bq, L0_xattn_Wkv, L0_xattn_bkv, L0_xattn_Wo, L0_xattn_bo, L0_ffn_gate_w, L0_ffn_up_w, L0_ffn_down_w, L0_ffn_fc1_w, L0_ffn_fc2_w, L0_ffn_expert_w, L0_ffn_ln_gamma, L0_ffn_ln_beta, L1_xattn_wq, L1_xattn_wk, L1_xattn_wv, L1_xattn_wo, L1_xattn_ln_w, L1_ffn_W_gate, L1_ffn_b_gate, L1_ffn_W_e, L1_ffn_b_e):
    import jax
    import jax.numpy as jnp

    def _L0_xattn_ref(query, kv, Wq, bq, Wkv, bkv, Wo, bo):
        import jax, jax.numpy as jnp
        import numpy as np
        HID = 512
        NHEAD = 32
        NKV = 8
        HDIM = 128
        G = NHEAD // NKV
        B, L, _ = query.shape
        Lk = kv.shape[1]
        scale = jnp.asarray(1.0 / np.sqrt(HDIM), query.dtype)
        q = (query @ Wq + bq).reshape(B, L, NKV, G, HDIM)
        k_, v_ = jnp.split(kv @ Wkv + bkv, 2, axis=-1)
        k = k_.reshape(B, Lk, NKV, HDIM)
        v = v_.reshape(B, Lk, NKV, HDIM)
        scores = jnp.einsum('blkgd,bmkd->bkglm', q, k) * scale
        attn = jax.nn.softmax(scores, axis=-1)
        o = jnp.einsum('bkglm,bmkd->blkgd', attn, v).reshape(B, L, NHEAD * HDIM)
        return o @ Wo + bo

    def _L0_ffn_ref(hidden_states, gate_w, up_w, down_w, fc1_w, fc2_w, expert_w, ln_gamma, ln_beta):
        import jax, jax.numpy as jnp
        import numpy as np
        HID, INT, LAT, NE, K = (512, 1024, 256, 8, 2)
        LN_EPS = 1e-05

        def _layernorm(x, gamma, beta):
            mu = jnp.mean(x, axis=-1, keepdims=True)
            var = jnp.var(x, axis=-1, keepdims=True)
            return (x - mu) * jax.lax.rsqrt(var + LN_EPS) * gamma + beta
        logits = jnp.einsum('bsh,he->bse', hidden_states, gate_w)
        routing_weights, selected_experts = jax.lax.top_k(logits, K)
        h = jax.nn.relu(jnp.einsum('bsh,hi->bsi', hidden_states, up_w)) ** 2
        shared_out = jnp.einsum('bsi,ih->bsh', h, down_w)
        x_latent = jnp.einsum('bsh,hl->bsl', hidden_states, fc1_w)
        expert_out = jnp.einsum('bsl,lm->bsm', x_latent, expert_w)
        moe_out = expert_out * jnp.sum(routing_weights, axis=-1, keepdims=True)
        routed_out = jnp.einsum('bsl,lh->bsh', moe_out, fc2_w)
        return _layernorm(shared_out + routed_out, ln_gamma, ln_beta)

    def _L1_xattn_ref(hidden_states, encoder_hidden_states, wq, wk, wv, wo, ln_w):
        import jax, jax.numpy as jnp
        import numpy as np
        HIDDEN = 512
        N_HEADS = 32
        N_KV_HEADS = 8
        HEAD_DIM = HIDDEN // N_HEADS
        N_REP = N_HEADS // N_KV_HEADS
        EPS = 1e-05

        def _rmsnorm(x, w):
            xf = x.astype(jnp.float32)
            var = jnp.mean(xf * xf, axis=-1, keepdims=True)
            return (xf * jax.lax.rsqrt(var + EPS)).astype(x.dtype) * w
        B, Qlen, _ = hidden_states.shape
        _, Klen, _ = encoder_hidden_states.shape
        x = _rmsnorm(hidden_states, ln_w)
        q = jnp.einsum('bqd,hd->bqh', x, wq).reshape(B, Qlen, N_HEADS, HEAD_DIM)
        k = jnp.einsum('bkd,hd->bkh', encoder_hidden_states, wk).reshape(B, Klen, N_KV_HEADS, HEAD_DIM)
        v = jnp.einsum('bkd,hd->bkh', encoder_hidden_states, wv).reshape(B, Klen, N_KV_HEADS, HEAD_DIM)
        q = q.transpose(0, 2, 1, 3)
        k = k.transpose(0, 2, 1, 3)
        v = v.transpose(0, 2, 1, 3)
        k = jnp.repeat(k, N_REP, axis=1)
        v = jnp.repeat(v, N_REP, axis=1)
        scores = jnp.einsum('bhqd,bhkd->bhqk', q, k) / np.sqrt(HEAD_DIM).astype(np.float32)
        attn = jax.nn.softmax(scores.astype(jnp.float32), axis=-1).astype(q.dtype)
        out = jnp.einsum('bhqk,bhkd->bhqd', attn, v)
        out = out.transpose(0, 2, 1, 3).reshape(B, Qlen, HIDDEN)
        return jnp.einsum('bqh,dh->bqd', out, wo)

    def _L1_ffn_ref(x, W_gate, b_gate, W_e, b_e):
        import jax, jax.numpy as jnp
        import numpy as np
        TOP_K = 2
        logits = x @ W_gate + b_gate
        _, top_idx = jax.lax.top_k(logits, TOP_K)
        y_all = jax.nn.relu(jnp.einsum('bsd,edh->bseh', x, W_e) + b_e)
        y = jnp.take_along_axis(y_all, top_idx[..., None], axis=2)
        return y.mean(axis=2)
    x = x + _L0_xattn_ref(_layernorm(x, axis=-1), ctx_4096, L0_xattn_Wq, L0_xattn_bq, L0_xattn_Wkv, L0_xattn_bkv, L0_xattn_Wo, L0_xattn_bo)
    x = x + _L0_ffn_ref(_layernorm(x, axis=-1), L0_ffn_gate_w, L0_ffn_up_w, L0_ffn_down_w, L0_ffn_fc1_w, L0_ffn_fc2_w, L0_ffn_expert_w, L0_ffn_ln_gamma, L0_ffn_ln_beta)
    x = x + _L1_xattn_ref(_layernorm(x, axis=-1), ctx_4096, L1_xattn_wq, L1_xattn_wk, L1_xattn_wv, L1_xattn_wo, L1_xattn_ln_w)
    x = x + _L1_ffn_ref(_layernorm(x, axis=-1), L1_ffn_W_gate, L1_ffn_b_gate, L1_ffn_W_e, L1_ffn_b_e)
    return x

_drawn_inputs = setup_inputs


def setup_inputs(seed=0):
    import zlib

    import numpy as np

    out = dict(_drawn_inputs(seed))
    spreads = {'L0_xattn_bq': (0.0, 0.367),
     'L0_xattn_bkv': (0.0, 0.1),
     'L0_xattn_bo': (0.0, 0.1),
     'L0_ffn_ln_gamma': (1.0, 0.2),
     'L0_ffn_ln_beta': (0.0, 0.1),
     'L1_xattn_ln_w': (1.0, 0.6),
     'L1_ffn_b_gate': (0.0, 0.1),
     'L1_ffn_b_e': (0.0, 0.1)}
    factors = {'L1_xattn_wq': 2.838}
    for name, (base, spread) in spreads.items():
        noise = np.random.default_rng([zlib.crc32(name.encode()), seed]).standard_normal(out[name].shape)
        drawn = base * np.exp(spread * noise) if base else spread * noise
        out[name] = jnp.asarray(drawn.astype(out[name].dtype))
    for name, factor in factors.items():
        out[name] = (out[name] * factor).astype(out[name].dtype)
    return out
```

```python
from contextlib import ExitStack

import concourse.bass as bass
from concourse import mybir

F32 = mybir.dt.float32
F16 = mybir.dt.float16
U32 = mybir.dt.uint32
ACT = mybir.ActivationFunctionType
ALU = mybir.AluOpType
AX = mybir.AxisListType
ds = bass.ds

P = 128
D = 512
KC = D // P
NTOK = 32 * 64
NT = NTOK // P
NC = 4
CH = NTOK // NC
TC = CH // P
BC = CH // 64
NG = 8
HG = 4
HD1 = 16
INT = 1024
LAT = 256
NE = 8
EPS = 1e-5
WS = 64.0
UN = 1.0 / WS
UN2 = UN * UN
PS = 64.0
SC0 = UN2 * P ** -0.5
SC1 = UN2 * HD1 ** -0.5
PASSES = ((0, 0), (0, 1), (1, 0))


def w(eng, sem, value):
    if not (isinstance(value, int) and value <= 0):
        eng.wait_ge(sem, value)


def build(nc, x, ctxT, wB, biasB, bo, up, down, small0, fc2, gam, bet, wq1, wkv1, wo1, lnw, we, be, bg, out):
    with ExitStack() as stack:
        def sb(name, cols, dt=F16):
            return stack.enter_context(nc.sbuf_tensor(name, [P, cols], dt))[:, :]

        def sem(name):
            return stack.enter_context(nc.semaphore(name))

        banks = [stack.enter_context(nc.psum_tensor(f"bank{i}", [P, 512], F32))[:, :] for i in range(8)]
        banks16 = [b.bitcast(F16) for b in banks]

        X = sb("X", NT * D, F32).rearrange("p (t d) -> p t d", t=NT)
        CT = sb("CT", NC * 2 * KC * CH).rearrange("p (c s k n) -> p c s k n", c=NC, s=2, k=KC)
        R1 = sb("R1", 16384)
        R2 = sb("R2", 21504)
        R3 = sb("R3", 4096, F32)
        AW = sb("AW", 10240)
        R4 = sb("R4", 13312)
        R5 = sb("R5", 1024, F32)
        xn = sb("xn", D, F32)
        ident = sb("ident", P)
        biases = sb("biases", 48, F32)
        lnwT = sb("lnwT", KC, F32)
        g0w = sb("g0w", 2 * KC * NE)
        g1w = sb("g1w", 2 * KC * NE)
        stat = sb("stat", 2 * 16, F32)
        ystat = sb("ystat", 16, F32)
        smx = sb("smx", 3 * 16, F32)
        m8 = sb("m8", TC * 8, F32)
        rsum = sb("rsum", TC, F32)
        lgt = sb("lgt", 8, F32)
        idx8 = sb("idx8", 8, U32)
        idxf = sb("idxf", 8, F32)
        msk = sb("msk", 3 * 8, F32)
        iota8 = sb("iota8", 8, F32)
        bgb = sb("bgb", 8, F32)

        def parts(region, off, k, n):
            return region[:, off:off + 2 * k * n].rearrange("p (s k n) -> p s k n", s=2, k=k)

        raw = R3.rearrange("p (s n) -> p s n", s=2)
        beb = R3.rearrange("p (e n) -> p e n", e=NE)
        xs = R4[:, 0:2048].rearrange("p (i s d) -> p i s d", i=2, s=2)
        XT = R1.rearrange("p (c s k n) -> p c s k n", c=NC, s=2, k=KC)
        GW = 10240
        WBq = [parts(R2, GW * i, KC, CH) for i in range(2)]
        WBkv = [parts(R2, GW * i + 4096, KC, 256) for i in range(2)]
        WBo = [parts(R2, GW * i + 6144, HG, D) for i in range(2)]
        qT = R4[:, 2048:6144].rearrange("p (s b h l) -> p s b h l", s=2, b=BC, h=HG)
        kT = R4[:, 6144:7168].rearrange("p (s n) -> p s n", s=2)
        V = R4[:, 7168:9216].rearrange("p (b s d) -> p b s d", b=BC, s=2)
        oT = R4[:, 9216:13312].rearrange("p (s h n) -> p s h n", s=2, h=HG)
        Eb = AW[:, 0:2048].bitcast(F32).rearrange("p (k m) -> p k m", m=64)
        PPb = AW[:, 2048:4096].rearrange("p (k s m) -> p k s m", s=2, m=64)
        PTb = AW[:, 4096:6144]
        Wup, Wfc1 = parts(R2, 0, KC, INT), parts(R2, 8192, KC, LAT)
        Wdn, Wex, Wfc2 = parts(R2, 10240, INT // P, D), parts(R2, 18432, LAT // P, LAT), parts(R2, 19456, LAT // P, D)
        Wg0, Wg1 = parts(g0w, 0, KC, NE), parts(g1w, 0, KC, NE)
        T1 = parts(R4, 2048, KC, CH)
        xlT, eoT = parts(R4, 6144, 2, CH), parts(R4, 8192, 2, CH)
        rel = R4[:, 10240:12288].bitcast(F32).rearrange("p (i n) -> p i n", i=2)
        h32 = R4[:, 12288:13312].bitcast(F32)
        hT = parts(R1, 8192, INT // P, CH)
        gamb, betb = R5[:, 0:D], R5[:, D:2 * D]
        bob = R5[:, 0:D]
        We = [parts(R1 if e < 4 else R2, 4096 * (e % 4), KC, D) for e in range(NE)]
        Wq1, Wkv1, Wo1 = parts(AW, 0, KC, D), parts(AW, 4096, KC, 256), parts(AW, 6144, 4, D)
        TA, TF = parts(R4, 2048, KC, P), parts(R4, 3072, KC, P)
        qs = R4[:, 4096:6144].rearrange("p (h s d) -> p h s d", h=32, s=4)
        PT1 = R4[:, 4096:6144]
        ks = R4[:, 6144:7168].rearrange("p (g j s d) -> p g j s d", g=NG, j=2, s=4)
        qT1 = R4[:, 7168:9216].rearrange("p (b t l) -> p b t l", b=2, t=16)
        kT1 = R4[:, 9216:10240].rearrange("p (g n) -> p g n", g=NG)
        V1 = R4[:, 10240:10752].rearrange("p (b s n) -> p b s n", b=2, s=2)
        E1 = R4[:, 10752:12800].bitcast(F32).rearrange("p (k m) -> p k m", m=64)
        on32 = R4[:, 12800:13312].bitcast(F32)
        PP1 = R2[:, 16384:18432].rearrange("p (k s m) -> p k s m", s=2, m=64)
        tmp = R2[:, 18432:20480].bitcast(F32).rearrange("p (i n) -> p i n", i=2)
        acc = R2[:, 20480:21504].bitcast(F32)
        onh = R5[:, 0:512].bitcast(F16).rearrange("p (b s n) -> p b s n", b=2, s=2)
        oT1 = R5[:, 512:1024].bitcast(F16).rearrange("p (s u n) -> p s u n", s=4, u=2)

        raw_in = [sem("raw_in0"), sem("raw_in1")]
        x_in, const_in, gb_in, be_in, out_done = sem("x_in"), sem("const_in"), sem("gb_in"), sem("be_in"), sem("out_done")
        w_scaled, w_hi, w_lo = sem("w_scaled"), sem("w_hi"), sem("w_lo")
        id_zero, id_ready, bias_ready, bo_added = sem("id_zero"), sem("id_ready"), sem("bias_ready"), sem("bo_added")
        n_bn, n_mv, n_arg, n_ln, n_r0, n_a, n_b, n_r = (sem("n_" + s) for s in "bn mv arg ln r0 a b r".split())
        n_xn, n_hi, n_lo, n_turned, n_stored = (sem("n_" + s) for s in "xn hi lo turned stored".split())
        p_mm, p_hi, p_lo = sem("p_mm"), sem("p_hi"), sem("p_lo")
        s_mm, s_max, s_sub, s_exp, s_sum, s_rec, s_prob, s_phi, s_plo = (
            sem("s_" + s) for s in "mm max sub exp sum rec prob phi plo".split())
        t_mm, t_ev = sem("t_mm"), sem("t_ev")
        o_mm, o_hi, o_lo = sem("o_mm"), sem("o_hi"), sem("o_lo")
        y_mm, y_add = sem("y_mm"), sem("y_add")
        u_mm, u_rel, u_sq, u_hi, u_lo = (sem("u_" + s) for s in "mm rel sq hi lo".split())
        g_mm, g_top, g_sum = sem("g_mm"), sem("g_top"), sem("g_sum")
        f_mm, f_rt, f_y, f_t, f_g, f_b, f_add = (sem("f_" + s) for s in "mm rt y t g b add".split())
        y_bn, y_mv, y_arg, y_ln, y_r0, y_a, y_b, y_r = (sem("y_" + s) for s in "bn mv arg ln r0 a b r".split())
        a_q, a_qhi, a_qlo, a_kv, a_kvhi, a_klo, a_kdup = (sem("a_" + s) for s in "q qhi qlo kv kvhi klo kdup".split())
        a_tq, a_tqev, a_tk, a_tkev = (sem("a_" + s) for s in "tq tqev tk tkev".split())
        b_s, b_max, b_sub, b_exp, b_sum, b_rec, b_phi, b_plo = (
            sem("b_" + s) for s in "s max sub exp sum rec phi plo".split())
        b_t, b_tev, b_o, b_on, b_ohi, b_olo = (sem("b_" + s) for s in "t tev o on ohi olo".split())
        a_to, a_toev, a_y, a_add = (sem("a_" + s) for s in "to toev y add".split())
        r_mm, r_lg, r_top, r_idx, r_f, r_m1, r_m2, r_mask = (sem("r_" + s) for s in "mm lg top idx f m1 m2 mask".split())
        e_mm, e_bias, e_rel, e_acc, x_done = (sem(s) for s in "e_mm e_bias e_rel e_acc x_done".split())
        z_ready = sem("z_ready")
        waits_passed = sem("waits_passed")

        def alone(eng, sem_, value):
            eng.wait_ge(sem_, value)
            eng.sem_inc(waits_passed, 1)

        block = stack.enter_context(nc.Block())

        def conv_of_group(g, j):
            return 1 + j if isinstance(g, int) and g == 0 else 4 + 3 * g + j

        @block.sync
        def _(sp):
            sp.dma_start(X[:, 0:TC, :], x[0:CH, :].rearrange("(t p) d -> p t d", p=P)).then_inc(x_in, 16)

            def piece(k, src, conv_before):
                w(sp, w_lo, conv_before)
                n = src.shape[1]
                sp.dma_start(raw[:, kp(k), 0:n], src).then_inc(raw_in[kp(k)], 16)

            def kp(k):
                return k[1] if isinstance(k, tuple) else k % 2

            cuts = ((0, 2048), (2048, 3072), (3072, 5120))
            piece(0, ctxT[0], 0)
            piece(1, wB[0, :, 0:2048], 0)
            sp.dma_start(biases, biasB).then_inc(const_in, 16)
            sp.dma_start(lnwT, lnw).then_inc(const_in, 16)
            sp.dma_start(bob, bo.broadcast_to([P, D])).then_inc(const_in, 16)
            sp.dma_start(bgb, bg.broadcast_to([P, NE])).then_inc(const_in, 16)
            piece(2, wB[0, :, 2048:3072], 1)
            for c in range(1, NC):
                sp.dma_start(X[:, c * TC:(c + 1) * TC, :],
                             x[c * CH:(c + 1) * CH, :].rearrange("(t p) d -> p t d", p=P)).then_inc(x_in, 16)
            piece(3, wB[0, :, 3072:5120], 2)
            for c in range(1, NC):
                piece(3 + c, ctxT[c], 2 + c)
            for j, (a, b) in enumerate(cuts):
                piece(7 + j, wB[1, :, a:b], 6 + j)
            with sp.Fori(0, 3) as i:
                for par in range(2):
                    for j, (a, b) in enumerate(cuts):
                        k = 3 * par + j
                        piece((None, k % 2), wB[ds(i * 2 + 2 + par, 1), :, a:b].rearrange("a p n -> (a p) n"),
                              i * 6 + 9 + k)
            sp.wait_ge(bo_added, NT)
            sp.dma_start(gamb, gam.broadcast_to([P, D])).then_inc(gb_in, 16)
            sp.dma_start(betb, bet.broadcast_to([P, D])).then_inc(gb_in, 16)
            piece(28, up[:, 0:2048], 27)
            piece(29, up[:, 2048:4096], 28)
            piece(30, small0, 29)
            piece(31, down[:, 0:2048], 30)
            piece(32, down[:, 2048:4096], 33)
            piece(33, fc2, 34)
            piece(34, wq1, 35)
            piece(35, wkv1, 36)
            piece(36, wo1, 37)
            piece(37, we[0], 39)
            piece(38, we[1], 40)
            for e in range(2, NE):
                piece(37 + e, we[e], 39 + e)
            sp.wait_ge(w_lo, 48)
            sp.dma_start(R3, be.broadcast_to([P, NE * D])).then_inc(be_in, 16)
            with sp.Fori(0, NT) as n:
                sp.wait_ge(x_done, n + 1)
                sp.dma_start(out[ds(n * P, P), :], X[:, ds(n, 1), :].rearrange("p a d -> p (a d)")).then_inc(out_done, 16)
            sp.wait_ge(out_done, 16 * NT)

        @block.gpsimd
        def _(pool):
            g = nc.gpsimd
            g.memset(ident, 0.0).then_inc(id_zero, 1)
            pool.wait_ge(id_zero, 1)
            g.affine_select(out=ident, in_=ident, compare_op=ALU.not_equal, fill=1.0, base=0,
                            pattern=[[-1, P]], channel_multiplier=1).then_inc(id_ready, 1)
            g.iota(iota8, pattern=[[1, NE]], base=0, channel_multiplier=0,
                   allow_small_or_imprecise_dtypes=True).then_inc(id_ready, 1)
            pool.wait_ge(const_in, 64)
            g.tensor_scalar(biases, biases, WS, 1.0, ALU.mult, ALU.mult).then_inc(bias_ready, 1)
            pool.wait_ge(bias_ready, 1)
            pool.wait_ge(id_ready, 2)
            g.memset(V[64:P, :, 1, :], 0.0).then_inc(z_ready, 1)
            pool.wait_ge(z_ready, 1)

            def split(conv, src, hi, lo, scale=WS, row_scale=None):
                if row_scale is None:
                    g.tensor_scalar(src, src, scale, 1.0, ALU.mult, ALU.mult).then_inc(w_scaled, 1)
                else:
                    for k in range(KC):
                        last = g.tensor_scalar(src[:, k * D:(k + 1) * D], src[:, k * D:(k + 1) * D],
                                               row_scale[:, k:k + 1], scale, ALU.mult, ALU.mult)
                    last.then_inc(w_scaled, 1)
                alone(pool, w_scaled, conv + 1)
                g.tensor_scalar(hi, src, 1.0, 1.0, ALU.mult, ALU.mult).then_inc(w_hi, 1)
                pool.wait_ge(w_hi, conv + 1)
                g.tensor_tensor(lo, src, hi, ALU.subtract).then_inc(w_lo, 1)

            def halves(region, off, total, start=0, n=None):
                n = total if n is None else n
                return region[:, off + start:off + start + n], region[:, off + total + start:off + total + start + n]

            def ctx_piece(k, c):
                pool.wait_ge(raw_in[k % 2], 16 * (k // 2 + 1))
                chunk = CT[:, c].rearrange("p s k n -> p s (k n)")
                split(k, raw[:, k % 2, :], chunk[:, 0], chunk[:, 1], 1.0)

            def group_piece(k, slot, arrivals, par, j):
                alone(pool, raw_in[slot], arrivals * 16)
                off, n = ((0, 2048), (4096, 1024), (6144, 2048))[j]
                hi, lo = halves(R2, GW * par + off, n)
                split(k, raw[:, slot, 0:n], hi, lo)

            ctx_piece(0, 0)
            for j in range(3):
                group_piece(1 + j, (1 + j) % 2, (1 + j) // 2 + 1, 0, j)
            for c in range(1, NC):
                ctx_piece(3 + c, c)
            with pool.Fori(0, NT) as n:
                pool.wait_ge(n_xn, n + 1)
                xt = X[:, ds(n, 1), :].rearrange("p a d -> p (a d)")
                g.tensor_tensor(xt, xt, bob, ALU.add).then_inc(bo_added, 1)
            for j in range(3):
                group_piece(7 + j, (7 + j) % 2, (7 + j) // 2 + 1, 1, j)
            with pool.Fori(0, 3) as i:
                for par in range(2):
                    pool.wait_ge(y_mm, i * 32 + 16 * (par + 1))
                    for j in range(3):
                        k = 3 * par + j
                        group_piece(i * 6 + 10 + k, k % 2, i * 3 + 5 + k // 2 + 1, par, j)

            def landed(k):
                pool.wait_ge(raw_in[k % 2], 16 * (k // 2 + 1))

            pool.wait_ge(y_mm, 7 * 16)
            for h in range(2):
                landed(28 + h)
                split(28 + h, raw[:, h, :], *halves(R2, 0, 4096, 2048 * h, 2048))
            pool.wait_ge(y_mm, 8 * 16)
            landed(30)
            split(30, raw[:, 0, 0:1024], *halves(R2, 8192, 1024))
            split(31, raw[:, 0, 1024:1536], *halves(R2, 18432, 512))
            split(32, raw[:, 0, 1536:1568], *halves(g0w, 0, 32))
            for h in range(2):
                landed(31 + h)
                split(33 + h, raw[:, (31 + h) % 2, :], *halves(R2, 10240, 4096, 2048 * h, 2048))
            landed(33)
            split(35, raw[:, 1, 0:1024], *halves(R2, 19456, 1024))
            landed(34)
            split(36, raw[:, 0, :], *halves(AW, 0, 2048), row_scale=lnwT)
            landed(35)
            split(37, raw[:, 1, 0:1024], *halves(AW, 4096, 1024))
            split(38, raw[:, 1, 1024:1056], *halves(g1w, 0, 32))
            landed(36)
            split(39, raw[:, 0, :], *halves(AW, 6144, 2048))
            for e in range(NE):
                if e == 2:
                    pool.wait_ge(f_mm, 2 * NT)
                landed(37 + e)
                split(40 + e, raw[:, (37 + e) % 2, :], *halves(R1 if e < 4 else R2, 4096 * (e % 4), 2048))

            pool.wait_ge(f_add, NT)
            pool.wait_ge(w_lo, 48)
            g.memset(V1[64:P, :, 1, :], 0.0).then_inc(z_ready, 1)
            pool.wait_ge(z_ready, 2)
            g.memset(ks[:, :, :, 3, :], 0.0).then_inc(z_ready, 1)
            g.memset(qs[:, :, 3, :], 0.0).then_inc(z_ready, 1)

            def k_copy(n):
                alone(pool, a_klo, n + 1)
                g.tensor_copy(ks[:, :, 1, 0:3, :], ks[:, :, 0, 0:3, :]).then_inc(a_kdup, 1)

            def add_experts(n):
                for e in range(1, NE):
                    pool.wait_ge(e_rel, n * NE + e + 1)
                    if e > 1:
                        pool.wait_ge(e_acc, n * (NE - 1) + e - 1)
                    g.tensor_tensor(acc, acc, tmp[:, e % 2, :], ALU.add).then_inc(e_acc, 1)
                pool.wait_ge(e_acc, n * (NE - 1) + NE - 1)
                xt = X[:, ds(n, 1), :].rearrange("p a d -> p (a d)")
                g.tensor_tensor(xt, xt, acc, ALU.add).then_inc(x_done, 1)

            k_copy(0)
            with pool.Fori(0, NT - 1) as n:
                k_copy(n + 1)
                add_experts(n)
            add_experts(NT - 1)

        def norm_stats(dve, n, par, xt, rms=False):
            s = stat[:, 16 * par:16 * par + 16]
            nc.vector.bn_stats(s[:, 0:6], xt).then_inc(n_bn, 1)
            alone(dve, n_bn, n + 1)
            nc.vector.bn_aggr(s[:, 6:8], s[:, 0:6]).then_inc(n_mv, 1)
            dve.wait_ge(n_mv, n + 1)
            nc.vector.tensor_scalar(s[:, 8:9], s[:, 7:8], 1.0 + EPS if rms else 1.0, EPS * EPS if rms else EPS,
                                    ALU.mult, ALU.add).then_inc(n_arg, 1)

        def norm_root(act, n, par):
            s = stat[:, 16 * par:16 * par + 16]
            act.wait_ge(n_arg, n + 1)
            nc.scalar.activation(s[:, 9:10], s[:, 8:9], ACT.Ln).then_inc(n_ln, 1)
            act.wait_ge(n_ln, n + 1)
            nc.scalar.activation(s[:, 10:11], s[:, 9:10], ACT.Exp, scale=-0.5).then_inc(n_r0, 1)

        def newton(dve, s, n, sem_r0, sem_a, sem_b, sem_r):
            dve.wait_ge(sem_r0, n + 1)
            nc.vector.scalar_tensor_tensor(out=s[:, 11:12], in0=s[:, 8:9], scalar=s[:, 10:11], in1=s[:, 10:11],
                                           op0=ALU.mult, op1=ALU.mult).then_inc(sem_a, 1)
            dve.wait_ge(sem_a, n + 1)
            nc.vector.tensor_scalar(s[:, 12:13], s[:, 11:12], -0.5, 1.5, ALU.mult, ALU.add).then_inc(sem_b, 1)
            dve.wait_ge(sem_b, n + 1)
            nc.vector.tensor_tensor(s[:, 13:14], s[:, 10:11], s[:, 12:13], ALU.mult).then_inc(sem_r, 1)
            dve.wait_ge(sem_r, n + 1)

        def norm_apply(dve, n, par, xt):
            s = stat[:, 16 * par:16 * par + 16]
            newton(dve, s, n, n_r0, n_a, n_b, n_r)
            nc.vector.tensor_scalar(xn, xt, s[:, 6:7], s[:, 13:14], ALU.subtract, ALU.mult).then_inc(n_xn, 1)
            dve.wait_ge(n_hi, n + 1)
            w(dve, n_turned, n - 1)
            nc.vector.tensor_tensor(xs[:, par, 1, :], xn, xs[:, par, 0, :], ALU.subtract).then_inc(n_lo, 1)

        def norm_hi(act, n, par):
            act.wait_ge(n_xn, n + 1)
            w(act, n_turned, n - 1)
            nc.scalar.activation(xs[:, par, 0, :], xn, ACT.Copy).then_inc(n_hi, 1)

        def norm_turn(pe, n, par, bank):
            pe.wait_ge(n_lo, n + 1)
            w(pe, n_stored, n)
            for sk in range(2 * KC):
                last = pe.transpose(banks16[bank][:, sk * P:(sk + 1) * P],
                                    xs[:, par, sk // KC, (sk % KC) * P:(sk % KC + 1) * P], ident)
            last.then_inc(n_turned, 1)

        def norm_store(act, n, bank, dst):
            act.wait_ge(n_turned, n + 1)
            nc.scalar.activation(dst, banks16[bank][:, 0:2 * KC * P].rearrange("p (a n) -> p a n", a=2 * KC),
                                 ACT.Copy).then_inc(n_stored, 1)

        def x_tile(n):
            return X[:, n, :] if isinstance(n, int) else X[:, ds(n, 1), :].rearrange("p a d -> p (a d)")

        @block.tensor
        def _(pe):
            pe.wait_ge(id_ready, 1)
            for par in range(2):
                norm_turn(pe, par, par, 4 + par)
            with pe.Fori(1, NT // 2) as i:
                for par in range(2):
                    norm_turn(pe, i * 2 + par, par, 4 + par)

            def group3(dst, pairs, incs):
                m = len(pairs) * len(PASSES)
                k = 0
                for a, b in pairs:
                    for sa, sb_ in PASSES:
                        last = pe.matmul(dst, a(sa), b(sb_), start=(k == 0), stop=(k == m - 1))
                        k += 1
                if incs is not None:
                    last.then_inc(incs, 1)
                return last

            def b_proj(s, c, par, j):
                n = s * 6 + j
                w(pe, p_lo, n - 1)
                if j < 5:
                    W_ = WBq[par] if j < 4 else WBkv[par]
                    src = XT if j < 4 else CT
                    cols = slice(j * P, (j + 1) * P) if j < 4 else slice(0, P)
                    group3(banks[j % 2], [(lambda p, k=k: W_[:, p, k, cols], lambda p, k=k: src[:, c, p, k, :])
                                          for k in range(KC)], p_mm)
                else:
                    for t in range(TC):
                        last = group3(banks[1][:, t * P:(t + 1) * P],
                                      [(lambda p, k=k: CT[:, c, p, k, t * P:(t + 1) * P],
                                        lambda p, k=k: WBkv[par][:, p, k, P:2 * P]) for k in range(KC)], None)
                    last.then_inc(p_mm, 1)

            def b_scores(s, hf):
                for blk in range(8):
                    b, hp = 4 * hf + blk // 2, blk % 2
                    last = group3(banks[2 + hf][:, blk * 64:(blk + 1) * 64],
                                  [(lambda p: qT[:, p, b, 2 * hp:2 * hp + 2, :].rearrange("p h l -> p (h l)"),
                                    lambda p: kT[:, p, b * 64:(b + 1) * 64])], None)
                last.then_inc(s_mm, 1)

            def b_turn(s, hf):
                pe.wait_ge(s_plo, s * 2 + hf + 1)
                for blk in range(8):
                    last = pe.transpose(banks16[4 + hf][:, blk * P:(blk + 1) * P],
                                        PPb[:, 8 * hf + blk].rearrange("p s m -> p (s m)"), ident)
                last.then_inc(t_mm, 1)

            def b_pv(s, jb):
                pe.wait_ge(t_ev, s * 2 + jb // 2 + 1)
                if jb == 0:
                    pe.wait_ge(p_lo, s * 6 + 6)
                if jb >= 2:
                    pe.wait_ge(o_lo, s * 4 + jb - 1)
                out_v = banks[6 + jb % 2].rearrange("p (h b l) -> p h b l", h=HG, b=2)
                for bb in range(2):
                    b = 2 * jb + bb
                    for p in range(2):
                        last = pe.matmul(out_v[:, :, bb, :], V[:, b, p, :],
                                         PTb[:, b * 256:(b + 1) * 256], start=(p == 0), stop=(p == 1))
                last.then_inc(o_mm, 1)

            def b_out(s, par, t):
                pe.wait_ge(o_lo, s * 4 + t + 1)
                if t >= 2:
                    pe.wait_ge(y_add, s * 4 + t - 1)
                group3(banks[4 + t % 2], [(lambda p, h=h: oT[:, p, h, t * P:(t + 1) * P],
                                           lambda p, h=h: WBo[par][:, p, h, :]) for h in range(HG)], y_mm)

            def b_step(s, c, par, last):
                pe.wait_ge(p_lo, s * 6 + 5)
                b_scores(s, 0)
                b_scores(s, 1)
                nxt = (s + 1, (c + 1) % NC, par if c < NC - 1 else 1 - par)

                def proj(j):
                    if not last:
                        b_proj(*nxt, j)

                if not last and c == NC - 1:
                    pe.wait_ge(w_lo, group_ready(s))
                for j in range(3):
                    proj(j)
                b_turn(s, 0)
                b_turn(s, 1)
                proj(3)
                b_pv(s, 0)
                b_pv(s, 1)
                proj(4)
                b_pv(s, 2)
                b_pv(s, 3)
                proj(5)
                for t in range(TC):
                    b_out(s, par, t)

            def group_ready(s):
                if isinstance(s, int):
                    return conv_of_group((s + 1) // NC, 2) + 1
                i, k = s_parts[0], s_parts[1]
                return i * 6 + (4 + 3 * ((k + 1) // NC) + 3)

            s_parts = [None, None]
            pe.wait_ge(n_stored, TC)
            pe.wait_ge(w_lo, 4)
            for j in range(6):
                if j == 5:
                    pe.wait_ge(z_ready, 1)
                b_proj(0, 0, 0, j)
            pe.wait_ge(n_stored, NT)
            pe.wait_ge(w_lo, 7)
            with pe.Fori(0, 3) as i:
                for k in range(8):
                    s_parts[0], s_parts[1] = i, k
                    b_step(i * 8 + k, k % NC, k // NC, False)
            for s in range(24, 32):
                b_step(s, s % NC, (s // NC) % 2, s == 31)

            pe.wait_ge(w_lo, 36)
            pe.wait_ge(y_add, 128)
            pe.wait_ge(p_lo, 192)
            with pe.Fori(0, NC) as c:
                for t in range(TC):
                    norm_turn(pe, c * TC + (NT + t), t % 2, 4 + t % 2)
                pe.wait_ge(n_stored, c * TC + (NT + TC))
                for j in range(12):
                    if j >= 2:
                        pe.wait_ge(u_lo, c * 12 + j - 1)
                    dst = banks[j % 2]
                    if j < 8:
                        group3(dst, [(lambda p, k=k: Wup[:, p, k, j * P:(j + 1) * P], lambda p, k=k: T1[:, p, k, :])
                                     for k in range(KC)], u_mm)
                    elif j < 10:
                        m = j - 8
                        group3(dst, [(lambda p, k=k: Wfc1[:, p, k, m * P:(m + 1) * P], lambda p, k=k: T1[:, p, k, :])
                                     for k in range(KC)], u_mm)
                    else:
                        m = j - 10
                        if m == 0:
                            for t in range(TC):
                                last = group3(banks[5][:, t * NE:(t + 1) * NE],
                                              [(lambda p, k=k: T1[:, p, k, t * P:(t + 1) * P],
                                                lambda p, k=k: Wg0[:, p, k, :]) for k in range(KC)], None)
                            last.then_inc(g_mm, 1)
                            pe.wait_ge(u_lo, c * 12 + 10)
                        group3(dst, [(lambda p, k=k: Wex[:, p, k, m * P:(m + 1) * P], lambda p, k=k: xlT[:, p, k, :])
                                     for k in range(2)], u_mm)
                for t in range(TC):
                    if t >= 2:
                        pe.wait_ge(f_y, c * TC + t - 1)
                    bd, bf = (6, 7) if t % 2 == 0 else (2, 3)
                    tt = slice(t * P, (t + 1) * P)
                    group3(banks[bd], [(lambda p, k=k: hT[:, p, k, tt], lambda p, k=k: Wdn[:, p, k, :])
                                       for k in range(INT // P)], f_mm)
                    if t == 0:
                        pe.wait_ge(u_lo, c * 12 + 12)
                    group3(banks[bf], [(lambda p, k=k: eoT[:, p, k, tt], lambda p, k=k: Wfc2[:, p, k, :])
                                       for k in range(2)], f_mm)

            def attn(n, par, ffn, nxt):
                pe.wait_ge(n_stored, attn_norm(n))
                group3(banks[0], [(lambda p, k=k: TA[:, p, k, :], lambda p, k=k: Wq1[:, p, k, :]) for k in range(KC)], a_q)
                ctx_t = ctx_tile(n)
                group3(banks[1][:, 0:256], [(lambda p, k=k: ctx_t(p, k), lambda p, k=k: Wkv1[:, p, k, :])
                                            for k in range(KC)], a_kv)

                def expert(*es):
                    if ffn is not None:
                        for e in es:
                            experts(n - 1, e)

                if ffn is not None:
                    norm_turn(pe, ffn, 0, 7)
                    gate(n - 1, ffn)
                expert(0)
                pe.wait_ge(a_qlo, n + 1)
                for t in range(16):
                    bank, k = 4 + t // 8, t % 8
                    last = pe.transpose(banks16[bank][:, k * P:(k + 1) * P],
                                        qs[:, 2 * t:2 * t + 2].rearrange("p h s d -> p (h s d)"), ident)
                last.then_inc(a_tq, 1)
                pe.wait_ge(a_kdup, n + 1)
                for g in range(NG):
                    last = pe.transpose(banks16[6][:, g * P:(g + 1) * P], ks[:, g].rearrange("p j s d -> p (j s d)"), ident)
                last.then_inc(a_tk, 1)
                expert(1)

                def scores(b):
                    pe.wait_ge(a_tqev, n + 1)
                    pe.wait_ge(a_tkev, n + 1)
                    if b == 0:
                        pe.wait_ge(a_klo, n + 1)
                        pe.wait_ge(a_kvhi, n + 1)
                    else:
                        pe.wait_ge(b_sub, n * 2 + 1)
                    for blk in range(16):
                        j, g = blk % 2, blk // 2
                        rows = slice(64 * j, 64 * j + 48)
                        last = pe.matmul(banks[j][:, g * 64:(g + 1) * 64],
                                         qT1[rows, b, 2 * g:2 * g + 2, :].rearrange("p t l -> p (t l)"),
                                         kT1[rows, g, b * 64:(b + 1) * 64], start=True, stop=True)
                    last.then_inc(b_s, 1)

                def turn(b):
                    pe.wait_ge(b_plo, n * 2 + b + 1)
                    if b == 1:
                        pe.wait_ge(b_tev, n * 2 + 1)
                    for blk in range(16):
                        last = pe.transpose(banks16[4 + blk // 8][:, (blk % 8) * P:(blk % 8 + 1) * P],
                                            PP1[:, blk].rearrange("p s m -> p (s m)"), ident)
                    last.then_inc(b_t, 1)

                def pv(b):
                    pe.wait_ge(b_tev, n * 2 + b + 1)
                    if b == 1:
                        pe.wait_ge(b_on, n * 2 + 1)
                    for blk in range(16):
                        g = blk % NG
                        for p in range(2):
                            last = pe.matmul(banks[6][:, blk * 16:(blk + 1) * 16], PT1[:, blk * P:(blk + 1) * P],
                                             V1[:, b, p, g * 16:(g + 1) * 16], start=(p == 0), stop=(p == 1))
                    last.then_inc(b_o, 1)

                scores(0)
                expert(2)
                scores(1)
                expert(3)
                turn(0)
                expert(4)
                pv(0)
                turn(1)
                expert(5)
                pv(1)
                expert(6)
                pe.wait_ge(b_olo, n * 2 + 2)
                for b in range(2):
                    for s in range(2):
                        for q in range(2):
                            k = b * 4 + s * 2 + q
                            last = pe.transpose(banks16[7][:, k * P:(k + 1) * P], onh[:, b, s, q * P:(q + 1) * P], ident)
                last.then_inc(a_to, 1)
                expert(7)
                pe.wait_ge(a_toev, n + 1)
                group3(banks[0], [(lambda p, qu=qu: oT1[:, 2 * p + qu // 2, qu % 2, :], lambda p, qu=qu: Wo1[:, p, qu, :])
                                  for qu in range(4)], a_y)
                if nxt is not None:
                    norm_turn(pe, nxt, 1, 7)

            def attn_norm(n):
                return 33 if isinstance(n, int) and n == 0 else n * 2 + 32

            def ctx_tile(n):
                if isinstance(n, int):
                    return lambda p, k: CT[:, n // TC, p, k, (n % TC) * P:(n % TC + 1) * P]
                return ct_of[0]

            ct_of = [None]

            def gate(n, norm):
                pe.wait_ge(n_stored, norm + 1)
                pe.wait_ge(a_klo, n + 2) if attn_running[0] else None
                pe.wait_ge(a_kvhi, n + 2) if attn_running[0] else None
                group3(banks[1][:, 256:256 + NE], [(lambda p, k=k: TF[:, p, k, :], lambda p, k=k: Wg1[:, p, k, :])
                                                   for k in range(KC)], r_mm)

            attn_running = [True]

            def experts(n, e):
                if not (isinstance(n, int) and n == 0 and e < 2):
                    pe.wait_ge(e_bias, n * NE + e - 1 if e > 0 else n * NE)
                group3(banks[2 + e % 2], [(lambda p, k=k: TF[:, p, k, :], lambda p, k=k: We[e][:, p, k, :])
                                          for k in range(KC)], e_mm)

            pe.wait_ge(f_add, NT)
            pe.wait_ge(w_lo, 40)
            pe.wait_ge(z_ready, 4)
            norm_turn(pe, 32, 0, 7)
            attn(0, 0, None, 33)
            pe.wait_ge(w_lo, 48)
            attn(1, 1, 34, 35)
            with pe.Fori(0, 3) as i:
                for k in range(2, 6):
                    n = i * 4 + k
                    ch = k // TC
                    ct_of[0] = lambda p, kc, ch=ch, k=k: CT[:, ds(i + ch, 1), p, kc, (k % TC) * P:(k % TC + 1) * P]\
                        .rearrange("p a n -> p (a n)")
                    attn(n, k % 2, n * 2 + 32, n * 2 + 33)
            for n in range(14, NT):
                attn(n, n % 2, n * 2 + 32, n * 2 + 33 if n < NT - 1 else None)
            attn_running[0] = False
            norm_turn(pe, 63, 1, 7)
            gate(NT - 1, 63)
            for e in range(NE):
                experts(NT - 1, e)

        @block.scalar
        def _(act):
            sc = nc.scalar
            act.preload_act_table_set("natural_log_exp_and_others")

            act.wait_ge(x_in, 16 * NC)
            def turn_x(n, t, dst):
                norm_root(act, n, t % 2)
                norm_hi(act, n, t % 2)
                norm_store(act, n, 4 + t % 2, dst)

            for t in range(TC):
                turn_x(t, t, XT[:, 0, :, :, t * P:(t + 1) * P].rearrange("p s k n -> p (s k) n"))
            with act.Fori(1, NC) as c:
                for t in range(TC):
                    turn_x(c * TC + t, t, XT[:, ds(c, 1), :, :, t * P:(t + 1) * P].rearrange("p a s k n -> p (a s k) n"))

            def bias_col(g, a):
                return biases[:, ds(g + a, 1)] if not isinstance(g, int) else biases[:, g + a:g + a + 1]

            def proj_hi(s, g, j):
                alone(act, p_mm, s * 6 + j + 1)
                if j < 4:
                    sc.activation(qT[:, 0, :, j, :], banks[j % 2].rearrange("p (b l) -> p b l", l=64), ACT.Identity, bias=bias_col(g * HG, j)).then_inc(p_hi, 1)
                elif j == 4:
                    sc.activation(kT[:, 0, :], banks[0], ACT.Identity, bias=bias_col(g, 32)).then_inc(p_hi, 1)
                else:
                    v = banks[1].rearrange("p (t d) -> p t d", t=TC)
                    for odd in range(2):
                        for half in range(2):
                            last = sc.activation(V[64 * half:64 * half + 64, odd:BC:2, 0, :],
                                                 v[64 * odd:64 * odd + 64], ACT.Copy, scale=UN)
                    last.then_inc(p_hi, 1)

            def o_part(s, g, jb):
                alone(act, o_mm, s * 4 + jb + 1)
                sc.activation(oT[:, 0, :, jb * P:(jb + 1) * P], banks[6 + jb % 2].rearrange("p (h n) -> p h n", h=HG), ACT.Identity,
                              bias=bias_col(g, 40)).then_inc(o_hi, 1)

            def b_step(s, g, gn, last):
                def proj(j):
                    if not last:
                        proj_hi(s + 1, gn, j)

                def exp(hf):
                    act.wait_ge(s_sub, s * 2 + hf + 1)
                    e = Eb[:, 8 * hf:8 * hf + 8, :]
                    sc.activation(e, e, ACT.Exp, scale=SC0).then_inc(s_exp, 1)

                def phi(hf):
                    act.wait_ge(s_prob, s * 2 + hf + 1)
                    sc.activation(PPb[:, 8 * hf:8 * hf + 8, 0, :], Eb[:, 8 * hf:8 * hf + 8, :], ACT.Copy).then_inc(s_phi, 1)

                def turned(hf):
                    act.wait_ge(t_mm, s * 2 + hf + 1)
                    sc.activation(PTb[:, hf * 1024:(hf + 1) * 1024], banks16[4 + hf], ACT.Copy).then_inc(t_ev, 1)

                exp(0)
                exp(1)
                proj(0)
                phi(0)
                phi(1)
                proj(1)
                proj(2)
                turned(0)
                turned(1)
                proj(3)
                o_part(s, g, 0)
                o_part(s, g, 1)
                proj(4)
                o_part(s, g, 2)
                o_part(s, g, 3)
                proj(5)

            act.wait_ge(bias_ready, 1)
            for j in range(6):
                proj_hi(0, 0, j)
            with act.Fori(0, 3) as i:
                for k in range(8):
                    b_step(i * 8 + k, i * 2 + k // NC, i * 2 + (k + 1) // NC, False)
            for s in range(24, 32):
                b_step(s, s // NC, (s + 1) // NC, s == 31)

            with act.Fori(0, NC) as c:
                for t in range(TC):
                    n = c * TC + (NT + t)
                    norm_root(act, n, t % 2)
                    norm_hi(act, n, t % 2)
                    norm_store(act, n, 4 + t % 2, T1[:, :, :, t * P:(t + 1) * P].rearrange("p s k n -> p (s k) n"))
                for j in range(12):
                    m = c * 12 + j
                    act.wait_ge(u_mm, m + 1)
                    if j < 8:
                        sc.activation(rel[:, j % 2, :], banks[j % 2], ACT.Relu, scale=UN).then_inc(u_rel, 1)
                        act.wait_ge(u_sq, c * 8 + j + 1)
                        sc.activation(hT[:, 0, j, :], h32, ACT.Copy).then_inc(u_hi, 1)
                    else:
                        dst = (xlT if j < 10 else eoT)[:, 0, j % 2, :]
                        sc.activation(dst, banks[j % 2], ACT.Copy, scale=UN).then_inc(u_hi, 1)
                for t in range(TC):
                    s = ystat
                    n = c * TC + t
                    act.wait_ge(y_arg, n + 1)
                    sc.activation(s[:, 9:10], s[:, 8:9], ACT.Ln).then_inc(y_ln, 1)
                    act.wait_ge(y_ln, n + 1)
                    sc.activation(s[:, 10:11], s[:, 9:10], ACT.Exp, scale=-0.5).then_inc(y_r0, 1)

            def norm(idx, par, dst):
                norm_root(act, idx, par)
                norm_hi(act, idx, par)
                norm_store(act, idx, 7, dst.rearrange("p s k n -> p (s k) n"))

            def expert(n, e):
                act.wait_ge(e_bias, n * NE + e + 1)
                if e == 0:
                    act.wait_ge(r_mask, n + 1)
                    w(act, x_done, n)
                dst = acc if e == 0 else tmp[:, e % 2, :]
                sc.activation(dst, tmp[:, e % 2, :], ACT.Relu, scale=msk[:, 16 + e:17 + e]).then_inc(e_rel, 1)

            def attn(n, ffn, nxt):
                act.wait_ge(a_q, n + 1)
                q = banks[0].rearrange("p (h d) -> p h d", h=32)
                sc.activation(qs[:, :, 0, :], q, ACT.Copy)
                sc.activation(qs[:, :, 2, :], q, ACT.Copy).then_inc(a_qhi, 1)
                act.wait_ge(a_kv, n + 1)
                k = banks[1][:, 0:P].rearrange("p (g d) -> p g d", g=NG)
                sc.activation(ks[:, :, 0, 0, :], k, ACT.Copy)
                sc.activation(ks[:, :, 0, 1, :], k, ACT.Copy)
                for b in range(2):
                    for half in range(2):
                        last = sc.activation(V1[64 * half:64 * half + 64, b, 0, :],
                                             banks[1][64 * b:64 * b + 64, P:2 * P], ACT.Copy, scale=UN)
                last.then_inc(a_kvhi, 1)
                if ffn is not None:
                    norm(ffn, 0, TF)

                def ex(*es):
                    if ffn is not None:
                        for e in es:
                            expert(n - 1, e)

                ex(0)
                act.wait_ge(a_tq, n + 1)
                for h in range(2):
                    last = sc.activation(qT1[:, :, 8 * h:8 * h + 8, :].rearrange("p b t l -> p t b l"),
                                         banks16[4 + h].rearrange("p (t b l) -> p t b l", t=8, b=2), ACT.Copy)
                last.then_inc(a_tqev, 1)
                act.wait_ge(a_tk, n + 1)
                sc.activation(kT1, banks16[6].rearrange("p (t n) -> p t n", t=8), ACT.Copy).then_inc(a_tkev, 1)
                ex(1)
                for b in range(2):
                    v = n * 2 + b + 1
                    if b == 1:
                        ex(3)
                    act.wait_ge(b_sub, v)
                    sc.activation(E1, E1, ACT.Exp, scale=SC1).then_inc(b_exp, 1)
                    act.wait_ge(b_exp, v)
                    if b == 1:
                        act.wait_ge(b_t, v - 1)
                    sc.activation(PP1[:, :, 0, :], E1, ACT.Copy, scale=PS).then_inc(b_phi, 1)
                    if b == 0:
                        ex(2)
                        act.wait_ge(b_t, v)
                        for h in range(2):
                            last = sc.activation(PT1[:, h * 1024:(h + 1) * 1024], banks16[4 + h], ACT.Copy)
                        last.then_inc(b_tev, 1)
                act.wait_ge(b_on, n * 2 + 1)
                sc.activation(onh[:, 0, 0, :], on32, ACT.Copy).then_inc(b_ohi, 1)
                ex(4)
                act.wait_ge(b_t, n * 2 + 2)
                act.wait_ge(b_o, n * 2 + 1)
                for h in range(2):
                    last = sc.activation(PT1[:, h * 1024:(h + 1) * 1024], banks16[4 + h], ACT.Copy)
                last.then_inc(b_tev, 1)
                ex(5)
                act.wait_ge(b_on, n * 2 + 2)
                sc.activation(onh[:, 1, 0, :], on32, ACT.Copy).then_inc(b_ohi, 1)
                ex(6)
                act.wait_ge(a_to, n + 1)
                for b in range(2):
                    last = sc.activation(oT1[:, :, :, b * 64:(b + 1) * 64],
                                         banks16[7][:, b * 512:(b + 1) * 512].rearrange("p (s u l) -> p s u l", s=4, u=2),
                                         ACT.Copy)
                last.then_inc(a_toev, 1)
                ex(7)
                if nxt is not None:
                    norm(nxt, 1, TA)

            act.wait_ge(f_add, NT)
            norm(32, 0, TA)
            act.wait_ge(z_ready, 4)
            attn(0, None, 33)
            attn(1, 34, 35)
            with act.Fori(0, 6) as i:
                for k in range(2, 4):
                    n = i * 2 + k
                    attn(n, n * 2 + 32, n * 2 + 33)
            attn(NT - 2, 2 * (NT - 2) + 32, 2 * (NT - 2) + 33)
            attn(NT - 1, 2 * (NT - 1) + 32, None)
            norm(63, 1, TF)
            for e in range(NE):
                expert(NT - 1, e)

        @block.vector
        def _(dve):
            v = nc.vector

            dve.wait_ge(x_in, 16 * NC)
            def turn_x(n, par):
                norm_stats(dve, n, par, x_tile(n))
                norm_apply(dve, n, par, x_tile(n))

            for par in range(2):
                turn_x(par, par)
            with dve.Fori(1, NT // 2) as i:
                for par in range(2):
                    turn_x(i * 2 + par, par)

            def bias_col(g, a):
                return biases[:, ds(g + a, 1)] if not isinstance(g, int) else biases[:, g + a:g + a + 1]

            def lo(dst, src, bias, hi, done):
                v.scalar_tensor_tensor(out=dst, in0=src, scalar=bias, in1=hi, op0=ALU.add, op1=ALU.subtract).then_inc(done, 1)

            def proj_lo(s, g, j):
                dve.wait_ge(p_hi, s * 6 + j + 1)
                if j < 4:
                    lo(qT[:, 1, :, j, :], banks[j % 2].rearrange("p (b l) -> p b l", l=64), bias_col(g * HG, j), qT[:, 0, :, j, :], p_lo)
                elif j == 4:
                    lo(kT[:, 1, :], banks[0], bias_col(g, 32), kT[:, 0, :], p_lo)
                else:
                    vv = banks[1].rearrange("p (t d) -> p t d", t=TC)
                    for odd in range(2):
                        h = slice(64 * odd, 64 * odd + 64)
                        last = v.scalar_tensor_tensor(out=V[0:64, odd:BC:2, 1, :], in0=vv[h], scalar=UN,
                                                      in1=V[h, odd:BC:2, 0, :], op0=ALU.mult, op1=ALU.subtract)
                    last.then_inc(p_lo, 1)

            def b_step(s, g, gn, last):
                def proj(j):
                    if not last:
                        proj_lo(s + 1, gn, j)

                def blocks(hf):
                    return slice(8 * hf, 8 * hf + 8)

                def wide(cols):
                    return cols.unsqueeze(2).to_broadcast([P, 8, 64])

                def shift(hf):
                    n = s * 2 + hf + 1
                    S = banks[2 + hf].rearrange("p (k m) -> p k m", m=64)
                    dve.wait_ge(s_mm, n)
                    v.tensor_reduce(smx[:, blocks(hf)], S, AX.X, ALU.max).then_inc(s_max, 1)
                    dve.wait_ge(s_max, n)
                    v.tensor_tensor(Eb[:, blocks(hf), :], S, wide(smx[:, blocks(hf)]), ALU.subtract).then_inc(s_sub, 1)

                def prob(hf):
                    n = s * 2 + hf + 1
                    sums, recs = smx[:, 16 + 8 * hf:24 + 8 * hf], smx[:, 32 + 8 * hf:40 + 8 * hf]
                    dve.wait_ge(s_exp, n)
                    v.tensor_reduce(sums, Eb[:, blocks(hf), :], AX.X, ALU.add).then_inc(s_sum, 1)
                    dve.wait_ge(s_sum, n)
                    v.reciprocal(recs, sums).then_inc(s_rec, 1)
                    dve.wait_ge(s_rec, n)
                    v.scalar_tensor_tensor(out=Eb[:, blocks(hf), :], in0=Eb[:, blocks(hf), :], scalar=PS,
                                           in1=wide(recs), op0=ALU.mult, op1=ALU.mult).then_inc(s_prob, 1)

                def plo(hf):
                    dve.wait_ge(s_phi, s * 2 + hf + 1)
                    v.tensor_tensor(PPb[:, blocks(hf), 1, :], Eb[:, blocks(hf), :], PPb[:, blocks(hf), 0, :],
                                    ALU.subtract).then_inc(s_plo, 1)

                def olo(jb):
                    dve.wait_ge(o_hi, s * 4 + jb + 1)
                    cols = slice(jb * P, (jb + 1) * P)
                    lo(oT[:, 1, :, cols], banks[6 + jb % 2].rearrange("p (h n) -> p h n", h=HG), bias_col(g, 40),
                       oT[:, 0, :, cols], o_lo)

                shift(0)
                shift(1)
                prob(0)
                prob(1)
                proj(0)
                plo(0)
                plo(1)
                proj(1)
                proj(2)
                proj(3)
                olo(0)
                olo(1)
                proj(4)
                olo(2)
                olo(3)
                proj(5)
                for t in range(TC):
                    dve.wait_ge(y_mm, s * 4 + t + 1)
                    xt = x_tile(((s if isinstance(s, int) else s_k[0]) % NC) * TC + t)
                    v.scalar_tensor_tensor(out=xt, in0=banks[4 + t % 2], scalar=UN2, in1=xt,
                                           op0=ALU.mult, op1=ALU.add).then_inc(y_add, 1)

            s_k = [0]
            for j in range(6):
                proj_lo(0, 0, j)
            dve.wait_ge(bo_added, NT)
            with dve.Fori(0, 3) as i:
                for k in range(8):
                    s_k[0] = k
                    b_step(i * 8 + k, i * 2 + k // NC, i * 2 + (k + 1) // NC, False)
            for s in range(24, 32):
                b_step(s, s // NC, (s + 1) // NC, s == 31)

            dve.wait_ge(y_add, 128)
            dve.wait_ge(gb_in, 32)
            with dve.Fori(0, NC) as c:
                for t in range(TC):
                    n = c * TC + (NT + t)
                    norm_stats(dve, n, t % 2, x_tile(c * TC + t))
                    norm_apply(dve, n, t % 2, x_tile(c * TC + t))
                for j in range(12):
                    if j == 10:
                        alone(dve, g_mm, c + 1)
                        for t in range(TC):
                            last = v.max(m8[:, t * NE:(t + 1) * NE], banks[5][:, t * NE:(t + 1) * NE])
                        last.then_inc(g_top, 1)
                        dve.wait_ge(g_top, c + 1)
                        for t in range(TC):
                            last = v.tensor_scalar(rsum[:, t:t + 1], m8[:, t * NE:t * NE + 1],
                                                   m8[:, t * NE + 1:t * NE + 2], UN2, ALU.add, ALU.mult)
                        last.then_inc(g_sum, 1)
                    if j < 8:
                        dve.wait_ge(u_rel, c * 8 + j + 1)
                        if j > 0:
                            dve.wait_ge(u_lo, c * 12 + j)
                        v.tensor_tensor(h32, rel[:, j % 2, :], rel[:, j % 2, :], ALU.mult).then_inc(u_sq, 1)
                        dve.wait_ge(u_hi, c * 12 + j + 1)
                        v.tensor_tensor(hT[:, 1, j, :], h32, hT[:, 0, j, :], ALU.subtract).then_inc(u_lo, 1)
                    else:
                        dst = xlT if j < 10 else eoT
                        dve.wait_ge(u_hi, c * 12 + j + 1)
                        v.scalar_tensor_tensor(out=dst[:, 1, j % 2, :], in0=banks[j % 2], scalar=UN,
                                               in1=dst[:, 0, j % 2, :], op0=ALU.mult, op1=ALU.subtract).then_inc(u_lo, 1)
                dve.wait_ge(g_sum, c + 1)
                for t in range(TC):
                    n = c * TC + t
                    bd, bf = (6, 7) if t % 2 == 0 else (2, 3)
                    xt = x_tile(n)
                    s = ystat
                    y = xn
                    dve.wait_ge(f_mm, n * 2 + 2)
                    v.tensor_scalar(h32, banks[bf], rsum[:, t:t + 1], None, ALU.mult).then_inc(f_rt, 1)
                    dve.wait_ge(f_rt, n + 1)
                    v.scalar_tensor_tensor(out=y, in0=banks[bd], scalar=UN, in1=h32, op0=ALU.mult, op1=ALU.add).then_inc(f_y, 1)
                    dve.wait_ge(f_y, n + 1)
                    v.bn_stats(s[:, 0:6], y).then_inc(y_bn, 1)
                    alone(dve, y_bn, n + 1)
                    v.bn_aggr(s[:, 6:8], s[:, 0:6]).then_inc(y_mv, 1)
                    dve.wait_ge(y_mv, n + 1)
                    v.tensor_scalar(s[:, 8:9], s[:, 7:8], EPS, None, ALU.add).then_inc(y_arg, 1)
                    newton(dve, s, n, y_r0, y_a, y_b, y_r)
                    v.tensor_scalar(y, y, s[:, 6:7], s[:, 13:14], ALU.subtract, ALU.mult).then_inc(f_t, 1)
                    dve.wait_ge(f_t, n + 1)
                    v.tensor_tensor(y, y, gamb, ALU.mult).then_inc(f_g, 1)
                    dve.wait_ge(f_g, n + 1)
                    v.tensor_tensor(y, y, betb, ALU.add).then_inc(f_b, 1)
                    dve.wait_ge(f_b, n + 1)
                    v.tensor_tensor(xt, xt, y, ALU.add).then_inc(f_add, 1)

            def mask_of(n):
                dve.wait_ge(r_mm, n + 1)
                v.scalar_tensor_tensor(out=lgt, in0=banks[1][:, 256:256 + NE], scalar=UN, in1=bgb,
                                       op0=ALU.mult, op1=ALU.add).then_inc(r_lg, 1)
                alone(dve, r_lg, n + 1)
                v.max(m8[:, 0:8], lgt).then_inc(r_top, 1)
                alone(dve, r_top, n + 1)
                v.max_index(idx8, m8[:, 0:8], lgt).then_inc(r_idx, 1)
                dve.wait_ge(r_idx, n + 1)
                v.tensor_copy(idxf, idx8).then_inc(r_f, 1)
                dve.wait_ge(r_f, n + 1)
                v.tensor_scalar(msk[:, 0:8], iota8, idxf[:, 0:1], 0.5, ALU.is_equal, ALU.mult).then_inc(r_m1, 1)
                v.tensor_scalar(msk[:, 8:16], iota8, idxf[:, 1:2], 0.5, ALU.is_equal, ALU.mult).then_inc(r_m2, 1)
                dve.wait_ge(r_m1, n + 1)
                dve.wait_ge(r_m2, n + 1)
                w(dve, e_rel, n * NE)
                v.tensor_tensor(msk[:, 16:24], msk[:, 0:8], msk[:, 8:16], ALU.add).then_inc(r_mask, 1)

            def expert(n, e):
                dve.wait_ge(e_mm, n * NE + e + 1)
                if e == 2:
                    dve.wait_ge(e_rel, n * NE + 1)
                elif e > 2:
                    dve.wait_ge(e_acc, n * (NE - 1) + e - 2)
                else:
                    w(dve, e_acc, n * (NE - 1))
                v.scalar_tensor_tensor(out=tmp[:, e % 2, :], in0=banks[2 + e % 2], scalar=UN, in1=beb[:, e, :],
                                       op0=ALU.mult, op1=ALU.add).then_inc(e_bias, 1)

            def norm(idx, par, n, rms):
                norm_stats(dve, idx, par, x_tile(n), rms)
                norm_apply(dve, idx, par, x_tile(n))

            def attn(n, ffn, nxt):
                dve.wait_ge(a_qhi, n + 1)
                v.tensor_tensor(qs[:, :, 1, :], banks[0].rearrange("p (h d) -> p h d", h=32), qs[:, :, 0, :],
                                ALU.subtract).then_inc(a_qlo, 1)
                dve.wait_ge(a_kvhi, n + 1)
                v.tensor_tensor(ks[:, :, 0, 2, :], banks[1][:, 0:P].rearrange("p (g d) -> p g d", g=NG),
                                ks[:, :, 0, 0, :], ALU.subtract)
                for b in range(2):
                    h = slice(64 * b, 64 * b + 64)
                    last = v.scalar_tensor_tensor(out=V1[0:64, b, 1, :], in0=banks[1][h, P:2 * P], scalar=UN,
                                                  in1=V1[h, b, 0, :], op0=ALU.mult, op1=ALU.subtract)
                last.then_inc(a_klo, 1)
                if ffn is not None:
                    norm(ffn, 0, n - 1, False)
                    mask_of(n - 1)

                def ex(*es):
                    if ffn is not None:
                        for e in es:
                            expert(n - 1, e)

                ex(0, 1)

                def wide(cols, k):
                    return cols.unsqueeze(2).to_broadcast([P, cols.shape[1], k])

                for b in range(2):
                    m = n * 2 + b + 1
                    dve.wait_ge(b_s, m)
                    for h in range(2):
                        last = v.tensor_reduce(smx[:, 8 * h:8 * h + 8], banks[h].rearrange("p (k m) -> p k m", m=64), AX.X, ALU.max)
                    last.then_inc(b_max, 1)
                    dve.wait_ge(b_max, m)
                    for h in range(2):
                        last = v.tensor_tensor(E1[:, 8 * h:8 * h + 8, :], banks[h].rearrange("p (k m) -> p k m", m=64),
                                               wide(smx[:, 8 * h:8 * h + 8], 64), ALU.subtract)
                    last.then_inc(b_sub, 1)
                    if b == 0:
                        ex(2)
                    dve.wait_ge(b_exp, m)
                    v.tensor_reduce(smx[:, 16:32], E1, AX.X, ALU.add).then_inc(b_sum, 1)
                    dve.wait_ge(b_sum, m)
                    if b == 1:
                        on(n, 0)
                    v.reciprocal(smx[:, 32:48], smx[:, 16:32]).then_inc(b_rec, 1)
                    dve.wait_ge(b_phi, m)
                    v.scalar_tensor_tensor(out=PP1[:, :, 1, :], in0=E1, scalar=PS, in1=PP1[:, :, 0, :],
                                           op0=ALU.mult, op1=ALU.subtract).then_inc(b_plo, 1)
                    if b == 0:
                        ex(3)
                ex(4, 5)
                on(n, 1)
                ex(6, 7)
                dve.wait_ge(a_y, n + 1)
                xt = x_tile(n)
                v.scalar_tensor_tensor(out=xt, in0=banks[0], scalar=UN2, in1=xt, op0=ALU.mult, op1=ALU.add).then_inc(a_add, 1)
                if nxt is not None:
                    norm(nxt, 1, n + 1, True)

            def on(n, b):
                m = n * 2 + b + 1
                dve.wait_ge(b_o, m)
                dve.wait_ge(b_rec, m)
                v.tensor_tensor(on32.rearrange("p (k d) -> p k d", d=16), banks[6][:, 0:256].rearrange("p (k d) -> p k d", d=16),
                                smx[:, 32:48].unsqueeze(2).to_broadcast([P, 16, 16]), ALU.mult).then_inc(b_on, 1)
                dve.wait_ge(b_ohi, m)
                v.tensor_tensor(onh[:, b, 1, :], on32, onh[:, b, 0, :], ALU.subtract).then_inc(b_olo, 1)

            dve.wait_ge(f_add, NT)
            norm(32, 0, 0, True)
            attn(0, None, 33)
            dve.wait_ge(be_in, 16)
            attn(1, 34, 35)
            with dve.Fori(0, 6) as i:
                for k in range(2, 4):
                    n = i * 2 + k
                    attn(n, n * 2 + 32, n * 2 + 33)
            attn(NT - 2, 2 * (NT - 2) + 32, 2 * (NT - 2) + 33)
            attn(NT - 1, 2 * (NT - 1) + 32, None)
            dve.wait_ge(a_add, NT)
            norm(63, 1, NT - 1, False)
            mask_of(NT - 1)
            for e in range(NE):
                expert(NT - 1, e)


def kernel(**inputs):
    import numpy as np
    import concourse.bacc as bacc
    from concourse.bass_utils import run_bass_kernel_spmd

    a = {k: np.asarray(v) for k, v in inputs.items()}

    def rows(m, k):
        return m.reshape(k, P, m.shape[1]).transpose(1, 0, 2).reshape(P, -1)

    ctx = a["ctx_4096"].reshape(NTOK, D)
    ctxT = np.stack([rows(ctx[c * CH:(c + 1) * CH].T, KC) for c in range(NC)])
    Wq, Wkv, Wo = a["L0_xattn_Wq"], a["L0_xattn_Wkv"], a["L0_xattn_Wo"]
    wB = np.stack([np.concatenate([
        rows(Wq[:, g * 512:(g + 1) * 512], KC),
        rows(np.concatenate([Wkv[:, g * P:(g + 1) * P], Wkv[:, 1024 + g * P:1024 + (g + 1) * P]], 1), KC),
        rows(Wo[g * 512:(g + 1) * 512], HG)], 1) for g in range(NG)])
    biasB = np.concatenate([a["L0_xattn_bq"].reshape(32, P).T, a["L0_xattn_bkv"].reshape(16, P).T], 1)
    wo1 = a["L1_xattn_wo"].T.reshape(NG, 2, 2, HD1, D)
    wo1 = wo1.transpose(0, 3, 2, 1, 4).reshape(P, 4 * D)
    arrays = {
        "x": a["x"].reshape(NTOK, D), "ctxT": ctxT, "wB": wB, "biasB": biasB,
        "bo": a["L0_xattn_bo"].reshape(1, D),
        "up": rows(a["L0_ffn_up_w"], KC), "down": rows(a["L0_ffn_down_w"], INT // P),
        "small0": np.concatenate([rows(a["L0_ffn_fc1_w"], KC), rows(a["L0_ffn_expert_w"], 2),
                                  rows(a["L0_ffn_gate_w"], KC)], 1),
        "fc2": rows(a["L0_ffn_fc2_w"], 2),
        "gam": a["L0_ffn_ln_gamma"].reshape(1, D), "bet": a["L0_ffn_ln_beta"].reshape(1, D),
        "wq1": rows(a["L1_xattn_wq"].T, KC),
        "wkv1": np.concatenate([rows(np.concatenate([a["L1_xattn_wk"], a["L1_xattn_wv"]], 0).T, KC),
                                rows(a["L1_ffn_W_gate"], KC)], 1),
        "wo1": wo1, "lnw": a["L1_xattn_ln_w"].reshape(KC, P).T,
        "we": np.stack([rows(a["L1_ffn_W_e"][e], KC) for e in range(NE)]),
        "be": a["L1_ffn_b_e"].reshape(1, NE * D), "bg": a["L1_ffn_b_gate"].reshape(1, NE),
    }
    arrays = {"in_" + k: np.ascontiguousarray(v) for k, v in arrays.items()}
    nc = bacc.Bacc("TRN2", target_bir_lowering=False, num_devices=1)
    args = [nc.dram_tensor(k, v.shape, mybir.dt.from_np(v.dtype), kind="ExternalInput").ap() for k, v in arrays.items()]
    args.append(nc.dram_tensor("out_0", (NTOK, D), F32, kind="ExternalOutput").ap())
    build(nc, *args)
    r = run_bass_kernel_spmd(nc, [arrays], core_ids=[0])
    return r.results[0]["out_0"].reshape(32, 64, D)
```

```python
from contextlib import ExitStack

import concourse.bass as bass
from concourse import mybir

F32 = mybir.dt.float32
F16 = mybir.dt.float16
U32 = mybir.dt.uint32
ACT = mybir.ActivationFunctionType
ALU = mybir.AluOpType
AX = mybir.AxisListType
ds = bass.ds

P = 128
D = 512
KC = D // P
NTOK = 32 * 64
NT = NTOK // P
NC = 4
CH = NTOK // NC
TC = CH // P
BC = CH // 64
NG = 8
HG = 4
HD1 = 16
INT = 1024
LAT = 256
NE = 8
EPS = 1e-5
WS = 64.0
UN = 1.0 / WS
UN2 = UN * UN
PS = 64.0
SC0 = UN2 * P ** -0.5
SC1 = UN2 * HD1 ** -0.5
EXPERT_ORDER = (0, 1, 4, 5, 2, 3, 6, 7)
PASSES = ((0, 0), (0, 1), (1, 0))


def w(eng, sem, value):
    if not (isinstance(value, int) and value <= 0):
        eng.wait_ge(sem, value)


def build(nc, x, ctxT, wB, biasB, bo, up, down, small0, fc2, gam, bet, wq1, wkv1, wo1, lnw, we, be, bg, out):
    with ExitStack() as stack:
        def sb(name, cols, dt=F16):
            return stack.enter_context(nc.sbuf_tensor(name, [P, cols], dt))[:, :]

        def sem(name):
            return stack.enter_context(nc.semaphore(name))

        banks = [stack.enter_context(nc.psum_tensor(f"bank{i}", [P, 512], F32))[:, :] for i in range(8)]
        banks16 = [b.bitcast(F16) for b in banks]

        X = sb("X", NT * D, F32).rearrange("p (t d) -> p t d", t=NT)
        CT = sb("CT", NC * 2 * KC * CH).rearrange("p (c s k n) -> p c s k n", c=NC, s=2, k=KC)
        R1 = sb("R1", 16384)
        R2 = sb("R2", 21504)
        R3 = sb("R3", 4096, F32)
        AW = sb("AW", 10240)
        R4 = sb("R4", 13312)
        R5 = sb("R5", 1024, F32)
        yn = sb("yn", D, F32)
        ident = sb("ident", P)
        biases = sb("biases", 48, F32)
        lnwT = sb("lnwT", KC, F32)
        g0w = sb("g0w", 2 * KC * NE)
        g1w = sb("g1w", 2 * KC * NE)
        stat = sb("stat", 2 * 16, F32)
        ystat = sb("ystat", 16, F32)
        cstat = sb("cstat", TC * 14, F32)
        smx = sb("smx", 3 * 16, F32)
        m8 = sb("m8", TC * 8, F32)
        rsum = sb("rsum", TC, F32)
        lgt = sb("lgt", 8, F32)
        idx8 = sb("idx8", 8, U32)
        idxf = sb("idxf", 8, F32)
        msk = sb("msk", 3 * 8, F32)
        iota8 = sb("iota8", 8, F32)
        bgb = sb("bgb", 8, F32)

        def parts(region, off, k, n):
            return region[:, off:off + 2 * k * n].rearrange("p (s k n) -> p s k n", s=2, k=k)

        raw = R3.rearrange("p (s n) -> p s n", s=2)
        beb = R3.rearrange("p (e n) -> p e n", e=NE)
        xs = R4[:, 0:2048].rearrange("p (i s d) -> p i s d", i=2, s=2)
        XT = R1.rearrange("p (c s k n) -> p c s k n", c=NC, s=2, k=KC)
        GW = 10240
        WBq = [parts(R2, GW * i, KC, CH) for i in range(2)]
        WBkv = [parts(R2, GW * i + 4096, KC, 256) for i in range(2)]
        WBo = [parts(R2, GW * i + 6144, HG, D) for i in range(2)]
        qT = R4[:, 2048:6144].rearrange("p (s b h l) -> p s b h l", s=2, b=BC, h=HG)
        kT = R4[:, 6144:7168].rearrange("p (s n) -> p s n", s=2)
        V = R4[:, 7168:9216].rearrange("p (b s d) -> p b s d", b=BC, s=2)
        oT = R4[:, 9216:13312].rearrange("p (s h n) -> p s h n", s=2, h=HG)
        Eb = AW[:, 0:2048].bitcast(F32).rearrange("p (k m) -> p k m", m=64)
        PPb = AW[:, 2048:4096].rearrange("p (k s m) -> p k s m", s=2, m=64)
        PTb = AW[:, 4096:6144]
        xnB = AW[:, 6144:8192].bitcast(F32).rearrange("p (i n) -> p i n", i=2)
        Wup, Wfc1 = parts(R2, 0, KC, INT), parts(R2, 8192, KC, LAT)
        Wdn, Wex, Wfc2 = parts(R2, 10240, INT // P, D), parts(R2, 18432, LAT // P, LAT), parts(R2, 19456, LAT // P, D)
        Wg0, Wg1 = parts(g0w, 0, KC, NE), parts(g1w, 0, KC, NE)
        T1 = parts(R4, 2048, KC, CH)
        xlT, eoT = parts(R4, 6144, 2, CH), parts(R4, 8192, 2, CH)
        rel = R4[:, 10240:12288].bitcast(F32).rearrange("p (i n) -> p i n", i=2)
        h32 = R4[:, 12288:13312].bitcast(F32)
        hT = parts(R1, 8192, INT // P, CH)
        gamb, betb = R5[:, 0:D], R5[:, D:2 * D]
        bob = R5[:, 0:D]
        We = [parts(R1 if e < 4 else R2, 4096 * (e % 4), KC, D) for e in range(NE)]
        Wq1, Wkv1, Wo1 = parts(AW, 0, KC, D), parts(AW, 4096, KC, 256), parts(AW, 6144, 4, D)
        TA, TF = parts(R4, 2048, KC, P), parts(R4, 3072, KC, P)
        qs = R4[:, 4096:6144].rearrange("p (h s d) -> p h s d", h=32, s=4)
        PT1 = R4[:, 4096:6144]
        ks = R4[:, 6144:7168].rearrange("p (g j s d) -> p g j s d", g=NG, j=2, s=4)
        qT1 = R4[:, 7168:9216].rearrange("p (b t l) -> p b t l", b=2, t=16)
        kT1 = R4[:, 9216:10240].rearrange("p (g n) -> p g n", g=NG)
        V1 = R4[:, 10240:10752].rearrange("p (b s n) -> p b s n", b=2, s=2)
        E1 = R4[:, 10752:12800].bitcast(F32).rearrange("p (k m) -> p k m", m=64)
        on32 = R4[:, 12800:13312].bitcast(F32)
        PP1 = R2[:, 16384:18432].rearrange("p (k s m) -> p k s m", s=2, m=64)
        tmp = R2[:, 18432:20480].bitcast(F32).rearrange("p (i n) -> p i n", i=2)
        acc = R2[:, 20480:21504].bitcast(F32)
        onh = R5[:, 0:512].bitcast(F16).rearrange("p (b s n) -> p b s n", b=2, s=2)
        oT1 = R5[:, 512:1024].bitcast(F16).rearrange("p (s u n) -> p s u n", s=4, u=2)

        raw_in = [sem("raw_in0"), sem("raw_in1")]
        x_in = [sem(f"x_in{c}") for c in range(NC)]
        const_in, gb_in, be_in, out_done = sem("const_in"), sem("gb_in"), sem("be_in"), sem("out_done")
        w_scaled, w_hi, w_lo = sem("w_scaled"), sem("w_hi"), sem("w_lo")
        id_zero, id_ready, bias_ready, bo_added = sem("id_zero"), sem("id_ready"), sem("bias_ready"), sem("bo_added")
        n_bn, n_mv, n_arg, n_ln, n_r0, n_a, n_a2, n_b, n_r = (sem("n_" + s) for s in "bn mv arg ln r0 a a2 b r".split())
        n_xn, n_hi, n_lo, n_turned, n_stored = (sem("n_" + s) for s in "xn hi lo turned stored".split())
        p_mm, p_hi, p_lo = sem("p_mm"), sem("p_hi"), sem("p_lo")
        s_mm, s_max, s_sub, s_exp, s_sum, s_rec, s_prob, s_phi, s_plo = (
            sem("s_" + s) for s in "mm max sub exp sum rec prob phi plo".split())
        t_mm, t_ev = sem("t_mm"), sem("t_ev")
        o_mm, o_hi, o_lo = sem("o_mm"), sem("o_hi"), sem("o_lo")
        y_mm, y_add = sem("y_mm"), sem("y_add")
        u_mm, u_rel, u_sq, u_hi, u_lo = (sem("u_" + s) for s in "mm rel sq hi lo".split())
        g_mm, g_top, g_sum = sem("g_mm"), sem("g_top"), sem("g_sum")
        f_mm, f_rt, f_y, f_t, f_g, f_b, f_add = (sem("f_" + s) for s in "mm rt y t g b add".split())
        y_bn, y_mv, y_arg, y_ln, y_r0, y_a, y_a2, y_b, y_r = (sem("y_" + s) for s in "bn mv arg ln r0 a a2 b r".split())
        a_q, a_qhi, a_qlo, a_kv, a_kvhi, a_klo, a_kdup = (sem("a_" + s) for s in "q qhi qlo kv kvhi klo kdup".split())
        a_tq, a_tqev, a_tk, a_tkev = (sem("a_" + s) for s in "tq tqev tk tkev".split())
        b_s, b_max, b_sub, b_exp, b_sum, b_rec, b_phi, b_plo = (
            sem("b_" + s) for s in "s max sub exp sum rec phi plo".split())
        b_t, b_tev, b_o, b_on, b_ohi, b_olo = (sem("b_" + s) for s in "t tev o on ohi olo".split())
        a_to, a_toev, a_y, a_add = (sem("a_" + s) for s in "to toev y add".split())
        r_mm, r_lg, r_top, r_idx, r_f, r_m1, r_m2, r_mask = (sem("r_" + s) for s in "mm lg top idx f m1 m2 mask".split())
        e_mm, e_bias, e_rel, e_acc, x_done = (sem(s) for s in "e_mm e_bias e_rel e_acc x_done".split())
        z_ready = sem("z_ready")
        waits_passed = sem("waits_passed")

        def alone(eng, sem_, value):
            eng.wait_ge(sem_, value)
            eng.sem_inc(waits_passed, 1)

        block = stack.enter_context(nc.Block())

        def conv_of_group(g, j):
            return 4 + 3 * g + j

        @block.sync
        def _(sp):
            def x_chunk(c):
                sp.dma_start(X[:, c * TC:(c + 1) * TC, :],
                             x[c * CH:(c + 1) * CH, :].rearrange("(t p) d -> p t d", p=P)).then_inc(x_in[c], 16)

            x_chunk(0)

            def piece(k, src, conv_before):
                w(sp, w_lo, conv_before)
                n = src.shape[1]
                sp.dma_start(raw[:, kp(k), 0:n], src).then_inc(raw_in[kp(k)], 16)

            def kp(k):
                return k[1] if isinstance(k, tuple) else k % 2

            cuts = ((0, 2048), (2048, 3072), (3072, 5120))
            piece(0, wB[0, :, 0:2048], 0)
            piece(1, ctxT[0], 0)
            sp.dma_start(biases, biasB).then_inc(const_in, 16)
            sp.dma_start(lnwT, lnw).then_inc(const_in, 16)
            sp.dma_start(bob, bo.broadcast_to([P, D])).then_inc(const_in, 16)
            sp.dma_start(bgb, bg.broadcast_to([P, NE])).then_inc(const_in, 16)
            piece(2, wB[0, :, 2048:3072], 1)
            for c in range(1, NC):
                x_chunk(c)
            piece(3, wB[0, :, 3072:5120], 2)
            for c in range(1, NC):
                piece(3 + c, ctxT[c], 2 + c)
            for j, (a, b) in enumerate(cuts):
                piece(7 + j, wB[1, :, a:b], 6 + j)
            with sp.Fori(0, 3) as i:
                for par in range(2):
                    for j, (a, b) in enumerate(cuts):
                        k = 3 * par + j
                        piece((None, k % 2), wB[ds(i * 2 + 2 + par, 1), :, a:b].rearrange("a p n -> (a p) n"),
                              i * 6 + 9 + k)
            sp.wait_ge(bo_added, NT)
            sp.dma_start(gamb, gam.broadcast_to([P, D])).then_inc(gb_in, 16)
            sp.dma_start(betb, bet.broadcast_to([P, D])).then_inc(gb_in, 16)
            piece(28, up[:, 0:2048], 27)
            piece(29, up[:, 2048:4096], 28)
            piece(30, small0, 29)
            piece(31, down[:, 0:2048], 30)
            piece(32, down[:, 2048:4096], 33)
            piece(33, fc2, 34)
            piece(34, wq1, 35)
            piece(35, wkv1, 36)
            piece(36, wo1, 37)
            for m, e in enumerate(EXPERT_ORDER):
                piece(37 + m, we[e], 39 + m)
            sp.wait_ge(w_lo, 48)
            sp.dma_start(R3, be.broadcast_to([P, NE * D])).then_inc(be_in, 16)
            with sp.Fori(0, NT) as n:
                sp.wait_ge(x_done, n + 1)
                sp.dma_start(out[ds(n * P, P), :], X[:, ds(n, 1), :].rearrange("p a d -> p (a d)")).then_inc(out_done, 16)
            sp.wait_ge(out_done, 16 * NT)

        @block.gpsimd
        def _(pool):
            g = nc.gpsimd
            g.memset(ident, 0.0).then_inc(id_zero, 1)
            pool.wait_ge(id_zero, 1)
            g.affine_select(out=ident, in_=ident, compare_op=ALU.not_equal, fill=1.0, base=0,
                            pattern=[[-1, P]], channel_multiplier=1).then_inc(id_ready, 1)
            g.iota(iota8, pattern=[[1, NE]], base=0, channel_multiplier=0,
                   allow_small_or_imprecise_dtypes=True).then_inc(id_ready, 1)
            pool.wait_ge(const_in, 64)
            g.tensor_scalar(biases, biases, WS, 1.0, ALU.mult, ALU.mult).then_inc(bias_ready, 1)
            pool.wait_ge(bias_ready, 1)
            pool.wait_ge(id_ready, 2)
            g.memset(V[64:P, :, 1, :], 0.0).then_inc(z_ready, 1)
            pool.wait_ge(z_ready, 1)

            def split(conv, src, hi, lo, scale=WS, row_scale=None):
                if row_scale is None:
                    g.tensor_scalar(src, src, scale, 1.0, ALU.mult, ALU.mult).then_inc(w_scaled, 1)
                else:
                    for k in range(KC):
                        last = g.tensor_scalar(src[:, k * D:(k + 1) * D], src[:, k * D:(k + 1) * D],
                                               row_scale[:, k:k + 1], scale, ALU.mult, ALU.mult)
                    last.then_inc(w_scaled, 1)
                alone(pool, w_scaled, conv + 1)
                g.tensor_scalar(hi, src, 1.0, 1.0, ALU.mult, ALU.mult).then_inc(w_hi, 1)
                pool.wait_ge(w_hi, conv + 1)
                g.tensor_tensor(lo, src, hi, ALU.subtract).then_inc(w_lo, 1)

            def halves(region, off, total, start=0, n=None):
                n = total if n is None else n
                return region[:, off + start:off + start + n], region[:, off + total + start:off + total + start + n]

            def ctx_piece(k, c):
                pool.wait_ge(raw_in[k % 2], 16 * (k // 2 + 1))
                chunk = CT[:, c].rearrange("p s k n -> p s (k n)")
                split(k, raw[:, k % 2, :], chunk[:, 0], chunk[:, 1], 1.0)

            def group_piece(k, slot, arrivals, par, j):
                alone(pool, raw_in[slot], arrivals * 16)
                off, n = ((0, 2048), (4096, 1024), (6144, 2048))[j]
                hi, lo = halves(R2, GW * par + off, n)
                split(k, raw[:, slot, 0:n], hi, lo)

            def add_bo(c):
                for t in range(c * TC, (c + 1) * TC):
                    pool.wait_ge(n_xn, t + 1)
                    g.tensor_tensor(X[:, t, :], X[:, t, :], bob, ALU.add).then_inc(bo_added, 1)

            group_piece(0, 0, 1, 0, 0)
            ctx_piece(1, 0)
            group_piece(2, 0, 2, 0, 1)
            group_piece(3, 1, 2, 0, 2)
            ctx_piece(4, 1)
            add_bo(0)
            ctx_piece(5, 2)
            ctx_piece(6, 3)
            add_bo(1)
            for j in range(3):
                group_piece(7 + j, (7 + j) % 2, (7 + j) // 2 + 1, 1, j)
            add_bo(2)
            add_bo(3)
            with pool.Fori(0, 3) as i:
                for par in range(2):
                    pool.wait_ge(y_mm, i * 32 + 16 * (par + 1))
                    for j in range(3):
                        k = 3 * par + j
                        group_piece(i * 6 + 10 + k, k % 2, i * 3 + 5 + k // 2 + 1, par, j)

            def landed(k):
                pool.wait_ge(raw_in[k % 2], 16 * (k // 2 + 1))

            pool.wait_ge(y_mm, 7 * 16)
            for h in range(2):
                landed(28 + h)
                split(28 + h, raw[:, h, :], *halves(R2, 0, 4096, 2048 * h, 2048))
            pool.wait_ge(y_mm, 8 * 16)
            landed(30)
            split(30, raw[:, 0, 0:1024], *halves(R2, 8192, 1024))
            split(31, raw[:, 0, 1024:1536], *halves(R2, 18432, 512))
            split(32, raw[:, 0, 1536:1568], *halves(g0w, 0, 32))
            for h in range(2):
                landed(31 + h)
                split(33 + h, raw[:, (31 + h) % 2, :], *halves(R2, 10240, 4096, 2048 * h, 2048))
            landed(33)
            split(35, raw[:, 1, 0:1024], *halves(R2, 19456, 1024))
            landed(34)
            split(36, raw[:, 0, :], *halves(AW, 0, 2048), row_scale=lnwT)
            landed(35)
            split(37, raw[:, 1, 0:1024], *halves(AW, 4096, 1024))
            split(38, raw[:, 1, 1024:1056], *halves(g1w, 0, 32))
            landed(36)
            pool.wait_ge(n_lo, NT + TC)
            split(39, raw[:, 0, :], *halves(AW, 6144, 2048))
            for m, e in enumerate(EXPERT_ORDER):
                if m == 2:
                    pool.wait_ge(u_mm, 12 * NC)
                if m == 4:
                    pool.wait_ge(g_mm, NC)
                    g.memset(ks[:, :, :, 3, :], 0.0).then_inc(z_ready, 1)
                    g.memset(qs[:, :, 3, :], 0.0).then_inc(z_ready, 1)
                    pool.wait_ge(f_mm, 2 * NT)
                    pool.wait_ge(n_lo, 2 * NT + 1)
                    pool.wait_ge(z_ready, 3)
                    pool.wait_ge(w_lo, 44)
                    g.memset(V1[64:P, :, 1, :], 0.0).then_inc(z_ready, 1)
                    pool.wait_ge(z_ready, 4)
                landed(37 + m)
                split(40 + m, raw[:, (37 + m) % 2, :], *halves(R1 if e < 4 else R2, 4096 * (e % 4), 2048))

            def add_experts(n):
                for e in range(1, NE):
                    pool.wait_ge(e_rel, n * NE + e + 1)
                    if e > 1:
                        pool.wait_ge(e_acc, n * (NE - 1) + e - 1)
                    g.tensor_tensor(acc, acc, tmp[:, e % 2, :], ALU.add).then_inc(e_acc, 1)
                pool.wait_ge(e_acc, n * (NE - 1) + NE - 1)
                xt = X[:, ds(n, 1), :].rearrange("p a d -> p (a d)")
                g.tensor_tensor(xt, xt, acc, ALU.add).then_inc(x_done, 1)

            add_experts(0)
            with pool.Fori(1, NT) as n:
                add_experts(n)

        def newton(dve, s, k, n, sem_r0, sem_a, sem_a2, sem_b, sem_r):
            v_, r0, a_, b_, r_ = (s[:, m * k:(m + 1) * k] for m in (0, 2, 3, 4, 5))
            dve.wait_ge(sem_r0, n + 1)
            nc.vector.tensor_tensor(a_, v_, r0, ALU.mult).then_inc(sem_a, 1)
            dve.wait_ge(sem_a, n + 1)
            nc.vector.tensor_tensor(b_, a_, r0, ALU.mult).then_inc(sem_a2, 1)
            dve.wait_ge(sem_a2, n + 1)
            nc.vector.tensor_scalar(a_, b_, -0.5, 1.5, ALU.mult, ALU.add).then_inc(sem_b, 1)
            dve.wait_ge(sem_b, n + 1)
            nc.vector.tensor_tensor(r_, r0, a_, ALU.mult).then_inc(sem_r, 1)
            dve.wait_ge(sem_r, n + 1)

        def root(act, s, k, n, sem_arg, sem_ln, sem_r0):
            act.wait_ge(sem_arg, n + 1)
            nc.scalar.activation(s[:, k:2 * k], s[:, 0:k], ACT.Ln).then_inc(sem_ln, 1)
            act.wait_ge(sem_ln, n + 1)
            nc.scalar.activation(s[:, 2 * k:3 * k], s[:, k:2 * k], ACT.Exp, scale=-0.5).then_inc(sem_r0, 1)

        cbn = cstat[:, 0:24].rearrange("p (t k) -> p t k", t=TC)
        cmv = cstat[:, 24:32].rearrange("p (t k) -> p t k", t=TC)
        croot = cstat[:, 32:56]

        def chunk_stats(dve, c, tile):
            for t in range(TC):
                nc.vector.bn_stats(cbn[:, t, :], tile(t)).then_inc(n_bn, 1)
            for t in range(TC):
                alone(dve, n_bn, c * TC + (t + 1))
                nc.vector.bn_aggr(cmv[:, t, :], cbn[:, t, :]).then_inc(n_mv, 1)
            dve.wait_ge(n_mv, c * TC + TC)
            nc.vector.tensor_scalar(croot[:, 0:TC], cmv[:, :, 1], EPS, None, ALU.add).then_inc(n_arg, 1)

        def chunk_root(act, c):
            root(act, croot, TC, c, n_arg, n_ln, n_r0)

        def chunk_newton(dve, c):
            newton(dve, croot, TC, c, n_r0, n_a, n_a2, n_b, n_r)

        def chunk_xn(dve, n, t, xt, buf):
            if t >= 2:
                dve.wait_ge(n_lo, n - 1)
            nc.vector.tensor_scalar(buf[:, t % 2, :], xt, cmv[:, t, 0:1], croot[:, 5 * TC + t:5 * TC + t + 1],
                                    ALU.subtract, ALU.mult).then_inc(n_xn, 1)

        def tile_lo(dve, n, par, src):
            dve.wait_ge(n_hi, n + 1)
            w(dve, n_turned, n - 1)
            nc.vector.tensor_tensor(xs[:, par, 1, :], src, xs[:, par, 0, :], ALU.subtract).then_inc(n_lo, 1)

        def tile_hi(act, n, par, src):
            act.wait_ge(n_xn, n + 1)
            w(act, n_turned, n - 1)
            nc.scalar.activation(xs[:, par, 0, :], src, ACT.Copy).then_inc(n_hi, 1)

        def tile_turn(pe, n, par, bank, stored):
            pe.wait_ge(n_lo, n + 1)
            w(pe, n_stored, stored)
            for sk in range(2 * KC):
                last = pe.transpose(banks16[bank][:, sk * P:(sk + 1) * P],
                                    xs[:, par, sk // KC, (sk % KC) * P:(sk % KC + 1) * P], ident)
            last.then_inc(n_turned, 1)

        def tile_store(act, n, bank, dst):
            act.wait_ge(n_turned, n + 1)
            nc.scalar.activation(dst, banks16[bank][:, 0:2 * KC * P].rearrange("p (a n) -> p a n", a=2 * KC),
                                 ACT.Copy).then_inc(n_stored, 1)

        def norm_stats(dve, n, par, xt, rms=False):
            s = stat[:, 16 * par:16 * par + 16]
            nc.vector.bn_stats(s[:, 0:6], xt).then_inc(n_bn, 1)
            alone(dve, n_bn, n + 1)
            nc.vector.bn_aggr(s[:, 6:8], s[:, 0:6]).then_inc(n_mv, 1)
            dve.wait_ge(n_mv, n + 1)
            nc.vector.tensor_scalar(s[:, 8:9], s[:, 7:8], 1.0 + EPS if rms else 1.0, EPS * EPS if rms else EPS,
                                    ALU.mult, ALU.add).then_inc(n_arg, 1)

        def norm_root(act, n, par):
            root(act, stat[:, 16 * par + 8:16 * par + 14], 1, n - 24, n_arg, n_ln, n_r0)

        def norm_apply(dve, n, par, xt, buf):
            s = stat[:, 16 * par:16 * par + 16]
            newton(dve, s[:, 8:14], 1, n - 24, n_r0, n_a, n_a2, n_b, n_r)
            nc.vector.tensor_scalar(buf, xt, s[:, 6:7], s[:, 13:14], ALU.subtract, ALU.mult).then_inc(n_xn, 1)
            tile_lo(dve, n, par, buf)

        def x_tile(n):
            return X[:, n, :] if isinstance(n, int) else X[:, ds(n, 1), :].rearrange("p a d -> p (a d)")

        @block.tensor
        def _(pe):
            pe.wait_ge(id_ready, 1)
            for t in range(TC):
                tile_turn(pe, t, t % 2, 2 + t % 2, t - 1)

            def group3(dst, pairs, incs):
                m = len(pairs) * len(PASSES)
                k = 0
                for a, b in pairs:
                    for sa, sb_ in PASSES:
                        last = pe.matmul(dst, a(sa), b(sb_), start=(k == 0), stop=(k == m - 1))
                        k += 1
                if incs is not None:
                    last.then_inc(incs, 1)
                return last

            def b_proj(s, c, par, j):
                n = s * 6 + j
                w(pe, p_lo, n - 1)
                if isinstance(s, int) and s < NC and j == 4:
                    pe.wait_ge(w_lo, 3 if s == 0 else s + 4)
                if j < 5:
                    W_ = WBq[par] if j < 4 else WBkv[par]
                    src = XT if j < 4 else CT
                    cols = slice(j * P, (j + 1) * P) if j < 4 else slice(0, P)
                    group3(banks[j % 2], [(lambda p, k=k: W_[:, p, k, cols], lambda p, k=k: src[:, c, p, k, :])
                                          for k in range(KC)], p_mm)
                else:
                    for t in range(TC):
                        last = group3(banks[1][:, t * P:(t + 1) * P],
                                      [(lambda p, k=k: CT[:, c, p, k, t * P:(t + 1) * P],
                                        lambda p, k=k: WBkv[par][:, p, k, P:2 * P]) for k in range(KC)], None)
                    last.then_inc(p_mm, 1)

            def b_scores(s, hf):
                for blk in range(8):
                    b, hp = 4 * hf + blk // 2, blk % 2
                    last = group3(banks[2 + hf][:, blk * 64:(blk + 1) * 64],
                                  [(lambda p: qT[:, p, b, 2 * hp:2 * hp + 2, :].rearrange("p h l -> p (h l)"),
                                    lambda p: kT[:, p, b * 64:(b + 1) * 64])], None)
                last.then_inc(s_mm, 1)

            def b_turn(s, hf):
                pe.wait_ge(s_plo, s * 2 + hf + 1)
                for blk in range(8):
                    last = pe.transpose(banks16[4 + hf][:, blk * P:(blk + 1) * P],
                                        PPb[:, 8 * hf + blk].rearrange("p s m -> p (s m)"), ident)
                last.then_inc(t_mm, 1)

            def b_pv(s, jb):
                pe.wait_ge(t_ev, s * 2 + jb // 2 + 1)
                if jb == 0:
                    pe.wait_ge(p_lo, s * 6 + 6)
                if jb >= 2:
                    pe.wait_ge(o_lo, s * 4 + jb - 1)
                out_v = banks[6 + jb % 2].rearrange("p (h b l) -> p h b l", h=HG, b=2)
                for bb in range(2):
                    b = 2 * jb + bb
                    for p in range(2):
                        last = pe.matmul(out_v[:, :, bb, :], V[:, b, p, :],
                                         PTb[:, b * 256:(b + 1) * 256], start=(p == 0), stop=(p == 1))
                last.then_inc(o_mm, 1)

            def b_out(s, par, t):
                pe.wait_ge(o_lo, s * 4 + t + 1)
                if t >= 2:
                    pe.wait_ge(y_add, s * 4 + t - 1)
                group3(banks[4 + t % 2], [(lambda p, h=h: oT[:, p, h, t * P:(t + 1) * P],
                                           lambda p, h=h: WBo[par][:, p, h, :]) for h in range(HG)], y_mm)

            def b_step(s, c, par, last, norm=None):
                def turn(t):
                    if norm is not None:
                        tile_turn(pe, norm + t, t % 2, 2 + t % 2, norm + t - 1)

                pe.wait_ge(p_lo, s * 6 + 5)
                b_scores(s, 0)
                b_scores(s, 1)
                nxt = (s + 1, (c + 1) % NC, par if c < NC - 1 else 1 - par)

                def proj(j):
                    if not last:
                        b_proj(*nxt, j)

                if not last and c == NC - 1:
                    pe.wait_ge(w_lo, group_ready(s))
                for j in range(3):
                    proj(j)
                b_turn(s, 0)
                b_turn(s, 1)
                proj(3)
                b_pv(s, 0)
                b_pv(s, 1)
                proj(4)
                b_pv(s, 2)
                b_pv(s, 3)
                proj(5)
                for t in range(TC):
                    b_out(s, par, t)
                    if t % 2 == 0:
                        turn(t)
                        turn(t + 1)
                if norm is not None:
                    pe.wait_ge(n_stored, norm + TC)

            def group_ready(s):
                if isinstance(s, int):
                    return conv_of_group((s + 1) // NC, 2) + 1
                i, k = s_parts[0], s_parts[1]
                return i * 6 + (7 + 3 * (1 + (k + 1) // NC))

            s_parts = [None, None]
            pe.wait_ge(n_stored, TC)
            pe.wait_ge(w_lo, 1)
            for j in range(6):
                if j == 5:
                    pe.wait_ge(z_ready, 1)
                b_proj(0, 0, 0, j)
                if j in (2, 3):
                    for t in (0, 1) if j == 2 else (2, 3):
                        tile_turn(pe, TC + t, t % 2, 2 + t % 2, TC + t - 1)
            pe.wait_ge(n_stored, 2 * TC)
            for s in range(NC):
                b_step(s, s, 0, False, (s + 2) * TC if s < 2 else None)
            with pe.Fori(0, 3) as i:
                for k in range(8):
                    s_parts[0], s_parts[1] = i, k
                    b_step(i * 8 + (NC + k), k % NC, 1 - k // NC, False)
            for s in range(28, 32):
                b_step(s, s % NC, 1, s == 31, NT if s == 31 else None)

            pe.wait_ge(w_lo, 30)

            def ffn_chunk(c, last):
                for j in range(12):
                    if 2 <= j < 10:
                        pe.wait_ge(u_rel, c * 8 + j - 1)
                    elif j >= 10:
                        pe.wait_ge(u_lo, c * 12 + j - 1)
                    dst = banks[j % 2]
                    if j < 8:
                        group3(dst, [(lambda p, k=k: Wup[:, p, k, j * P:(j + 1) * P], lambda p, k=k: T1[:, p, k, :])
                                     for k in range(KC)], u_mm)
                    elif j < 10:
                        m = j - 8
                        if m == 0:
                            pe.wait_ge(w_lo, 33)
                        group3(dst, [(lambda p, k=k: Wfc1[:, p, k, m * P:(m + 1) * P], lambda p, k=k: T1[:, p, k, :])
                                     for k in range(KC)], u_mm)
                    else:
                        m = j - 10
                        if m == 0:
                            for t in range(TC):
                                mm = group3(banks[5][:, t * NE:(t + 1) * NE],
                                            [(lambda p, k=k: T1[:, p, k, t * P:(t + 1) * P],
                                              lambda p, k=k: Wg0[:, p, k, :]) for k in range(KC)], None)
                            mm.then_inc(g_mm, 1)
                            pe.wait_ge(u_lo, c * 12 + 10)
                        group3(dst, [(lambda p, k=k: Wex[:, p, k, m * P:(m + 1) * P], lambda p, k=k: xlT[:, p, k, :])
                                     for k in range(2)], u_mm)
                for t in range(TC):
                    if t >= 2:
                        pe.wait_ge(f_y, c * TC + t - 1)
                    bd, bf = (6, 7) if t % 2 == 0 else (2, 3)
                    tt = slice(t * P, (t + 1) * P)
                    if t == 0:
                        pe.wait_ge(w_lo, 35)
                        pe.wait_ge(u_lo, c * 12 + 12)
                    group3(banks[bd], [(lambda p, k=k: hT[:, p, k, tt], lambda p, k=k: Wdn[:, p, k, :])
                                       for k in range(INT // P)], f_mm)
                    if t == 0:
                        pe.wait_ge(w_lo, 36)
                    group3(banks[bf], [(lambda p, k=k: eoT[:, p, k, tt], lambda p, k=k: Wfc2[:, p, k, :])
                                       for k in range(2)], f_mm)
                    n = c * TC + NT + TC
                    if last and t == 0:
                        tile_turn(pe, 32, 0, 4, 32)
                    elif not last and t < 2:
                        for u in (2 * t, 2 * t + 1):
                            tile_turn(pe, n + u, u % 2, 4 + u % 2, n + (u - 1))
                if not last:
                    pe.wait_ge(n_stored, n + TC)

            with pe.Fori(0, NC - 1) as c:
                ffn_chunk(c, False)
            ffn_chunk(NC - 1, True)

            def attn(n, par, ffn, nxt):
                pe.wait_ge(n_stored, attn_norm(n))
                w(pe, a_add, n)
                group3(banks[0], [(lambda p, k=k: TA[:, p, k, :], lambda p, k=k: Wq1[:, p, k, :]) for k in range(KC)], a_q)
                ctx_t = ctx_tile(n)
                group3(banks[1][:, 0:256], [(lambda p, k=k: ctx_t(p, k), lambda p, k=k: Wkv1[:, p, k, :])
                                            for k in range(KC)], a_kv)

                def expert(*es):
                    if ffn is not None:
                        for e in es:
                            experts(n - 1, e)

                if ffn is not None:
                    tile_turn(pe, ffn, 0, 7, ffn)
                    gate(n - 1, ffn)
                expert(0)
                pe.wait_ge(a_qlo, n + 1)
                if isinstance(n, int) and n == 0:
                    pe.wait_ge(z_ready, 4)
                for t in range(16):
                    bank, k = 4 + t // 8, t % 8
                    last = pe.transpose(banks16[bank][:, k * P:(k + 1) * P],
                                        qs[:, 2 * t:2 * t + 2].rearrange("p h s d -> p (h s d)"), ident)
                last.then_inc(a_tq, 1)
                pe.wait_ge(a_kdup, n + 1)
                for g in range(NG):
                    last = pe.transpose(banks16[6][:, g * P:(g + 1) * P], ks[:, g].rearrange("p j s d -> p (j s d)"), ident)
                last.then_inc(a_tk, 1)
                expert(1)

                def scores(b):
                    pe.wait_ge(a_tqev, n + 1)
                    pe.wait_ge(a_tkev, n + 1)
                    if b == 0:
                        pe.wait_ge(a_klo, n + 1)
                        pe.wait_ge(a_kvhi, n + 1)
                    else:
                        pe.wait_ge(b_sub, n * 2 + 1)
                    for blk in range(16):
                        j, g = blk % 2, blk // 2
                        rows = slice(64 * j, 64 * j + 48)
                        last = pe.matmul(banks[j][:, g * 64:(g + 1) * 64],
                                         qT1[rows, b, 2 * g:2 * g + 2, :].rearrange("p t l -> p (t l)"),
                                         kT1[rows, g, b * 64:(b + 1) * 64], start=True, stop=True)
                    last.then_inc(b_s, 1)

                def turn(b):
                    pe.wait_ge(b_plo, n * 2 + b + 1)
                    if b == 1:
                        pe.wait_ge(b_tev, n * 2 + 1)
                    for blk in range(16):
                        last = pe.transpose(banks16[4 + blk // 8][:, (blk % 8) * P:(blk % 8 + 1) * P],
                                            PP1[:, blk].rearrange("p s m -> p (s m)"), ident)
                    last.then_inc(b_t, 1)

                def pv(b):
                    pe.wait_ge(b_tev, n * 2 + b + 1)
                    if b == 1:
                        pe.wait_ge(b_on, n * 2 + 1)
                    for blk in range(16):
                        g = blk % NG
                        for p in range(2):
                            last = pe.matmul(banks[6][:, blk * 16:(blk + 1) * 16], PT1[:, blk * P:(blk + 1) * P],
                                             V1[:, b, p, g * 16:(g + 1) * 16], start=(p == 0), stop=(p == 1))
                    last.then_inc(b_o, 1)

                scores(0)
                expert(2)
                scores(1)
                expert(3)
                turn(0)
                expert(4)
                pv(0)
                turn(1)
                expert(5)
                pv(1)
                expert(6)
                pe.wait_ge(b_olo, n * 2 + 2)
                for b in range(2):
                    for s in range(2):
                        for q in range(2):
                            k = b * 4 + s * 2 + q
                            last = pe.transpose(banks16[7][:, k * P:(k + 1) * P], onh[:, b, s, q * P:(q + 1) * P], ident)
                last.then_inc(a_to, 1)
                pe.wait_ge(a_toev, n + 1)
                if nxt is not None:
                    tile_turn(pe, nxt, 1, 7, nxt)
                group3(banks[0], [(lambda p, qu=qu: oT1[:, 2 * p + qu // 2, qu % 2, :], lambda p, qu=qu: Wo1[:, p, qu, :])
                                  for qu in range(4)], a_y)
                expert(7)

            def attn_norm(n):
                return 33 if isinstance(n, int) and n == 0 else n * 2 + 32

            def ctx_tile(n):
                if isinstance(n, int):
                    return lambda p, k: CT[:, n // TC, p, k, (n % TC) * P:(n % TC + 1) * P]
                return ct_of[0]

            ct_of = [None]

            def gate(n, norm):
                pe.wait_ge(n_stored, norm + 1)
                pe.wait_ge(a_klo, n + 2) if attn_running[0] else None
                pe.wait_ge(a_kvhi, n + 2) if attn_running[0] else None
                group3(banks[1][:, 256:256 + NE], [(lambda p, k=k: TF[:, p, k, :], lambda p, k=k: Wg1[:, p, k, :])
                                                   for k in range(KC)], r_mm)

            attn_running = [True]

            def experts(n, e):
                if isinstance(n, int) and n == 0:
                    pe.wait_ge(w_lo, 41 + EXPERT_ORDER.index(e))
                if not (isinstance(n, int) and n == 0 and e < 2):
                    pe.wait_ge(e_bias, n * NE + e - 1 if e > 0 else n * NE)
                group3(banks[2 + e % 2], [(lambda p, k=k: TF[:, p, k, :], lambda p, k=k: We[e][:, p, k, :])
                                          for k in range(KC)], e_mm)

            pe.wait_ge(w_lo, 40)
            attn(0, 0, None, 33)
            attn(1, 1, 34, 35)
            with pe.Fori(0, 3) as i:
                for k in range(2, 6):
                    n = i * 4 + k
                    ch = k // TC
                    ct_of[0] = lambda p, kc, ch=ch, k=k: CT[:, ds(i + ch, 1), p, kc, (k % TC) * P:(k % TC + 1) * P]\
                        .rearrange("p a n -> p (a n)")
                    attn(n, k % 2, n * 2 + 32, n * 2 + 33)
            for n in range(14, NT):
                attn(n, n % 2, n * 2 + 32, n * 2 + 33 if n < NT - 1 else None)
            attn_running[0] = False
            tile_turn(pe, 63, 1, 7, 63)
            gate(NT - 1, 63)
            for e in range(NE):
                experts(NT - 1, e)

        @block.scalar
        def _(act):
            sc = nc.scalar
            act.preload_act_table_set("natural_log_exp_and_others")

            def x_turned(n, t):
                tile_store(act, n, 2 + t % 2, XT[:, n // TC, :, :, t * P:(t + 1) * P].rearrange("p s k n -> p (s k) n"))

            chunk_root(act, 0)
            for t in range(TC):
                tile_hi(act, t, t % 2, xnB[:, t % 2, :])
                if t > 0:
                    x_turned(t - 1, t - 1)
            x_turned(TC - 1, TC - 1)

            def bias_col(g, a):
                return biases[:, ds(g + a, 1)] if not isinstance(g, int) else biases[:, g + a:g + a + 1]

            def proj_hi(s, g, j):
                alone(act, p_mm, s * 6 + j + 1)
                if j < 4:
                    sc.activation(qT[:, 0, :, j, :], banks[j % 2].rearrange("p (b l) -> p b l", l=64), ACT.Identity, bias=bias_col(g * HG, j)).then_inc(p_hi, 1)
                elif j == 4:
                    sc.activation(kT[:, 0, :], banks[0], ACT.Identity, bias=bias_col(g, 32)).then_inc(p_hi, 1)
                else:
                    v = banks[1].rearrange("p (t d) -> p t d", t=TC)
                    for odd in range(2):
                        for half in range(2):
                            last = sc.activation(V[64 * half:64 * half + 64, odd:BC:2, 0, :],
                                                 v[64 * odd:64 * odd + 64], ACT.Copy, scale=UN)
                    last.then_inc(p_hi, 1)

            def o_part(s, g, jb):
                alone(act, o_mm, s * 4 + jb + 1)
                sc.activation(oT[:, 0, :, jb * P:(jb + 1) * P], banks[6 + jb % 2].rearrange("p (h n) -> p h n", h=HG), ACT.Identity,
                              bias=bias_col(g, 40)).then_inc(o_hi, 1)

            def b_step(s, g, gn, last, norm=None):
                def proj(j):
                    if not last:
                        proj_hi(s + 1, gn, j)

                def hi(t):
                    if norm is not None:
                        tile_hi(act, norm + t, t % 2, xnB[:, t % 2, :])

                def turned_x(t):
                    if norm is not None and norm < NT:
                        x_turned(norm + t, t)
                    elif norm is not None:
                        tile_store(act, norm + t, 2 + t % 2, T1[:, :, :, t * P:(t + 1) * P].rearrange("p s k n -> p (s k) n"))

                def exp(hf):
                    act.wait_ge(s_sub, s * 2 + hf + 1)
                    e = Eb[:, 8 * hf:8 * hf + 8, :]
                    sc.activation(e, e, ACT.Exp, scale=SC0).then_inc(s_exp, 1)

                def phi(hf):
                    act.wait_ge(s_prob, s * 2 + hf + 1)
                    sc.activation(PPb[:, 8 * hf:8 * hf + 8, 0, :], Eb[:, 8 * hf:8 * hf + 8, :], ACT.Copy).then_inc(s_phi, 1)

                def turned(hf):
                    act.wait_ge(t_mm, s * 2 + hf + 1)
                    sc.activation(PTb[:, hf * 1024:(hf + 1) * 1024], banks16[4 + hf], ACT.Copy).then_inc(t_ev, 1)

                exp(0)
                exp(1)
                proj(0)
                phi(0)
                phi(1)
                proj(1)
                proj(2)
                turned(0)
                turned(1)
                if norm is not None:
                    chunk_root(act, norm // TC)
                proj(3)
                o_part(s, g, 0)
                o_part(s, g, 1)
                hi(0)
                proj(4)
                hi(1)
                o_part(s, g, 2)
                o_part(s, g, 3)
                proj(5)
                turned_x(0)
                hi(2)
                turned_x(1)
                hi(3)
                turned_x(2)
                turned_x(3)

            act.wait_ge(bias_ready, 1)
            chunk_root(act, 1)
            proj_hi(0, 0, 0)
            tile_hi(act, 4, 0, xnB[:, 0, :])
            tile_hi(act, 5, 1, xnB[:, 1, :])
            proj_hi(0, 0, 1)
            proj_hi(0, 0, 2)
            x_turned(4, 0)
            tile_hi(act, 6, 0, xnB[:, 0, :])
            x_turned(5, 1)
            tile_hi(act, 7, 1, xnB[:, 1, :])
            proj_hi(0, 0, 3)
            x_turned(6, 2)
            x_turned(7, 3)
            proj_hi(0, 0, 4)
            proj_hi(0, 0, 5)
            for s in range(NC):
                b_step(s, 0, (s + 1) // NC, False, (s + 2) * TC if s < 2 else None)
            with act.Fori(0, 3) as i:
                for k in range(8):
                    b_step(i * 8 + (NC + k), i * 2 + (1 + k // NC), i * 2 + (1 + (k + 1) // NC), False)
            for s in range(28, 32):
                b_step(s, s // NC, (s + 1) // NC, s == 31, NT if s == 31 else None)

            def ffn_chunk(c, last):
                for j in range(12):
                    m = c * 12 + j
                    act.wait_ge(u_mm, m + 1)
                    if j < 8:
                        sc.activation(rel[:, j % 2, :], banks[j % 2], ACT.Relu, scale=UN).then_inc(u_rel, 1)
                        act.wait_ge(u_sq, c * 8 + j + 1)
                        sc.activation(hT[:, 0, j, :], h32, ACT.Copy).then_inc(u_hi, 1)
                    else:
                        dst = (xlT if j < 10 else eoT)[:, 0, j % 2, :]
                        sc.activation(dst, banks[j % 2], ACT.Copy, scale=UN).then_inc(u_hi, 1)
                n = c * TC + NT + TC

                def store(t):
                    tile_store(act, n + t, 4 + t % 2, T1[:, :, :, t * P:(t + 1) * P].rearrange("p s k n -> p (s k) n"))

                if last:
                    norm_root(act, 32, 0)
                    tile_hi(act, 32, 0, rel[:, 0, :])
                    tile_store(act, 32, 4, TA.rearrange("p s k n -> p (s k) n"))
                else:
                    chunk_root(act, c + 5)
                    tile_hi(act, n, 0, rel[:, 0, :])
                    tile_hi(act, n + 1, 1, rel[:, 1, :])
                for t in range(TC):
                    if t == 0 and not last:
                        store(0)
                        tile_hi(act, n + 2, 0, rel[:, 0, :])
                    root(act, ystat[:, 8:14], 1, c * TC + t, y_arg, y_ln, y_r0)
                    if t == 0 and not last:
                        store(1)
                        tile_hi(act, n + 3, 1, rel[:, 1, :])
                    if t == 1 and not last:
                        store(2)
                        store(3)

            with act.Fori(0, NC - 1) as c:
                ffn_chunk(c, False)
            ffn_chunk(NC - 1, True)

            def norm_hi(idx, par):
                norm_root(act, idx, par)
                tile_hi(act, idx, par, yn)

            def norm_store(idx, dst):
                tile_store(act, idx, 7, dst.rearrange("p s k n -> p (s k) n"))

            def expert(n, e):
                act.wait_ge(e_bias, n * NE + e + 1)
                if e == 0:
                    act.wait_ge(r_mask, n + 1)
                    w(act, x_done, n)
                dst = acc if e == 0 else tmp[:, e % 2, :]
                sc.activation(dst, tmp[:, e % 2, :], ACT.Relu, scale=msk[:, 16 + e:17 + e]).then_inc(e_rel, 1)

            def attn(n, ffn, nxt):
                act.wait_ge(a_q, n + 1)
                q = banks[0].rearrange("p (h d) -> p h d", h=32)
                sc.activation(qs[:, :, 0, :], q, ACT.Copy)
                sc.activation(qs[:, :, 2, :], q, ACT.Copy).then_inc(a_qhi, 1)
                act.wait_ge(a_kv, n + 1)
                k = banks[1][:, 0:P].rearrange("p (g d) -> p g d", g=NG)
                sc.activation(ks[:, :, 0, 0, :], k, ACT.Copy)
                sc.activation(ks[:, :, 0, 1, :], k, ACT.Copy)
                for b in range(2):
                    for half in range(2):
                        last = sc.activation(V1[64 * half:64 * half + 64, b, 0, :],
                                             banks[1][64 * b:64 * b + 64, P:2 * P], ACT.Copy, scale=UN)
                last.then_inc(a_kvhi, 1)
                if ffn is not None:
                    norm_store(ffn, TF)

                def ex(*es):
                    if ffn is not None:
                        for e in es:
                            expert(n - 1, e)

                ex(0)
                act.wait_ge(a_tq, n + 1)
                for h in range(2):
                    last = sc.activation(qT1[:, :, 8 * h:8 * h + 8, :].rearrange("p b t l -> p t b l"),
                                         banks16[4 + h].rearrange("p (t b l) -> p t b l", t=8, b=2), ACT.Copy)
                last.then_inc(a_tqev, 1)
                act.wait_ge(a_tk, n + 1)
                sc.activation(kT1, banks16[6].rearrange("p (t n) -> p t n", t=8), ACT.Copy).then_inc(a_tkev, 1)
                ex(1)
                for b in range(2):
                    v = n * 2 + b + 1
                    if b == 1:
                        ex(3)
                    act.wait_ge(b_sub, v)
                    sc.activation(E1, E1, ACT.Exp, scale=SC1).then_inc(b_exp, 1)
                    act.wait_ge(b_exp, v)
                    if b == 1:
                        act.wait_ge(b_t, v - 1)
                    sc.activation(PP1[:, :, 0, :], E1, ACT.Copy, scale=PS).then_inc(b_phi, 1)
                    if b == 0:
                        ex(2)
                        act.wait_ge(b_t, v)
                        for h in range(2):
                            last = sc.activation(PT1[:, h * 1024:(h + 1) * 1024], banks16[4 + h], ACT.Copy)
                        last.then_inc(b_tev, 1)
                act.wait_ge(b_on, n * 2 + 1)
                sc.activation(onh[:, 0, 0, :], on32, ACT.Copy).then_inc(b_ohi, 1)
                ex(4)
                act.wait_ge(b_t, n * 2 + 2)
                act.wait_ge(b_o, n * 2 + 1)
                for h in range(2):
                    last = sc.activation(PT1[:, h * 1024:(h + 1) * 1024], banks16[4 + h], ACT.Copy)
                last.then_inc(b_tev, 1)
                ex(5)
                if nxt is not None:
                    norm_hi(nxt, 1)
                act.wait_ge(b_on, n * 2 + 2)
                sc.activation(onh[:, 1, 0, :], on32, ACT.Copy).then_inc(b_ohi, 1)
                ex(6)
                act.wait_ge(a_to, n + 1)
                for b in range(2):
                    last = sc.activation(oT1[:, :, :, b * 64:(b + 1) * 64],
                                         banks16[7][:, b * 512:(b + 1) * 512].rearrange("p (s u l) -> p s u l", s=4, u=2),
                                         ACT.Copy)
                last.then_inc(a_toev, 1)
                if nxt is not None:
                    norm_store(nxt, TA)
                norm_hi(nxt + 1 if nxt is not None else 63, 0 if nxt is not None else 1)
                ex(7)

            attn(0, None, 33)
            attn(1, 34, 35)
            with act.Fori(0, 6) as i:
                for k in range(2, 4):
                    n = i * 2 + k
                    attn(n, n * 2 + 32, n * 2 + 33)
            attn(NT - 2, 2 * (NT - 2) + 32, 2 * (NT - 2) + 33)
            attn(NT - 1, 2 * (NT - 1) + 32, None)
            norm_store(63, TF)
            for e in range(NE):
                expert(NT - 1, e)

        @block.vector
        def _(dve):
            v = nc.vector

            def xn_of(n, t, tile):
                chunk_xn(dve, n, t, tile, xnB)

            def lo_of(n, t):
                tile_lo(dve, n, t % 2, xnB[:, t % 2, :])

            dve.wait_ge(x_in[0], 16)
            chunk_stats(dve, 0, x_tile)
            chunk_newton(dve, 0)
            for t in range(TC):
                xn_of(t, t, x_tile(t))
                if t > 0:
                    lo_of(t - 1, t - 1)
            lo_of(TC - 1, TC - 1)

            def bias_col(g, a):
                return biases[:, ds(g + a, 1)] if not isinstance(g, int) else biases[:, g + a:g + a + 1]

            def lo(dst, src, bias, hi, done):
                v.scalar_tensor_tensor(out=dst, in0=src, scalar=bias, in1=hi, op0=ALU.add, op1=ALU.subtract).then_inc(done, 1)

            def proj_lo(s, g, j):
                dve.wait_ge(p_hi, s * 6 + j + 1)
                if j < 4:
                    lo(qT[:, 1, :, j, :], banks[j % 2].rearrange("p (b l) -> p b l", l=64), bias_col(g * HG, j), qT[:, 0, :, j, :], p_lo)
                elif j == 4:
                    lo(kT[:, 1, :], banks[0], bias_col(g, 32), kT[:, 0, :], p_lo)
                else:
                    vv = banks[1].rearrange("p (t d) -> p t d", t=TC)
                    for odd in range(2):
                        h = slice(64 * odd, 64 * odd + 64)
                        last = v.scalar_tensor_tensor(out=V[0:64, odd:BC:2, 1, :], in0=vv[h], scalar=UN,
                                                      in1=V[h, odd:BC:2, 0, :], op0=ALU.mult, op1=ALU.subtract)
                    last.then_inc(p_lo, 1)

            def b_step(s, g, gn, last, norm=None):
                first = None if norm is None else norm % NT

                def stats():
                    if norm is not None:
                        if norm < NT:
                            dve.wait_ge(x_in[norm // TC], 16)
                        chunk_stats(dve, norm // TC, lambda t: x_tile(first + t))

                def xnorm(t):
                    if norm is not None:
                        xn_of(norm + t, t, x_tile(first + t))

                def xlo(t):
                    if norm is not None:
                        lo_of(norm + t, t)

                def proj(j):
                    if not last:
                        proj_lo(s + 1, gn, j)

                def blocks(hf):
                    return slice(8 * hf, 8 * hf + 8)

                def wide(cols):
                    return cols.unsqueeze(2).to_broadcast([P, 8, 64])

                def shift(hf):
                    n = s * 2 + hf + 1
                    S = banks[2 + hf].rearrange("p (k m) -> p k m", m=64)
                    dve.wait_ge(s_mm, n)
                    v.tensor_reduce(smx[:, blocks(hf)], S, AX.X, ALU.max).then_inc(s_max, 1)
                    dve.wait_ge(s_max, n)
                    v.tensor_tensor(Eb[:, blocks(hf), :], S, wide(smx[:, blocks(hf)]), ALU.subtract).then_inc(s_sub, 1)

                def prob(hf):
                    n = s * 2 + hf + 1
                    sums, recs = smx[:, 16 + 8 * hf:24 + 8 * hf], smx[:, 32 + 8 * hf:40 + 8 * hf]
                    dve.wait_ge(s_exp, n)
                    v.tensor_reduce(sums, Eb[:, blocks(hf), :], AX.X, ALU.add).then_inc(s_sum, 1)
                    dve.wait_ge(s_sum, n)
                    v.reciprocal(recs, sums).then_inc(s_rec, 1)
                    dve.wait_ge(s_rec, n)
                    v.scalar_tensor_tensor(out=Eb[:, blocks(hf), :], in0=Eb[:, blocks(hf), :], scalar=PS,
                                           in1=wide(recs), op0=ALU.mult, op1=ALU.mult).then_inc(s_prob, 1)

                def plo(hf):
                    dve.wait_ge(s_phi, s * 2 + hf + 1)
                    v.tensor_tensor(PPb[:, blocks(hf), 1, :], Eb[:, blocks(hf), :], PPb[:, blocks(hf), 0, :],
                                    ALU.subtract).then_inc(s_plo, 1)

                def olo(jb):
                    dve.wait_ge(o_hi, s * 4 + jb + 1)
                    cols = slice(jb * P, (jb + 1) * P)
                    lo(oT[:, 1, :, cols], banks[6 + jb % 2].rearrange("p (h n) -> p h n", h=HG), bias_col(g, 40),
                       oT[:, 0, :, cols], o_lo)

                shift(0)
                shift(1)
                prob(0)
                prob(1)
                proj(0)
                plo(0)
                plo(1)
                proj(1)
                stats()
                proj(2)
                proj(3)
                if norm is not None:
                    chunk_newton(dve, norm // TC)
                xnorm(0)
                xnorm(1)
                olo(0)
                olo(1)
                proj(4)
                xlo(0)
                xlo(1)
                olo(2)
                olo(3)
                proj(5)
                xnorm(2)
                for t in range(TC):
                    dve.wait_ge(y_mm, s * 4 + t + 1)
                    if isinstance(s, int) and s < NC:
                        dve.wait_ge(bo_added, s * TC + t + 1)
                    xt = x_tile(((s if isinstance(s, int) else s_k[0]) % NC) * TC + t)
                    v.scalar_tensor_tensor(out=xt, in0=banks[4 + t % 2], scalar=UN2, in1=xt,
                                           op0=ALU.mult, op1=ALU.add).then_inc(y_add, 1)
                    if t == 0:
                        xlo(2)
                    if t == 1:
                        xnorm(3)
                        xlo(3)

            s_k = [0]
            dve.wait_ge(x_in[1], 16)
            chunk_stats(dve, 1, lambda t: x_tile(TC + t))
            dve.wait_ge(bias_ready, 1)
            proj_lo(0, 0, 0)
            chunk_newton(dve, 1)
            xn_of(4, 0, x_tile(4))
            xn_of(5, 1, x_tile(5))
            proj_lo(0, 0, 1)
            lo_of(4, 0)
            lo_of(5, 1)
            proj_lo(0, 0, 2)
            xn_of(6, 2, x_tile(6))
            lo_of(6, 2)
            xn_of(7, 3, x_tile(7))
            lo_of(7, 3)
            for j in range(3, 6):
                proj_lo(0, 0, j)
            for s in range(NC):
                b_step(s, 0, (s + 1) // NC, False, (s + 2) * TC if s < 2 else None)
            with dve.Fori(0, 3) as i:
                for k in range(8):
                    s_k[0] = k
                    b_step(i * 8 + (NC + k), i * 2 + (1 + k // NC), i * 2 + (1 + (k + 1) // NC), False)
            for s in range(28, 32):
                b_step(s, s // NC, (s + 1) // NC, s == 31, NT if s == 31 else None)

            dve.wait_ge(y_add, 128)
            dve.wait_ge(gb_in, 32)

            def ffn_chunk(c, last):
                for j in range(12):
                    if j == 10:
                        alone(dve, g_mm, c + 1)
                        for t in range(TC):
                            mm = v.max(m8[:, t * NE:(t + 1) * NE], banks[5][:, t * NE:(t + 1) * NE])
                        mm.then_inc(g_top, 1)
                        dve.wait_ge(g_top, c + 1)
                        for t in range(TC):
                            mm = v.tensor_scalar(rsum[:, t:t + 1], m8[:, t * NE:t * NE + 1],
                                                 m8[:, t * NE + 1:t * NE + 2], UN2, ALU.add, ALU.mult)
                        mm.then_inc(g_sum, 1)
                    if j < 8:
                        dve.wait_ge(u_rel, c * 8 + j + 1)
                        if j > 0:
                            dve.wait_ge(u_lo, c * 12 + j)
                        v.tensor_tensor(h32, rel[:, j % 2, :], rel[:, j % 2, :], ALU.mult).then_inc(u_sq, 1)
                        dve.wait_ge(u_hi, c * 12 + j + 1)
                        v.tensor_tensor(hT[:, 1, j, :], h32, hT[:, 0, j, :], ALU.subtract).then_inc(u_lo, 1)
                    else:
                        dst = xlT if j < 10 else eoT
                        dve.wait_ge(u_hi, c * 12 + j + 1)
                        v.scalar_tensor_tensor(out=dst[:, 1, j % 2, :], in0=banks[j % 2], scalar=UN,
                                               in1=dst[:, 0, j % 2, :], op0=ALU.mult, op1=ALU.subtract).then_inc(u_lo, 1)
                m = c * TC + NT + TC

                def xnorm(t):
                    chunk_xn(dve, m + t, t, x_tile(c * TC + TC + t), rel)

                def xlo(t):
                    tile_lo(dve, m + t, t % 2, rel[:, t % 2, :])

                if last:
                    norm_stats(dve, 32, 0, x_tile(0), True)
                    norm_apply(dve, 32, 0, x_tile(0), rel[:, 0, :])
                else:
                    chunk_stats(dve, c + 5, lambda t: x_tile(c * TC + TC + t))
                    chunk_newton(dve, c + 5)
                    xnorm(0)
                    xnorm(1)
                    xlo(0)
                    xlo(1)
                    xnorm(2)
                dve.wait_ge(g_sum, c + 1)
                for t in range(TC):
                    n = c * TC + t
                    bd, bf = (6, 7) if t % 2 == 0 else (2, 3)
                    xt = x_tile(n)
                    s = ystat
                    y = yn
                    dve.wait_ge(f_mm, n * 2 + 2)
                    v.tensor_scalar(h32, banks[bf], rsum[:, t:t + 1], None, ALU.mult).then_inc(f_rt, 1)
                    dve.wait_ge(f_rt, n + 1)
                    v.scalar_tensor_tensor(out=y, in0=banks[bd], scalar=UN, in1=h32, op0=ALU.mult, op1=ALU.add).then_inc(f_y, 1)
                    dve.wait_ge(f_y, n + 1)
                    v.bn_stats(s[:, 0:6], y).then_inc(y_bn, 1)
                    alone(dve, y_bn, n + 1)
                    v.bn_aggr(s[:, 6:8], s[:, 0:6]).then_inc(y_mv, 1)
                    dve.wait_ge(y_mv, n + 1)
                    v.tensor_scalar(s[:, 8:9], s[:, 7:8], EPS, None, ALU.add).then_inc(y_arg, 1)
                    if t == 0 and not last:
                        xlo(2)
                        xnorm(3)
                        xlo(3)
                    newton(dve, s[:, 8:14], 1, n, y_r0, y_a, y_a2, y_b, y_r)
                    v.tensor_scalar(y, y, s[:, 6:7], s[:, 13:14], ALU.subtract, ALU.mult).then_inc(f_t, 1)
                    dve.wait_ge(f_t, n + 1)
                    v.tensor_tensor(y, y, gamb, ALU.mult).then_inc(f_g, 1)
                    dve.wait_ge(f_g, n + 1)
                    v.tensor_tensor(y, y, betb, ALU.add).then_inc(f_b, 1)
                    dve.wait_ge(f_b, n + 1)
                    v.tensor_tensor(xt, xt, y, ALU.add).then_inc(f_add, 1)

            with dve.Fori(0, NC - 1) as c:
                ffn_chunk(c, False)
            ffn_chunk(NC - 1, True)

            def mask_of(n):
                dve.wait_ge(r_mm, n + 1)
                v.scalar_tensor_tensor(out=lgt, in0=banks[1][:, 256:256 + NE], scalar=UN, in1=bgb,
                                       op0=ALU.mult, op1=ALU.add).then_inc(r_lg, 1)
                alone(dve, r_lg, n + 1)
                v.max(m8[:, 0:8], lgt).then_inc(r_top, 1)
                alone(dve, r_top, n + 1)
                v.max_index(idx8, m8[:, 0:8], lgt).then_inc(r_idx, 1)
                dve.wait_ge(r_idx, n + 1)
                v.tensor_copy(idxf, idx8).then_inc(r_f, 1)
                dve.wait_ge(r_f, n + 1)
                v.tensor_scalar(msk[:, 0:8], iota8, idxf[:, 0:1], 0.5, ALU.is_equal, ALU.mult).then_inc(r_m1, 1)
                v.tensor_scalar(msk[:, 8:16], iota8, idxf[:, 1:2], 0.5, ALU.is_equal, ALU.mult).then_inc(r_m2, 1)
                dve.wait_ge(r_m1, n + 1)
                dve.wait_ge(r_m2, n + 1)
                w(dve, e_rel, n * NE)
                v.tensor_tensor(msk[:, 16:24], msk[:, 0:8], msk[:, 8:16], ALU.add).then_inc(r_mask, 1)

            def expert(n, e):
                dve.wait_ge(e_mm, n * NE + e + 1)
                if e == 2:
                    dve.wait_ge(e_rel, n * NE + 1)
                elif e > 2:
                    dve.wait_ge(e_acc, n * (NE - 1) + e - 2)
                else:
                    w(dve, e_acc, n * (NE - 1))
                v.scalar_tensor_tensor(out=tmp[:, e % 2, :], in0=banks[2 + e % 2], scalar=UN, in1=beb[:, e, :],
                                       op0=ALU.mult, op1=ALU.add).then_inc(e_bias, 1)

            def attn(n, ffn, nxt):
                dve.wait_ge(a_qhi, n + 1)
                v.tensor_tensor(qs[:, :, 1, :], banks[0].rearrange("p (h d) -> p h d", h=32), qs[:, :, 0, :],
                                ALU.subtract).then_inc(a_qlo, 1)
                dve.wait_ge(a_kvhi, n + 1)
                v.tensor_tensor(ks[:, :, 0, 2, :], banks[1][:, 0:P].rearrange("p (g d) -> p g d", g=NG),
                                ks[:, :, 0, 0, :], ALU.subtract)
                for b in range(2):
                    h = slice(64 * b, 64 * b + 64)
                    last = v.scalar_tensor_tensor(out=V1[0:64, b, 1, :], in0=banks[1][h, P:2 * P], scalar=UN,
                                                  in1=V1[h, b, 0, :], op0=ALU.mult, op1=ALU.subtract)
                last.then_inc(a_klo, 1)
                alone(dve, a_klo, n + 1)
                v.tensor_copy(ks[:, :, 1, 0:3, :], ks[:, :, 0, 0:3, :]).then_inc(a_kdup, 1)
                if ffn is not None:
                    mask_of(n - 1)

                def ex(*es):
                    if ffn is not None:
                        for e in es:
                            expert(n - 1, e)

                ex(0, 1)

                def wide(cols, k):
                    return cols.unsqueeze(2).to_broadcast([P, cols.shape[1], k])

                for b in range(2):
                    m = n * 2 + b + 1
                    dve.wait_ge(b_s, m)
                    for h in range(2):
                        last = v.tensor_reduce(smx[:, 8 * h:8 * h + 8], banks[h].rearrange("p (k m) -> p k m", m=64), AX.X, ALU.max)
                    last.then_inc(b_max, 1)
                    dve.wait_ge(b_max, m)
                    for h in range(2):
                        last = v.tensor_tensor(E1[:, 8 * h:8 * h + 8, :], banks[h].rearrange("p (k m) -> p k m", m=64),
                                               wide(smx[:, 8 * h:8 * h + 8], 64), ALU.subtract)
                    last.then_inc(b_sub, 1)
                    if b == 0:
                        ex(2)
                    dve.wait_ge(b_exp, m)
                    v.tensor_reduce(smx[:, 16:32], E1, AX.X, ALU.add).then_inc(b_sum, 1)
                    dve.wait_ge(b_sum, m)
                    if b == 1:
                        on(n, 0)
                    v.reciprocal(smx[:, 32:48], smx[:, 16:32]).then_inc(b_rec, 1)
                    dve.wait_ge(b_phi, m)
                    v.scalar_tensor_tensor(out=PP1[:, :, 1, :], in0=E1, scalar=PS, in1=PP1[:, :, 0, :],
                                           op0=ALU.mult, op1=ALU.subtract).then_inc(b_plo, 1)
                    if b == 0:
                        ex(3)
                if nxt is not None:
                    norm_stats(dve, nxt, 1, x_tile(n + 1), True)
                ex(4, 5)
                if nxt is not None:
                    norm_apply(dve, nxt, 1, x_tile(n + 1), yn)
                on(n, 1)
                ex(6)
                dve.wait_ge(a_y, n + 1)
                xt = x_tile(n)
                v.scalar_tensor_tensor(out=xt, in0=banks[0], scalar=UN2, in1=xt, op0=ALU.mult, op1=ALU.add).then_inc(a_add, 1)
                idx, par = (nxt + 1, 0) if nxt is not None else (63, 1)
                alone(dve, a_add, n + 1)
                norm_stats(dve, idx, par, xt, False)
                norm_apply(dve, idx, par, xt, yn)
                ex(7)

            def on(n, b):
                m = n * 2 + b + 1
                dve.wait_ge(b_o, m)
                dve.wait_ge(b_rec, m)
                v.tensor_tensor(on32.rearrange("p (k d) -> p k d", d=16), banks[6][:, 0:256].rearrange("p (k d) -> p k d", d=16),
                                smx[:, 32:48].unsqueeze(2).to_broadcast([P, 16, 16]), ALU.mult).then_inc(b_on, 1)
                dve.wait_ge(b_ohi, m)
                v.tensor_tensor(onh[:, b, 1, :], on32, onh[:, b, 0, :], ALU.subtract).then_inc(b_olo, 1)

            attn(0, None, 33)
            dve.wait_ge(be_in, 16)
            attn(1, 34, 35)
            with dve.Fori(0, 6) as i:
                for k in range(2, 4):
                    n = i * 2 + k
                    attn(n, n * 2 + 32, n * 2 + 33)
            attn(NT - 2, 2 * (NT - 2) + 32, 2 * (NT - 2) + 33)
            attn(NT - 1, 2 * (NT - 1) + 32, None)
            mask_of(NT - 1)
            for e in range(NE):
                expert(NT - 1, e)


def kernel(**inputs):
    import numpy as np
    import concourse.bacc as bacc
    from concourse.bass_utils import run_bass_kernel_spmd

    a = {k: np.asarray(v) for k, v in inputs.items()}

    def rows(m, k):
        return m.reshape(k, P, m.shape[1]).transpose(1, 0, 2).reshape(P, -1)

    ctx = a["ctx_4096"].reshape(NTOK, D)
    ctxT = np.stack([rows(ctx[c * CH:(c + 1) * CH].T, KC) for c in range(NC)])
    Wq, Wkv, Wo = a["L0_xattn_Wq"], a["L0_xattn_Wkv"], a["L0_xattn_Wo"]
    wB = np.stack([np.concatenate([
        rows(Wq[:, g * 512:(g + 1) * 512], KC),
        rows(np.concatenate([Wkv[:, g * P:(g + 1) * P], Wkv[:, 1024 + g * P:1024 + (g + 1) * P]], 1), KC),
        rows(Wo[g * 512:(g + 1) * 512], HG)], 1) for g in range(NG)])
    biasB = np.concatenate([a["L0_xattn_bq"].reshape(32, P).T, a["L0_xattn_bkv"].reshape(16, P).T], 1)
    wo1 = a["L1_xattn_wo"].T.reshape(NG, 2, 2, HD1, D)
    wo1 = wo1.transpose(0, 3, 2, 1, 4).reshape(P, 4 * D)
    arrays = {
        "x": a["x"].reshape(NTOK, D), "ctxT": ctxT, "wB": wB, "biasB": biasB,
        "bo": a["L0_xattn_bo"].reshape(1, D),
        "up": rows(a["L0_ffn_up_w"], KC), "down": rows(a["L0_ffn_down_w"], INT // P),
        "small0": np.concatenate([rows(a["L0_ffn_fc1_w"], KC), rows(a["L0_ffn_expert_w"], 2),
                                  rows(a["L0_ffn_gate_w"], KC)], 1),
        "fc2": rows(a["L0_ffn_fc2_w"], 2),
        "gam": a["L0_ffn_ln_gamma"].reshape(1, D), "bet": a["L0_ffn_ln_beta"].reshape(1, D),
        "wq1": rows(a["L1_xattn_wq"].T, KC),
        "wkv1": np.concatenate([rows(np.concatenate([a["L1_xattn_wk"], a["L1_xattn_wv"]], 0).T, KC),
                                rows(a["L1_ffn_W_gate"], KC)], 1),
        "wo1": wo1, "lnw": a["L1_xattn_ln_w"].reshape(KC, P).T,
        "we": np.stack([rows(a["L1_ffn_W_e"][e], KC) for e in range(NE)]),
        "be": a["L1_ffn_b_e"].reshape(1, NE * D), "bg": a["L1_ffn_b_gate"].reshape(1, NE),
    }
    arrays = {"in_" + k: np.ascontiguousarray(v) for k, v in arrays.items()}
    nc = bacc.Bacc("TRN2", target_bir_lowering=False, num_devices=1)
    args = [nc.dram_tensor(k, v.shape, mybir.dt.from_np(v.dtype), kind="ExternalInput").ap() for k, v in arrays.items()]
    args.append(nc.dram_tensor("out_0", (NTOK, D), F32, kind="ExternalOutput").ap())
    build(nc, *args)
    r = run_bass_kernel_spmd(nc, [arrays], core_ids=[0])
    return r.results[0]["out_0"].reshape(32, 64, D)
```

```python
from contextlib import ExitStack

import concourse.bass as bass
from concourse import mybir

F32 = mybir.dt.float32
F16 = mybir.dt.float16
U32 = mybir.dt.uint32
ACT = mybir.ActivationFunctionType
ALU = mybir.AluOpType
AX = mybir.AxisListType
ds = bass.ds

P = 128
D = 512
KC = D // P
NTOK = 32 * 64
NT = NTOK // P
NC = 4
CH = NTOK // NC
TC = CH // P
BC = CH // 64
NG = 8
HG = 4
HD1 = 16
INT = 1024
LAT = 256
NE = 8
EPS = 1e-5
WS = 64.0
UN = 1.0 / WS
UN2 = UN * UN
PS = 64.0
SC0 = UN2 * P ** -0.5
SC1 = UN2 * HD1 ** -0.5
UP, FC1, EX = "up", "fc1", "ex"
JOBS = ((UP, 0), (UP, 1), (FC1, 0), (FC1, 1), (UP, 2), (EX, 0), (UP, 3), (EX, 1)) + tuple((UP, m) for m in range(4, 8))
EXPERT_ORDER = (0, 1, 4, 5, 2, 3, 6, 7)
PASSES = ((0, 0), (0, 1), (1, 0))


def w(eng, sem, value):
    if not (isinstance(value, int) and value <= 0):
        eng.wait_ge(sem, value)


def build(nc, x, ctxT, wB, biasB, bo, up, down, small0, fc2, gam, bet, wq1, wkv1, wo1, lnw, we, be, bg, out):
    with ExitStack() as stack:
        def sb(name, cols, dt=F16):
            return stack.enter_context(nc.sbuf_tensor(name, [P, cols], dt))[:, :]

        def sem(name):
            return stack.enter_context(nc.semaphore(name))

        banks = [stack.enter_context(nc.psum_tensor(f"bank{i}", [P, 512], F32))[:, :] for i in range(8)]
        banks16 = [b.bitcast(F16) for b in banks]

        X = sb("X", NT * D, F32).rearrange("p (t d) -> p t d", t=NT)
        CT = sb("CT", NC * 2 * KC * CH).rearrange("p (c s k n) -> p c s k n", c=NC, s=2, k=KC)
        R1 = sb("R1", 16384)
        R2 = sb("R2", 21504)
        R3 = sb("R3", 4096, F32)
        AW = sb("AW", 10240)
        R4 = sb("R4", 13312)
        R5 = sb("R5", 1024, F32)
        yn = sb("yn", D, F32)
        ident = sb("ident", P)
        biases = sb("biases", 48, F32)
        lnwT = sb("lnwT", KC, F32)
        g0w = sb("g0w", 2 * KC * NE)
        g1w = sb("g1w", 2 * KC * NE)
        stat = sb("stat", 2 * 16, F32)
        ystat = sb("ystat", 16, F32)
        cstat = sb("cstat", TC * 14, F32)
        smx = sb("smx", 3 * 16, F32)
        m8 = sb("m8", TC * 8, F32)
        rsum = sb("rsum", TC, F32)
        lgt = sb("lgt", 8, F32)
        idx8 = sb("idx8", 8, U32)
        idxf = sb("idxf", 8, F32)
        msk = sb("msk", 3 * 8, F32)
        iota8 = sb("iota8", 8, F32)
        bgb = sb("bgb", 8, F32)

        def parts(region, off, k, n):
            return region[:, off:off + 2 * k * n].rearrange("p (s k n) -> p s k n", s=2, k=k)

        raw = R3.rearrange("p (s n) -> p s n", s=2)
        beb = R3.rearrange("p (e n) -> p e n", e=NE)
        xs = R4[:, 0:2048].rearrange("p (i s d) -> p i s d", i=2, s=2)
        XT = R1.rearrange("p (c s k n) -> p c s k n", c=NC, s=2, k=KC)
        GW = 10240
        WBq = [parts(R2, GW * i, KC, CH) for i in range(2)]
        WBkv = [parts(R2, GW * i + 4096, KC, 256) for i in range(2)]
        WBo = [parts(R2, GW * i + 6144, HG, D) for i in range(2)]
        qT = R4[:, 2048:6144].rearrange("p (s b h l) -> p s b h l", s=2, b=BC, h=HG)
        staged = {2: R2[:, GW:GW + 2048].bitcast(F32), 3: R2[:, GW + 2048:GW + 6144].bitcast(F32)}
        kT = R4[:, 6144:7168].rearrange("p (s n) -> p s n", s=2)
        V = R4[:, 7168:9216].rearrange("p (b s d) -> p b s d", b=BC, s=2)
        oT = R4[:, 9216:13312].rearrange("p (s h n) -> p s h n", s=2, h=HG)
        Eb = AW[:, 0:2048].bitcast(F32).rearrange("p (k m) -> p k m", m=64)
        PPb = AW[:, 2048:4096].rearrange("p (k s m) -> p k s m", s=2, m=64)
        PTb = AW[:, 4096:6144]
        xnB = AW[:, 6144:8192].bitcast(F32).rearrange("p (i n) -> p i n", i=2)
        Wup, Wfc1 = parts(R2, 0, KC, INT), parts(R2, 8192, KC, LAT)
        Wdn, Wex, Wfc2 = parts(R2, 10240, INT // P, D), parts(R2, 18432, LAT // P, LAT), parts(R2, 19456, LAT // P, D)
        Wg0, Wg1 = parts(g0w, 0, KC, NE), parts(g1w, 0, KC, NE)
        T1 = parts(R4, 2048, KC, CH)
        xlT, eoT = parts(R4, 6144, 2, CH), parts(R4, 8192, 2, CH)
        rel = R4[:, 10240:12288].bitcast(F32).rearrange("p (i n) -> p i n", i=2)
        h32 = R4[:, 12288:13312].bitcast(F32)
        hT = parts(R1, 8192, INT // P, CH)
        gamb, betb = R5[:, 0:D], R5[:, D:2 * D]
        bob = R5[:, 0:D]
        We = [parts(R1 if e < 4 else R2, 4096 * (e % 4), KC, D) for e in range(NE)]
        Wq1, Wkv1, Wo1 = parts(AW, 0, KC, D), parts(AW, 4096, KC, 256), parts(AW, 6144, 4, D)
        T2 = [parts(R4, 2048, KC, P), parts(R4, 3072, KC, P)]
        qs = R4[:, 4096:6144].rearrange("p (h s d) -> p h s d", h=32, s=4)
        PT1 = R4[:, 4096:6144]
        ks = R4[:, 6144:7168].rearrange("p (g j s d) -> p g j s d", g=NG, j=2, s=4)
        qT1 = R4[:, 7168:9216].rearrange("p (b t l) -> p b t l", b=2, t=16)
        kT1 = R4[:, 9216:10240].rearrange("p (g n) -> p g n", g=NG)
        V1 = R4[:, 10240:10752].rearrange("p (b s n) -> p b s n", b=2, s=2)
        E1 = R4[:, 10752:12800].bitcast(F32).rearrange("p (k m) -> p k m", m=64)
        on32 = R4[:, 12800:13312].bitcast(F32)
        PP1 = R2[:, 16384:18432].rearrange("p (k s m) -> p k s m", s=2, m=64)
        tmp = R2[:, 18432:20480].bitcast(F32).rearrange("p (i n) -> p i n", i=2)
        acc = R2[:, 20480:21504].bitcast(F32)
        onh = R5[:, 0:512].bitcast(F16).rearrange("p (b s n) -> p b s n", b=2, s=2)
        oT1 = R5[:, 512:1024].bitcast(F16).rearrange("p (s u n) -> p s u n", s=4, u=2)

        raw_in = [sem("raw_in0"), sem("raw_in1")]
        x_in = [sem(f"x_in{c}") for c in range(NC)]
        const_in, gb_in, be_in, out_done = sem("const_in"), sem("gb_in"), sem("be_in"), sem("out_done")
        w_scaled, w_hi, w_lo = sem("w_scaled"), sem("w_hi"), sem("w_lo")
        w0_hi, w0_half = sem("w0_hi"), sem("w0_half")
        ctx_hi, ctx_lo = sem("ctx_hi"), sem("ctx_lo")
        id_zero, id_ready, bias_ready, bo_added = sem("id_zero"), sem("id_ready"), sem("bias_ready"), sem("bo_added")
        n_bn, n_mv, n_arg, n_ln, n_r0, n_a, n_a2, n_b, n_r = (sem("n_" + s) for s in "bn mv arg ln r0 a a2 b r".split())
        n_xn, n_hi, n_lo, n_turned, n_stored = (sem("n_" + s) for s in "xn hi lo turned stored".split())
        p_mm, p_hi, p_lo = sem("p_mm"), sem("p_hi"), sem("p_lo")
        s_mm, s_max, s_sub, s_exp, s_sum, s_rec, s_prob, s_phi, s_plo = (
            sem("s_" + s) for s in "mm max sub exp sum rec prob phi plo".split())
        t_mm, t_ev = sem("t_mm"), sem("t_ev")
        o_mm, o_hi, o_lo = sem("o_mm"), sem("o_hi"), sem("o_lo")
        y_mm, y_add = sem("y_mm"), sem("y_add")
        u_mm, u_rel, u_sq, u_hi, u_lo = (sem("u_" + s) for s in "mm rel sq hi lo".split())
        g_mm, g_top, g_sum = sem("g_mm"), sem("g_top"), sem("g_sum")
        f_mm, f_rt, f_y, f_t, f_g, f_b, f_add = (sem("f_" + s) for s in "mm rt y t g b add".split())
        y_bn, y_mv, y_arg, y_ln, y_r0, y_a, y_a2, y_b, y_r = (sem("y_" + s) for s in "bn mv arg ln r0 a a2 b r".split())
        a_q, a_qhi, a_qlo, a_kv, a_kvhi, a_klo, a_kdup = (sem("a_" + s) for s in "q qhi qlo kv kvhi klo kdup".split())
        a_tq, a_tqev, a_tk, a_tkev = (sem("a_" + s) for s in "tq tqev tk tkev".split())
        b_s, b_max, b_sub, b_exp, b_sum, b_rec, b_phi, b_plo = (
            sem("b_" + s) for s in "s max sub exp sum rec phi plo".split())
        b_t, b_tev, b_o, b_on, b_ohi, b_olo = (sem("b_" + s) for s in "t tev o on ohi olo".split())
        a_to, a_toev, a_y, a_add = (sem("a_" + s) for s in "to toev y add".split())
        r_mm, r_lg, r_top, r_idx, r_f, r_m1, r_m2, r_mask = (sem("r_" + s) for s in "mm lg top idx f m1 m2 mask".split())
        e_mm, e_bias, e_rel, e_acc, x_done = (sem(s) for s in "e_mm e_bias e_rel e_acc x_done".split())
        z_ready = sem("z_ready")
        waits_passed = sem("waits_passed")

        def alone(eng, sem_, value):
            eng.wait_ge(sem_, value)
            eng.sem_inc(waits_passed, 1)

        block = stack.enter_context(nc.Block())

        def conv_of_group(g, j):
            return 4 + 3 * g + j

        @block.sync
        def _(sp):
            def x_chunk(c):
                sp.dma_start(X[:, c * TC:(c + 1) * TC, :],
                             x[c * CH:(c + 1) * CH, :].rearrange("(t p) d -> p t d", p=P)).then_inc(x_in[c], 16)

            x_chunk(0)

            def piece(k, src, conv_before):
                w(sp, w_lo, conv_before)
                n = src.shape[1]
                sp.dma_start(raw[:, kp(k), 0:n], src).then_inc(raw_in[kp(k)], 16)

            def kp(k):
                return k[1] if isinstance(k, tuple) else k % 2

            cuts = ((0, 2048), (2048, 3072), (3072, 5120))
            piece(0, wB[0, :, 0:2048], 0)
            piece(1, ctxT[0], 0)
            x_chunk(1)
            sp.dma_start(biases, biasB).then_inc(const_in, 16)
            sp.dma_start(lnwT, lnw).then_inc(const_in, 16)
            sp.dma_start(bob, bo.broadcast_to([P, D])).then_inc(const_in, 16)
            sp.dma_start(bgb, bg.broadcast_to([P, NE])).then_inc(const_in, 16)
            for k, (a, b) in ((2, cuts[1]), (3, cuts[2])):
                sp.wait_ge(raw_in[k % 2], 16)
                sp.dma_start(staged[k], wB[0, :, a:b]).then_inc(raw_in[k % 2], 16)
            for c in range(2, NC):
                x_chunk(c)
            for c in range(1, NC):
                piece(3 + c, ctxT[c], 2 + c)
            for j, (a, b) in enumerate(cuts):
                piece(7 + j, wB[1, :, a:b], 6 + j)
            with sp.Fori(0, 3) as i:
                for par in range(2):
                    for j, (a, b) in enumerate(cuts):
                        k = 3 * par + j
                        piece((None, k % 2), wB[ds(i * 2 + 2 + par, 1), :, a:b].rearrange("a p n -> (a p) n"),
                              i * 6 + 9 + k)
            sp.wait_ge(bo_added, NT)
            sp.dma_start(gamb, gam.broadcast_to([P, D])).then_inc(gb_in, 16)
            sp.dma_start(betb, bet.broadcast_to([P, D])).then_inc(gb_in, 16)
            piece(28, up[:, 0:2048], 27)
            piece(29, up[:, 2048:4096], 28)
            piece(30, small0, 29)
            piece(31, down[:, 0:2048], 30)
            piece(32, down[:, 2048:4096], 33)
            piece(33, fc2, 34)
            piece(34, wq1, 35)
            piece(35, wkv1, 36)
            piece(36, wo1, 37)
            for m, e in enumerate(EXPERT_ORDER):
                piece(37 + m, we[e], 39 + m)
            sp.wait_ge(w_lo, 48)
            sp.dma_start(R3, be.broadcast_to([P, NE * D])).then_inc(be_in, 16)
            with sp.Fori(0, NT) as n:
                sp.wait_ge(x_done, n + 1)
                sp.dma_start(out[ds(n * P, P), :], X[:, ds(n, 1), :].rearrange("p a d -> p (a d)")).then_inc(out_done, 16)
            sp.wait_ge(out_done, 16 * NT)

        @block.gpsimd
        def _(pool):
            g = nc.gpsimd
            g.memset(ident, 0.0).then_inc(id_zero, 1)
            pool.wait_ge(id_zero, 1)
            g.affine_select(out=ident, in_=ident, compare_op=ALU.not_equal, fill=1.0, base=0,
                            pattern=[[-1, P]], channel_multiplier=1).then_inc(id_ready, 1)
            g.iota(iota8, pattern=[[1, NE]], base=0, channel_multiplier=0,
                   allow_small_or_imprecise_dtypes=True).then_inc(id_ready, 1)

            def split(conv, src, hi, lo, scale=WS, row_scale=None):
                if row_scale is None:
                    g.tensor_scalar(src, src, scale, 1.0, ALU.mult, ALU.mult).then_inc(w_scaled, 1)
                else:
                    for k in range(KC):
                        last = g.tensor_scalar(src[:, k * D:(k + 1) * D], src[:, k * D:(k + 1) * D],
                                               row_scale[:, k:k + 1], scale, ALU.mult, ALU.mult)
                    last.then_inc(w_scaled, 1)
                alone(pool, w_scaled, conv + 1)
                g.tensor_scalar(hi, src, 1.0, 1.0, ALU.mult, ALU.mult).then_inc(w_hi, 1)
                pool.wait_ge(w_hi, conv + 1)
                g.tensor_tensor(lo, src, hi, ALU.subtract).then_inc(w_lo, 1)

            def halves(region, off, total, start=0, n=None):
                n = total if n is None else n
                return region[:, off + start:off + start + n], region[:, off + total + start:off + total + start + n]

            def ctx_piece(k, c):
                pool.wait_ge(raw_in[k % 2], 16 * (k // 2 + 1))
                chunk = CT[:, c].rearrange("p s k n -> p s (k n)")
                split(k, raw[:, k % 2, :], chunk[:, 0], chunk[:, 1], 1.0)

            def group_piece(k, slot, arrivals, par, j):
                alone(pool, raw_in[slot], arrivals * 16)
                off, n = ((0, 2048), (4096, 1024), (6144, 2048))[j]
                hi, lo = halves(R2, GW * par + off, n)
                split(k, raw[:, slot, 0:n], hi, lo)

            def add_bo(c):
                for t in range(c * TC, (c + 1) * TC):
                    pool.wait_ge(n_xn, t + 1)
                    g.tensor_tensor(X[:, t, :], X[:, t, :], bob, ALU.add).then_inc(bo_added, 1)

            pool.wait_ge(raw_in[0], 16)
            src = raw[:, 0, :]
            g.tensor_scalar(src, src, WS, 1.0, ALU.mult, ALU.mult).then_inc(w_scaled, 1)
            pool.wait_ge(w_scaled, 1)
            for h in range(2):
                cols = slice(h * 256, h * 256 + 256)
                src_h = src.rearrange("p (k n) -> p k n", k=KC)[:, :, cols]
                g.tensor_scalar(WBq[0][:, 0, :, cols], src_h, 1.0, 1.0, ALU.mult, ALU.mult).then_inc(w0_hi, 1)
                pool.wait_ge(w0_hi, h + 1)
                last = g.tensor_tensor(WBq[0][:, 1, :, cols], src_h, WBq[0][:, 0, :, cols], ALU.subtract)
                last.then_inc(w0_half if h == 0 else w_lo, 1)
            pool.wait_ge(const_in, 64)
            g.tensor_scalar(biases, biases, WS, 1.0, ALU.mult, ALU.mult).then_inc(bias_ready, 1)
            pool.sem_inc(w_hi, 1)

            def staged_piece(k, conv, j):
                off, n = ((0, 2048), (4096, 1024), (6144, 2048))[j]
                pool.wait_ge(raw_in[k % 2], 32)
                split(conv, staged[k], *halves(R2, off, n))

            staged_piece(2, 1, 1)
            pool.wait_ge(w_lo, 2)
            pool.wait_ge(bias_ready, 1)
            pool.wait_ge(id_ready, 2)
            g.memset(V[64:P, :, 1, :], 0.0).then_inc(z_ready, 1)
            pool.wait_ge(z_ready, 1)
            pool.wait_ge(ctx_lo, 1)
            for counted in (w_scaled, w_hi, w_lo):
                pool.sem_inc(counted, 1)
            staged_piece(3, 3, 2)
            ctx_piece(4, 1)
            add_bo(0)
            ctx_piece(5, 2)
            ctx_piece(6, 3)
            add_bo(1)
            for j in range(3):
                group_piece(7 + j, (7 + j) % 2, (7 + j) // 2 + 1, 1, j)
            add_bo(2)
            add_bo(3)
            with pool.Fori(0, 3) as i:
                for par in range(2):
                    pool.wait_ge(y_mm, i * 32 + 16 * (par + 1))
                    for j in range(3):
                        k = 3 * par + j
                        group_piece(i * 6 + 10 + k, k % 2, i * 3 + 5 + k // 2 + 1, par, j)

            def landed(k):
                pool.wait_ge(raw_in[k % 2], 16 * (k // 2 + 1))

            pool.wait_ge(y_mm, 7 * 16)
            for h in range(2):
                landed(28 + h)
                split(28 + h, raw[:, h, :], *halves(R2, 0, 4096, 2048 * h, 2048))
            landed(30)
            split(30, raw[:, 0, 0:1024], *halves(R2, 8192, 1024))
            pool.wait_ge(y_mm, 8 * 16)
            split(31, raw[:, 0, 1024:1536], *halves(R2, 18432, 512))
            split(32, raw[:, 0, 1536:1568], *halves(g0w, 0, 32))
            for h in range(2):
                landed(31 + h)
                split(33 + h, raw[:, (31 + h) % 2, :], *halves(R2, 10240, 4096, 2048 * h, 2048))
            landed(33)
            split(35, raw[:, 1, 0:1024], *halves(R2, 19456, 1024))
            landed(34)
            split(36, raw[:, 0, :], *halves(AW, 0, 2048), row_scale=lnwT)
            landed(35)
            split(37, raw[:, 1, 0:1024], *halves(AW, 4096, 1024))
            split(38, raw[:, 1, 1024:1056], *halves(g1w, 0, 32))
            landed(36)
            pool.wait_ge(n_lo, NT + TC)
            split(39, raw[:, 0, :], *halves(AW, 6144, 2048))
            for m, e in enumerate(EXPERT_ORDER):
                if m == 2:
                    pool.wait_ge(u_mm, 12 * NC)
                if m == 4:
                    pool.wait_ge(g_mm, NC)
                    g.memset(ks[:, :, :, 3, :], 0.0).then_inc(z_ready, 1)
                    g.memset(qs[:, :, 3, :], 0.0).then_inc(z_ready, 1)
                    pool.wait_ge(f_mm, 2 * NT)
                    pool.wait_ge(n_lo, 2 * NT + 1)
                    pool.wait_ge(z_ready, 3)
                    pool.wait_ge(w_lo, 44)
                    g.memset(V1[64:P, :, 1, :], 0.0).then_inc(z_ready, 1)
                    pool.wait_ge(z_ready, 4)
                landed(37 + m)
                split(40 + m, raw[:, (37 + m) % 2, :], *halves(R1 if e < 4 else R2, 4096 * (e % 4), 2048))

            def add_experts(n):
                for e in range(1, NE):
                    pool.wait_ge(e_rel, n * NE + e + 1)
                    if e > 1:
                        pool.wait_ge(e_acc, n * (NE - 1) + e - 1)
                    g.tensor_tensor(acc, acc, tmp[:, e % 2, :], ALU.add).then_inc(e_acc, 1)
                pool.wait_ge(e_acc, n * (NE - 1) + NE - 1)
                xt = X[:, ds(n, 1), :].rearrange("p a d -> p (a d)")
                g.tensor_tensor(xt, xt, acc, ALU.add).then_inc(x_done, 1)

            add_experts(0)
            with pool.Fori(1, NT) as n:
                add_experts(n)

        def newton(dve, s, k, n, sem_r0, sem_a, sem_a2, sem_b, sem_r):
            v_, r0, a_, b_, r_ = (s[:, m * k:(m + 1) * k] for m in (0, 2, 3, 4, 5))
            dve.wait_ge(sem_r0, n + 1)
            nc.vector.tensor_tensor(a_, v_, r0, ALU.mult).then_inc(sem_a, 1)
            dve.wait_ge(sem_a, n + 1)
            nc.vector.tensor_tensor(b_, a_, r0, ALU.mult).then_inc(sem_a2, 1)
            dve.wait_ge(sem_a2, n + 1)
            nc.vector.tensor_scalar(a_, b_, -0.5, 1.5, ALU.mult, ALU.add).then_inc(sem_b, 1)
            dve.wait_ge(sem_b, n + 1)
            nc.vector.tensor_tensor(r_, r0, a_, ALU.mult).then_inc(sem_r, 1)
            dve.wait_ge(sem_r, n + 1)

        def root(act, s, k, n, sem_arg, sem_ln, sem_r0):
            act.wait_ge(sem_arg, n + 1)
            nc.scalar.activation(s[:, k:2 * k], s[:, 0:k], ACT.Ln).then_inc(sem_ln, 1)
            act.wait_ge(sem_ln, n + 1)
            nc.scalar.activation(s[:, 2 * k:3 * k], s[:, k:2 * k], ACT.Exp, scale=-0.5).then_inc(sem_r0, 1)

        cbn = cstat[:, 0:24].rearrange("p (t k) -> p t k", t=TC)
        cmv = cstat[:, 24:32].rearrange("p (t k) -> p t k", t=TC)
        croot = cstat[:, 32:56]

        def chunk_stats(dve, c, tile):
            for t in range(TC):
                nc.vector.bn_stats(cbn[:, t, :], tile(t)).then_inc(n_bn, 1)
            chunk_var(dve, c)

        def chunk_var(dve, c):
            for t in range(TC):
                alone(dve, n_bn, c * TC + (t + 1))
                nc.vector.bn_aggr(cmv[:, t, :], cbn[:, t, :]).then_inc(n_mv, 1)
            dve.wait_ge(n_mv, c * TC + TC)
            nc.vector.tensor_scalar(croot[:, 0:TC], cmv[:, :, 1], EPS, None, ALU.add).then_inc(n_arg, 1)

        def chunk_root(act, c):
            root(act, croot, TC, c, n_arg, n_ln, n_r0)

        def chunk_newton(dve, c):
            newton(dve, croot, TC, c, n_r0, n_a, n_a2, n_b, n_r)

        def chunk_xn(dve, n, t, xt, buf):
            if t >= 2:
                dve.wait_ge(n_lo, n - 1)
            nc.vector.tensor_scalar(buf[:, t % 2, :], xt, cmv[:, t, 0:1], croot[:, 5 * TC + t:5 * TC + t + 1],
                                    ALU.subtract, ALU.mult).then_inc(n_xn, 1)

        def tile_lo(dve, n, par, src, turned=None):
            dve.wait_ge(n_hi, n + 1)
            w(dve, n_turned, n - 1 if turned is None else turned)
            nc.vector.tensor_tensor(xs[:, par, 1, :], src, xs[:, par, 0, :], ALU.subtract).then_inc(n_lo, 1)

        def tile_hi(act, n, par, src, turned=None):
            act.wait_ge(n_xn, n + 1)
            w(act, n_turned, n - 1 if turned is None else turned)
            nc.scalar.activation(xs[:, par, 0, :], src, ACT.Copy).then_inc(n_hi, 1)

        def tile_turn(pe, n, par, bank, stored):
            pe.wait_ge(n_lo, n + 1)
            w(pe, n_stored, stored)
            for sk in range(2 * KC):
                last = pe.transpose(banks16[bank][:, sk * P:(sk + 1) * P],
                                    xs[:, par, sk // KC, (sk % KC) * P:(sk % KC + 1) * P], ident)
            last.then_inc(n_turned, 1)

        def tile_store(act, n, bank, dst):
            act.wait_ge(n_turned, n + 1)
            nc.scalar.activation(dst, banks16[bank][:, 0:2 * KC * P].rearrange("p (a n) -> p a n", a=2 * KC),
                                 ACT.Copy).then_inc(n_stored, 1)

        def norm_stats(dve, n, par, xt, rms=False):
            s = stat[:, 16 * par:16 * par + 16]
            nc.vector.bn_stats(s[:, 0:6], xt).then_inc(n_bn, 1)
            alone(dve, n_bn, n + 1)
            nc.vector.bn_aggr(s[:, 6:8], s[:, 0:6]).then_inc(n_mv, 1)
            dve.wait_ge(n_mv, n + 1)
            nc.vector.tensor_scalar(s[:, 8:9], s[:, 7:8], 1.0 + EPS if rms else 1.0, EPS * EPS if rms else EPS,
                                    ALU.mult, ALU.add).then_inc(n_arg, 1)

        def norm_root(act, n, par):
            root(act, stat[:, 16 * par + 8:16 * par + 14], 1, n - 24, n_arg, n_ln, n_r0)

        def norm_apply(dve, n, par, xt, buf):
            s = stat[:, 16 * par:16 * par + 16]
            newton(dve, s[:, 8:14], 1, n - 24, n_r0, n_a, n_a2, n_b, n_r)
            nc.vector.tensor_scalar(buf, xt, s[:, 6:7], s[:, 13:14], ALU.subtract, ALU.mult).then_inc(n_xn, 1)

        def attn_stat(n):
            return n * 2 + 30 if not isinstance(n, int) or n > 1 else 32 + n

        def ffn_stat(n):
            return n * 2 + 35 if not isinstance(n, int) or n < NT - 2 else 48 + n

        def attn_turn(n):
            return n * 2 + 31 if not isinstance(n, int) or n > 0 else 32

        def ffn_turn(n):
            return n * 2 + 34 if not isinstance(n, int) or n < NT - 1 else 63

        def n_is_first(n):
            return isinstance(n, int) and n == 0

        def has(n, back):
            return not isinstance(n, int) or 0 <= n - back < NT

        def x_tile(n):
            return X[:, n, :] if isinstance(n, int) else X[:, ds(n, 1), :].rearrange("p a d -> p (a d)")

        @block.tensor
        def _(pe):
            pe.wait_ge(id_ready, 1)
            for t in range(TC):
                tile_turn(pe, t, t % 2, 2 + t % 2, t - 1)

            def group3(dst, pairs, incs, last_needs=None):
                m = len(pairs) * len(PASSES)
                k = 0
                for a, b in pairs:
                    if k == m - len(PASSES) and last_needs is not None:
                        pe.wait_ge(*last_needs)
                    for sa, sb_ in PASSES:
                        last = pe.matmul(dst, a(sa), b(sb_), start=(k == 0), stop=(k == m - 1))
                        k += 1
                if incs is not None:
                    last.then_inc(incs, 1)
                return last

            def b_proj(s, c, par, j):
                n = s * 6 + j
                w(pe, p_lo, n - 1)
                if isinstance(s, int) and s < NC and j == 4:
                    pe.wait_ge(w_lo, 3 if s == 0 else s + 4)
                if j < 5:
                    W_ = WBq[par] if j < 4 else WBkv[par]
                    src = XT if j < 4 else CT
                    cols = slice(j * P, (j + 1) * P) if j < 4 else slice(0, P)
                    group3(banks[j % 2], [(lambda p, k=k: W_[:, p, k, cols], lambda p, k=k: src[:, c, p, k, :])
                                          for k in range(KC)], p_mm)
                else:
                    for t in range(TC):
                        last = group3(banks[1][:, t * P:(t + 1) * P],
                                      [(lambda p, k=k: CT[:, c, p, k, t * P:(t + 1) * P],
                                        lambda p, k=k: WBkv[par][:, p, k, P:2 * P]) for k in range(KC)], None)
                    last.then_inc(p_mm, 1)

            def b_scores(s, hf):
                for blk in range(8):
                    b, hp = 4 * hf + blk // 2, blk % 2
                    last = group3(banks[2 + hf][:, blk * 64:(blk + 1) * 64],
                                  [(lambda p: qT[:, p, b, 2 * hp:2 * hp + 2, :].rearrange("p h l -> p (h l)"),
                                    lambda p: kT[:, p, b * 64:(b + 1) * 64])], None)
                last.then_inc(s_mm, 1)

            def b_turn(s, hf):
                pe.wait_ge(s_plo, s * 2 + hf + 1)
                for blk in range(8):
                    last = pe.transpose(banks16[4 + hf][:, blk * P:(blk + 1) * P],
                                        PPb[:, 8 * hf + blk].rearrange("p s m -> p (s m)"), ident)
                last.then_inc(t_mm, 1)

            def b_pv(s, jb):
                pe.wait_ge(t_ev, s * 2 + jb // 2 + 1)
                if jb == 0:
                    pe.wait_ge(p_lo, s * 6 + 6)
                if jb >= 2:
                    pe.wait_ge(o_lo, s * 4 + jb - 1)
                out_v = banks[6 + jb % 2].rearrange("p (h b l) -> p h b l", h=HG, b=2)
                for bb in range(2):
                    b = 2 * jb + bb
                    for p in range(2):
                        last = pe.matmul(out_v[:, :, bb, :], V[:, b, p, :],
                                         PTb[:, b * 256:(b + 1) * 256], start=(p == 0), stop=(p == 1))
                last.then_inc(o_mm, 1)

            def b_out(s, par, t):
                pe.wait_ge(o_lo, s * 4 + t + 1)
                if t >= 2:
                    pe.wait_ge(y_add, s * 4 + t - 1)
                group3(banks[4 + t % 2], [(lambda p, h=h: oT[:, p, h, t * P:(t + 1) * P],
                                           lambda p, h=h: WBo[par][:, p, h, :]) for h in range(HG)], y_mm)

            def bank_read(c, q):
                kind, m = JOBS[q]
                if kind == UP:
                    pe.wait_ge(u_rel, c * 8 + m + 1)
                else:
                    pe.wait_ge(u_lo, c * 12 + q + 1)

            def ffn_job(c, q):
                kind, m = JOBS[q]
                if q >= 2:
                    bank_read(c, q - 2)
                if isinstance(c, int) and c == 0 and kind != UP:
                    pe.wait_ge(w_lo, 31 if kind == FC1 else 33)
                wt, src, n = {UP: (Wup, T1, KC), FC1: (Wfc1, T1, KC), EX: (Wex, xlT, 2)}[kind]
                if q == 5:
                    for t in range(TC):
                        mm = group3(banks[5][:, t * NE:(t + 1) * NE],
                                    [(lambda p, k=k: T1[:, p, k, t * P:(t + 1) * P],
                                      lambda p, k=k: Wg0[:, p, k, :]) for k in range(KC)], None)
                    mm.then_inc(g_mm, 1)
                    pe.wait_ge(u_lo, c * 12 + 4)
                group3(banks[q % 2], [(lambda p, k=k: wt[:, p, k, m * P:(m + 1) * P], lambda p, k=k: src[:, p, k, :])
                                      for k in range(n)], u_mm)

            def b_step(s, c, par, last, norm=None, split=None):
                def turn(t):
                    if norm is not None:
                        tile_turn(pe, norm + t, t % 2, 2 + t % 2, norm + t - 1)

                pe.wait_ge(p_lo, s * 6 + 5)
                b_scores(s, 0)
                b_scores(s, 1)
                if last:
                    for t in range(TC):
                        b_out(s - 1, par, t)
                    pe.wait_ge(y_add, s * 4)
                    b_turn(s, 0)
                    b_turn(s, 1)
                    b_pv(s, 0)
                    b_pv(s, 1)
                    turn(0)
                    turn(1)
                    b_pv(s, 2)
                    b_pv(s, 3)
                    b_out(s, par, 0)
                    b_out(s, par, 1)
                    turn(2)
                    turn(3)
                    b_out(s, par, 2)
                    b_out(s, par, 3)
                    pe.wait_ge(n_stored, norm + TC)
                    return

                def proj(j):
                    b_proj(s + 1, (c + 1) % NC, par if c < NC - 1 else 1 - par, j)

                if split is not None:
                    pe.wait_ge(w_lo, split)
                for j in range(3):
                    proj(j)
                b_turn(s, 0)
                b_turn(s, 1)
                proj(3)
                b_pv(s, 0)
                b_pv(s, 1)
                proj(4)
                b_pv(s, 2)
                b_pv(s, 3)
                proj(5)
                for t in range(TC):
                    if not (isinstance(s, int) and s == NG * NC - 2):
                        b_out(s, par, t)
                    if t % 2 == 0:
                        turn(t)
                        turn(t + 1)
                if norm is not None:
                    pe.wait_ge(n_stored, norm + TC)

            pe.wait_ge(n_stored, TC)
            pe.wait_ge(w0_half, 1)
            for j in range(6):
                if j == 2:
                    pe.wait_ge(w_lo, 1)
                if j == 5:
                    pe.wait_ge(z_ready, 1)
                b_proj(0, 0, 0, j)
                if j in (2, 3):
                    for t in (0, 1) if j == 2 else (2, 3):
                        tile_turn(pe, TC + t, t % 2, 2 + t % 2, TC + t - 1)
            pe.wait_ge(n_stored, 2 * TC)
            for s in range(NC):
                b_step(s, s, 0, False, (s + 2) * TC if s < 2 else None, conv_of_group(1, 2) + 1 if s == NC - 1 else None)
            with pe.Fori(0, 3) as i:
                for k in range(8):
                    split = i * 6 + (conv_of_group(2 + k // NC, 2) + 1) if k % NC == NC - 1 else None
                    b_step(i * 8 + (NC + k), k % NC, 1 - k // NC, False, None, split)
            for s in range(28, 32):
                b_step(s, s % NC, 1, s == 31, NT if s == 31 else None)

            def ffn_chunk(c, last):
                for q in range(12):
                    ffn_job(c, q)
                for t in range(TC):
                    if t >= 2:
                        pe.wait_ge(f_y, c * TC + t - 1)
                    bd, bf = (6, 7) if t % 2 == 0 else (2, 3)
                    tt = slice(t * P, (t + 1) * P)
                    if t == 0 and isinstance(c, int):
                        pe.wait_ge(w_lo, 36)
                    if t == 0:
                        pe.wait_ge(u_lo, c * 12 + 11)
                    group3(banks[bd], [(lambda p, k=k: hT[:, p, k, tt], lambda p, k=k: Wdn[:, p, k, :])
                                       for k in range(INT // P)], f_mm, (u_lo, c * 12 + 12) if t == 0 else None)
                    group3(banks[bf], [(lambda p, k=k: eoT[:, p, k, tt], lambda p, k=k: Wfc2[:, p, k, :])
                                       for k in range(2)], f_mm)
                    n = c * TC + NT + TC
                    if last and t == 0:
                        tile_turn(pe, 32, 0, 4, 32)
                    elif not last and t < 2:
                        for u in (2 * t, 2 * t + 1):
                            tile_turn(pe, n + u, u % 2, 4 + u % 2, n + (u - 1))
                if not last:
                    pe.wait_ge(n_stored, n + TC)

            pe.wait_ge(w_lo, 30)
            ffn_chunk(0, False)
            with pe.Fori(1, NC - 1) as c:
                ffn_chunk(c, False)
            ffn_chunk(NC - 1, True)

            def project(n, ctx_t, tt):
                pe.wait_ge(n_stored, attn_turn(n) + 1)
                group3(banks[0], [(lambda p, k=k: tt[:, p, k, :], lambda p, k=k: Wq1[:, p, k, :]) for k in range(KC)], a_q)
                group3(banks[1][:, 0:256], [(lambda p, k=k: ctx_t(p, k), lambda p, k=k: Wkv1[:, p, k, :])
                                            for k in range(KC)], a_kv)

            def turn_q(n):
                pe.wait_ge(a_qlo, n + 1)
                for t in range(16):
                    bank, k = 4 + t // 8, t % 8
                    last = pe.transpose(banks16[bank][:, k * P:(k + 1) * P],
                                        qs[:, 2 * t:2 * t + 2].rearrange("p h s d -> p (h s d)"), ident)
                last.then_inc(a_tq, 1)

            def turn_k(n):
                pe.wait_ge(a_kdup, n + 1)
                for g in range(NG):
                    last = pe.transpose(banks16[6][:, g * P:(g + 1) * P], ks[:, g].rearrange("p j s d -> p (j s d)"), ident)
                last.then_inc(a_tk, 1)

            def scores(n, b):
                if b == 0:
                    w(pe, a_add, n)
                    pe.wait_ge(a_kvhi, n + 1)
                    pe.wait_ge(a_klo, n + 1)
                    pe.wait_ge(a_tqev, n + 1)
                    pe.wait_ge(a_tkev, n + 1)
                else:
                    pe.wait_ge(b_sub, n * 2 + 1)
                for blk in range(16):
                    j, g = blk % 2, blk // 2
                    rows = slice(64 * j, 64 * j + 48)
                    last = pe.matmul(banks[j][:, g * 64:(g + 1) * 64],
                                     qT1[rows, b, 2 * g:2 * g + 2, :].rearrange("p t l -> p (t l)"),
                                     kT1[rows, g, b * 64:(b + 1) * 64], start=True, stop=True)
                last.then_inc(b_s, 1)

            def turn_p(n, b):
                pe.wait_ge(b_plo, n * 2 + b + 1)
                if b == 1:
                    pe.wait_ge(b_tev, n * 2 + 1)
                for blk in range(16):
                    last = pe.transpose(banks16[4 + blk // 8][:, (blk % 8) * P:(blk % 8 + 1) * P],
                                        PP1[:, blk].rearrange("p s m -> p (s m)"), ident)
                last.then_inc(b_t, 1)

            def weigh_v(n, b):
                pe.wait_ge(b_tev, n * 2 + b + 1)
                if b == 1:
                    pe.wait_ge(b_on, n * 2 + 1)
                for blk in range(16):
                    g = blk % NG
                    for p in range(2):
                        last = pe.matmul(banks[6][:, blk * 16:(blk + 1) * 16], PT1[:, blk * P:(blk + 1) * P],
                                         V1[:, b, p, g * 16:(g + 1) * 16], start=(p == 0), stop=(p == 1))
                last.then_inc(b_o, 1)

            def turn_o(n):
                pe.wait_ge(b_olo, n * 2 + 2)
                for b in range(2):
                    for p in range(2):
                        for q in range(2):
                            k = b * 4 + p * 2 + q
                            last = pe.transpose(banks16[7][:, k * P:(k + 1) * P], onh[:, b, p, q * P:(q + 1) * P], ident)
                last.then_inc(a_to, 1)

            def output(n):
                pe.wait_ge(a_toev, n + 1)
                group3(banks[0], [(lambda p, qu=qu: oT1[:, 2 * p + qu // 2, qu % 2, :], lambda p, qu=qu: Wo1[:, p, qu, :])
                                  for qu in range(4)], a_y)

            def gate(n, tt):
                pe.wait_ge(n_stored, ffn_turn(n) + 1)
                group3(banks[7][:, 0:NE], [(lambda p, k=k: tt[:, p, k, :], lambda p, k=k: Wg1[:, p, k, :])
                                           for k in range(KC)], r_mm)

            def expert(n, e, tt):
                if isinstance(n, int) and n == 0:
                    pe.wait_ge(w_lo, 41 + EXPERT_ORDER.index(e))
                if not (isinstance(n, int) and n == 0 and e < 2):
                    pe.wait_ge(e_bias, n * NE + e - 1 if e > 0 else n * NE)
                group3(banks[2 + e % 2], [(lambda p, k=k: tt[:, p, k, :], lambda p, k=k: We[e][:, p, k, :])
                                          for k in range(KC)], e_mm)

            def attn_step(n, buf, ctx_t):
                one, two, more = has(n, 1), has(n, 2), has(n, -1)
                scores(n, 0)
                if two:
                    expert(n - 2, 6, T2[buf])
                scores(n, 1)
                if two:
                    expert(n - 2, 7, T2[buf])
                if one:
                    tile_turn(pe, ffn_stat(n - 1), 0, 7, ffn_turn(n - 1))
                turn_p(n, 0)
                if one:
                    gate(n - 1, T2[1 - buf])
                    expert(n - 1, 0, T2[1 - buf])
                if more and not n_is_first(n):
                    pe.wait_ge(r_lg, n)
                    tile_turn(pe, attn_stat(n + 1), 1, 7, attn_turn(n + 1))
                weigh_v(n, 0)
                if one:
                    expert(n - 1, 1, T2[1 - buf])
                turn_p(n, 1)
                if n_is_first(n):
                    weigh_v(n, 1)
                    tile_turn(pe, attn_stat(1), 1, 7, attn_turn(1))
                if more:
                    project(n + 1, ctx_t, T2[buf])
                else:
                    expert(n - 1, 2, T2[1 - buf])
                if not n_is_first(n):
                    weigh_v(n, 1)
                if one:
                    expert(n - 1, 2 if more else 3, T2[1 - buf])
                if not more:
                    pe.wait_ge(r_lg, n)
                turn_o(n)
                if more:
                    turn_q(n + 1)
                if one:
                    expert(n - 1, 3 if more else 4, T2[1 - buf])
                if more:
                    pe.wait_ge(b_on, n * 2 + 2)
                    turn_k(n + 1)
                output(n)
                if one and more:
                    expert(n - 1, 4, T2[1 - buf])
                if one:
                    expert(n - 1, 5, T2[1 - buf])

            def ctx_tile(n):
                return lambda p, k: CT[:, n // TC, p, k, (n % TC) * P:(n % TC + 1) * P]

            pe.wait_ge(w_lo, 40)
            project(0, ctx_tile(0), T2[1])
            pe.wait_ge(z_ready, 4)
            turn_q(0)
            turn_k(0)
            for n in range(2):
                attn_step(n, n % 2, ctx_tile(n + 1))
            pe.wait_ge(w_lo, 48)
            with pe.Fori(0, 3) as i:
                for k in range(2, 6):
                    ch, t = (k + 1) // TC, (k + 1) % TC
                    attn_step(i * 4 + k, k % 2, lambda p, kc, ch=ch, t=t: CT[:, ds(i + ch, 1), p, kc, t * P:(t + 1) * P]
                              .rearrange("p a n -> p (a n)"))
            for n in range(NT - 2, NT):
                attn_step(n, n % 2, ctx_tile(n + 1) if n < NT - 1 else None)
            n = NT - 1
            for e in (6, 7):
                expert(n - 1, e, T2[1 - n % 2])
            tile_turn(pe, ffn_stat(n), 0, 7, ffn_turn(n))
            gate(n, T2[n % 2])
            for e in range(NE):
                expert(n, e, T2[n % 2])

        @block.scalar
        def _(act):
            sc = nc.scalar
            act.preload_act_table_set("natural_log_exp_and_others")

            def x_turned(n, t):
                tile_store(act, n, 2 + t % 2, XT[:, n // TC, :, :, t * P:(t + 1) * P].rearrange("p s k n -> p (s k) n"))

            chunk_root(act, 0)
            for t in range(TC):
                tile_hi(act, t, t % 2, xnB[:, t % 2, :])
                if t > 0:
                    x_turned(t - 1, t - 1)
            x_turned(TC - 1, TC - 1)
            act.wait_ge(raw_in[1], 16)
            sc.activation(CT[:, 0, 0].rearrange("p k n -> p (k n)"), raw[:, 1, :], ACT.Copy).then_inc(ctx_hi, 1)

            def bias_col(g, a):
                return biases[:, ds(g + a, 1)] if not isinstance(g, int) else biases[:, g + a:g + a + 1]

            def proj_hi(s, g, j):
                alone(act, p_mm, s * 6 + j + 1)
                if j < 4:
                    sc.activation(qT[:, 0, :, j, :], banks[j % 2].rearrange("p (b l) -> p b l", l=64), ACT.Identity, bias=bias_col(g * HG, j)).then_inc(p_hi, 1)
                elif j == 4:
                    sc.activation(kT[:, 0, :], banks[0], ACT.Identity, bias=bias_col(g, 32)).then_inc(p_hi, 1)
                else:
                    v = banks[1].rearrange("p (t d) -> p t d", t=TC)
                    for odd in range(2):
                        for half in range(2):
                            last = sc.activation(V[64 * half:64 * half + 64, odd:BC:2, 0, :],
                                                 v[64 * odd:64 * odd + 64], ACT.Copy, scale=UN)
                    last.then_inc(p_hi, 1)

            def o_part(s, g, jb):
                alone(act, o_mm, s * 4 + jb + 1)
                sc.activation(oT[:, 0, :, jb * P:(jb + 1) * P], banks[6 + jb % 2].rearrange("p (h n) -> p h n", h=HG), ACT.Identity,
                              bias=bias_col(g, 40)).then_inc(o_hi, 1)

            def b_step(s, g, gn, last, norm=None):
                def proj(j):
                    if not last:
                        proj_hi(s + 1, gn, j)

                def hi(t):
                    if norm is not None:
                        tile_hi(act, norm + t, t % 2, xnB[:, t % 2, :])

                def turned_x(t):
                    if norm is not None and norm < NT:
                        x_turned(norm + t, t)
                    elif norm is not None:
                        tile_store(act, norm + t, 2 + t % 2, T1[:, :, :, t * P:(t + 1) * P].rearrange("p s k n -> p (s k) n"))

                def exp(hf):
                    act.wait_ge(s_sub, s * 2 + hf + 1)
                    e = Eb[:, 8 * hf:8 * hf + 8, :]
                    sc.activation(e, e, ACT.Exp, scale=SC0).then_inc(s_exp, 1)

                def phi(hf):
                    act.wait_ge(s_prob, s * 2 + hf + 1)
                    sc.activation(PPb[:, 8 * hf:8 * hf + 8, 0, :], Eb[:, 8 * hf:8 * hf + 8, :], ACT.Copy).then_inc(s_phi, 1)

                def turned(hf):
                    act.wait_ge(t_mm, s * 2 + hf + 1)
                    sc.activation(PTb[:, hf * 1024:(hf + 1) * 1024], banks16[4 + hf], ACT.Copy).then_inc(t_ev, 1)

                if last:
                    chunk_root(act, norm // TC)
                    exp(0)
                    exp(1)
                    phi(0)
                    phi(1)
                    turned(0)
                    turned(1)
                    hi(0)
                    hi(1)
                    o_part(s, g, 0)
                    o_part(s, g, 1)
                    turned_x(0)
                    turned_x(1)
                    o_part(s, g, 2)
                    o_part(s, g, 3)
                    hi(2)
                    hi(3)
                    turned_x(2)
                    turned_x(3)
                    return
                exp(0)
                exp(1)
                proj(0)
                phi(0)
                phi(1)
                proj(1)
                proj(2)
                turned(0)
                turned(1)
                if norm is not None:
                    chunk_root(act, norm // TC)
                proj(3)
                o_part(s, g, 0)
                o_part(s, g, 1)
                hi(0)
                proj(4)
                hi(1)
                o_part(s, g, 2)
                o_part(s, g, 3)
                proj(5)
                turned_x(0)
                hi(2)
                turned_x(1)
                hi(3)
                turned_x(2)
                turned_x(3)

            act.wait_ge(bias_ready, 1)
            proj_hi(0, 0, 0)
            chunk_root(act, 1)
            tile_hi(act, 4, 0, xnB[:, 0, :])
            tile_hi(act, 5, 1, xnB[:, 1, :])
            proj_hi(0, 0, 1)
            proj_hi(0, 0, 2)
            x_turned(4, 0)
            tile_hi(act, 6, 0, xnB[:, 0, :])
            x_turned(5, 1)
            tile_hi(act, 7, 1, xnB[:, 1, :])
            proj_hi(0, 0, 3)
            x_turned(6, 2)
            x_turned(7, 3)
            proj_hi(0, 0, 4)
            proj_hi(0, 0, 5)
            for s in range(NC):
                b_step(s, 0, (s + 1) // NC, False, (s + 2) * TC if s < 2 else None)
            with act.Fori(0, 3) as i:
                for k in range(8):
                    b_step(i * 8 + (NC + k), i * 2 + (1 + k // NC), i * 2 + (1 + (k + 1) // NC), False)
            for s in range(28, 32):
                b_step(s, s // NC, (s + 1) // NC, s == 31, NT if s == 31 else None)

            act.wait_ge(y_mm, NG * NC * TC)
            def y_root(n):
                root(act, ystat[:, 8:14], 1, n, y_arg, y_ln, y_r0)

            def ffn_chunk(c, last):
                for q, (kind, m) in enumerate(JOBS):
                    act.wait_ge(u_mm, c * 12 + q + 1)
                    if kind == UP:
                        sc.activation(rel[:, m % 2, :], banks[q % 2], ACT.Relu, scale=UN).then_inc(u_rel, 1)
                        act.wait_ge(u_sq, c * 8 + m + 1)
                        sc.activation(hT[:, 0, m, :], h32, ACT.Copy).then_inc(u_hi, 1)
                    else:
                        dst = (xlT if kind == FC1 else eoT)[:, 0, m, :]
                        sc.activation(dst, banks[q % 2], ACT.Copy, scale=UN).then_inc(u_hi, 1)
                    if q == 0:
                        if not (isinstance(c, int) and c == 0):
                            y_root(c * TC - 1)
                    if q == 10:
                        if last:
                            norm_root(act, 32, 0)
                        else:
                            chunk_root(act, c + 5)
                n = c * TC + NT + TC

                def store(t):
                    tile_store(act, n + t, 4 + t % 2, T1[:, :, :, t * P:(t + 1) * P].rearrange("p s k n -> p (s k) n"))

                if last:
                    tile_hi(act, 32, 0, rel[:, 0, :])
                    tile_store(act, 32, 4, T2[1].rearrange("p s k n -> p (s k) n"))
                else:
                    tile_hi(act, n, 0, rel[:, 0, :])
                    tile_hi(act, n + 1, 1, rel[:, 1, :])
                for t in range(TC):
                    if t == 0 and not last:
                        store(0)
                        tile_hi(act, n + 2, 0, rel[:, 0, :])
                    if t < TC - 1:
                        y_root(c * TC + t)
                    if t == 0 and not last:
                        store(1)
                        tile_hi(act, n + 3, 1, rel[:, 1, :])
                    if t == 1 and not last:
                        store(2)
                        store(3)

            ffn_chunk(0, False)
            with act.Fori(1, NC - 1) as c:
                ffn_chunk(c, False)
            ffn_chunk(NC - 1, True)

            def norm_store(n, buf):
                tile_store(act, n, 7, T2[buf].rearrange("p s k n -> p (s k) n"))

            def expert(n, e):
                act.wait_ge(e_bias, n * NE + e + 1)
                if e == 0:
                    act.wait_ge(r_mask, n + 1)
                    w(act, x_done, n)
                dst = acc if e == 0 else tmp[:, e % 2, :]
                sc.activation(dst, tmp[:, e % 2, :], ACT.Relu, scale=msk[:, 16 + e:17 + e]).then_inc(e_rel, 1)

            def project_hi(n):
                act.wait_ge(a_q, n + 1)
                q = banks[0].rearrange("p (h d) -> p h d", h=32)
                sc.activation(qs[:, :, 0, :], q, ACT.Copy)
                sc.activation(qs[:, :, 2, :], q, ACT.Copy).then_inc(a_qhi, 1)
                act.wait_ge(a_kv, n + 1)
                k = banks[1][:, 0:P].rearrange("p (g d) -> p g d", g=NG)
                sc.activation(ks[:, :, 0, 0, :], k, ACT.Copy)
                sc.activation(ks[:, :, 0, 1, :], k, ACT.Copy)
                for b in range(2):
                    for half in range(2):
                        last = sc.activation(V1[64 * half:64 * half + 64, b, 0, :],
                                             banks[1][64 * b:64 * b + 64, P:2 * P], ACT.Copy, scale=UN)
                last.then_inc(a_kvhi, 1)

            def turned_q(n):
                act.wait_ge(a_tq, n + 1)
                for h in range(2):
                    last = sc.activation(qT1[:, :, 8 * h:8 * h + 8, :].rearrange("p b t l -> p t b l"),
                                         banks16[4 + h].rearrange("p (t b l) -> p t b l", t=8, b=2), ACT.Copy)
                last.then_inc(a_tqev, 1)

            def turned_k(n):
                act.wait_ge(a_tk, n + 1)
                sc.activation(kT1, banks16[6].rearrange("p (t n) -> p t n", t=8), ACT.Copy).then_inc(a_tkev, 1)

            def exponentials(n, b):
                m = n * 2 + b + 1
                act.wait_ge(b_sub, m)
                sc.activation(E1, E1, ACT.Exp, scale=SC1).then_inc(b_exp, 1)
                act.wait_ge(b_exp, m)
                sc.activation(PP1[:, :, 0, :], E1, ACT.Copy, scale=PS).then_inc(b_phi, 1)

            def turned_p(n, b):
                act.wait_ge(b_t, n * 2 + b + 1)
                if b == 1:
                    act.wait_ge(b_o, n * 2 + 1)
                for h in range(2):
                    last = sc.activation(PT1[:, h * 1024:(h + 1) * 1024], banks16[4 + h], ACT.Copy)
                last.then_inc(b_tev, 1)

            def out_hi(n, b):
                act.wait_ge(b_on, n * 2 + b + 1)
                sc.activation(onh[:, b, 0, :], on32, ACT.Copy).then_inc(b_ohi, 1)

            def attn_step(n, buf):
                one, two, more = has(n, 1), has(n, 2), has(n, -1)
                exponentials(n, 0)
                if n_is_first(n):
                    y_root(NT - 1)
                if two:
                    expert(n - 2, 5)
                    expert(n - 2, 6)
                if one:
                    norm_store(ffn_turn(n - 1), 1 - buf)
                if two:
                    expert(n - 2, 7)
                turned_p(n, 0)
                exponentials(n, 1)
                if more and not n_is_first(n):
                    norm_store(attn_turn(n + 1), buf)
                out_hi(n, 0)
                if one:
                    expert(n - 1, 0)
                    expert(n - 1, 1)
                turned_p(n, 1)
                if n_is_first(n):
                    norm_root(act, attn_stat(1), 1)
                    tile_hi(act, attn_stat(1), 1, yn)
                    norm_store(attn_turn(1), buf)
                if has(n, -2):
                    norm_root(act, attn_stat(n + 2), 1)
                out_hi(n, 1)
                if more:
                    act.wait_ge(b_o, n * 2 + 2)
                    project_hi(n + 1)
                if one:
                    expert(n - 1, 2)
                act.wait_ge(a_to, n + 1)
                for b in range(2):
                    last = sc.activation(oT1[:, :, :, b * 64:(b + 1) * 64],
                                         banks16[7][:, b * 512:(b + 1) * 512].rearrange("p (s u l) -> p s u l", s=4, u=2),
                                         ACT.Copy)
                last.then_inc(a_toev, 1)
                if has(n, -2):
                    tile_hi(act, attn_stat(n + 2), 1, yn, attn_turn(n + 1) + 1)
                if more:
                    turned_q(n + 1)
                if one:
                    expert(n - 1, 3)
                if more:
                    turned_k(n + 1)
                norm_root(act, ffn_stat(n), 0)
                if one:
                    expert(n - 1, 4)
                tile_hi(act, ffn_stat(n), 0, yn, ffn_turn(n - 1) + 1 if one else 33)

            project_hi(0)
            turned_q(0)
            turned_k(0)
            for n in range(2):
                attn_step(n, n % 2)
            with act.Fori(0, 6) as i:
                for k in range(2, 4):
                    attn_step(i * 2 + k, k % 2)
            for n in range(NT - 2, NT):
                attn_step(n, n % 2)
            n = NT - 1
            for e in (5, 6, 7):
                expert(n - 1, e)
            norm_store(ffn_turn(n), n % 2)
            for e in range(NE):
                expert(n, e)

        @block.vector
        def _(dve):
            v = nc.vector

            def xn_of(n, t, tile):
                chunk_xn(dve, n, t, tile, xnB)

            def lo_of(n, t):
                tile_lo(dve, n, t % 2, xnB[:, t % 2, :])

            dve.wait_ge(x_in[0], 16)
            chunk_stats(dve, 0, x_tile)
            chunk_newton(dve, 0)
            for t in range(TC):
                xn_of(t, t, x_tile(t))
                if t > 0:
                    lo_of(t - 1, t - 1)
            lo_of(TC - 1, TC - 1)
            dve.wait_ge(ctx_hi, 1)
            v.tensor_tensor(CT[:, 0, 1].rearrange("p k n -> p (k n)"), raw[:, 1, :],
                            CT[:, 0, 0].rearrange("p k n -> p (k n)"), ALU.subtract).then_inc(ctx_lo, 1)

            def bias_col(g, a):
                return biases[:, ds(g + a, 1)] if not isinstance(g, int) else biases[:, g + a:g + a + 1]

            def lo(dst, src, bias, hi, done):
                v.scalar_tensor_tensor(out=dst, in0=src, scalar=bias, in1=hi, op0=ALU.add, op1=ALU.subtract).then_inc(done, 1)

            def proj_lo(s, g, j):
                dve.wait_ge(p_hi, s * 6 + j + 1)
                if j < 4:
                    lo(qT[:, 1, :, j, :], banks[j % 2].rearrange("p (b l) -> p b l", l=64), bias_col(g * HG, j), qT[:, 0, :, j, :], p_lo)
                elif j == 4:
                    lo(kT[:, 1, :], banks[0], bias_col(g, 32), kT[:, 0, :], p_lo)
                else:
                    vv = banks[1].rearrange("p (t d) -> p t d", t=TC)
                    for odd in range(2):
                        h = slice(64 * odd, 64 * odd + 64)
                        last = v.scalar_tensor_tensor(out=V[0:64, odd:BC:2, 1, :], in0=vv[h], scalar=UN,
                                                      in1=V[h, odd:BC:2, 0, :], op0=ALU.mult, op1=ALU.subtract)
                    last.then_inc(p_lo, 1)

            def b_step(s, c, g, gn, last, norm=None):
                first = None if norm is None else norm % NT

                def stats():
                    if isinstance(s, int) and s == NG * NC - 2:
                        chunk_stats(dve, NC, x_tile)
                    elif norm is not None:
                        if norm < NT:
                            dve.wait_ge(x_in[norm // TC], 16)
                        chunk_stats(dve, norm // TC, lambda t: x_tile(first + t))

                def xnorm(t):
                    if norm is not None:
                        xn_of(norm + t, t, x_tile(first + t))

                def xlo(t):
                    if norm is not None:
                        lo_of(norm + t, t)

                def proj(j):
                    if not last:
                        proj_lo(s + 1, gn, j)

                def blocks(hf):
                    return slice(8 * hf, 8 * hf + 8)

                def wide(cols):
                    return cols.unsqueeze(2).to_broadcast([P, 8, 64])

                def shift(hf):
                    n = s * 2 + hf + 1
                    S = banks[2 + hf].rearrange("p (k m) -> p k m", m=64)
                    dve.wait_ge(s_mm, n)
                    v.tensor_reduce(smx[:, blocks(hf)], S, AX.X, ALU.max).then_inc(s_max, 1)
                    dve.wait_ge(s_max, n)
                    v.tensor_tensor(Eb[:, blocks(hf), :], S, wide(smx[:, blocks(hf)]), ALU.subtract).then_inc(s_sub, 1)

                def prob(hf):
                    n = s * 2 + hf + 1
                    sums, recs = smx[:, 16 + 8 * hf:24 + 8 * hf], smx[:, 32 + 8 * hf:40 + 8 * hf]
                    dve.wait_ge(s_exp, n)
                    v.tensor_reduce(sums, Eb[:, blocks(hf), :], AX.X, ALU.add).then_inc(s_sum, 1)
                    dve.wait_ge(s_sum, n)
                    v.reciprocal(recs, sums).then_inc(s_rec, 1)
                    dve.wait_ge(s_rec, n)
                    v.scalar_tensor_tensor(out=Eb[:, blocks(hf), :], in0=Eb[:, blocks(hf), :], scalar=PS,
                                           in1=wide(recs), op0=ALU.mult, op1=ALU.mult).then_inc(s_prob, 1)

                def plo(hf):
                    dve.wait_ge(s_phi, s * 2 + hf + 1)
                    v.tensor_tensor(PPb[:, blocks(hf), 1, :], Eb[:, blocks(hf), :], PPb[:, blocks(hf), 0, :],
                                    ALU.subtract).then_inc(s_plo, 1)

                def olo(jb):
                    dve.wait_ge(o_hi, s * 4 + jb + 1)
                    cols = slice(jb * P, (jb + 1) * P)
                    lo(oT[:, 1, :, cols], banks[6 + jb % 2].rearrange("p (h n) -> p h n", h=HG), bias_col(g, 40),
                       oT[:, 0, :, cols], o_lo)

                def add(s, c, t):
                    dve.wait_ge(y_mm, s * 4 + t + 1)
                    if isinstance(s, int) and s < NC:
                        dve.wait_ge(bo_added, s * TC + t + 1)
                    xt = x_tile(c * TC + t)
                    v.scalar_tensor_tensor(out=xt, in0=banks[4 + t % 2], scalar=UN2, in1=xt,
                                           op0=ALU.mult, op1=ALU.add).then_inc(y_add, 1)

                if last:
                    shift(0)
                    add(s - 1, c - 1, 0)
                    shift(1)
                    prob(0)
                    add(s - 1, c - 1, 1)
                    prob(1)
                    plo(0)
                    plo(1)
                    add(s - 1, c - 1, 2)
                    add(s - 1, c - 1, 3)
                    chunk_newton(dve, norm // TC)
                    xnorm(0)
                    xnorm(1)
                    xlo(0)
                    xlo(1)
                    olo(0)
                    olo(1)
                    xnorm(2)
                    xnorm(3)
                    olo(2)
                    olo(3)
                    add(s, c, 0)
                    xlo(2)
                    xlo(3)
                    for t in range(1, TC):
                        add(s, c, t)
                    return
                    for t in range(TC):
                        add(s, c, t)
                    return
                shift(0)
                shift(1)
                prob(0)
                proj(0)
                prob(1)
                plo(0)
                plo(1)
                proj(1)
                stats()
                proj(2)
                proj(3)
                if norm is not None:
                    chunk_newton(dve, norm // TC)
                xnorm(0)
                xnorm(1)
                olo(0)
                olo(1)
                proj(4)
                xlo(0)
                xlo(1)
                olo(2)
                olo(3)
                proj(5)
                xnorm(2)
                for t in range(TC):
                    if not (isinstance(s, int) and s == NG * NC - 2):
                        add(s, c, t)
                    if t == 0:
                        xlo(2)
                    if t == 1:
                        xnorm(3)
                        xlo(3)

            dve.wait_ge(bias_ready, 1)
            proj_lo(0, 0, 0)
            dve.wait_ge(x_in[1], 16)
            chunk_stats(dve, 1, lambda t: x_tile(TC + t))
            chunk_newton(dve, 1)
            xn_of(4, 0, x_tile(4))
            xn_of(5, 1, x_tile(5))
            proj_lo(0, 0, 1)
            lo_of(4, 0)
            lo_of(5, 1)
            proj_lo(0, 0, 2)
            xn_of(6, 2, x_tile(6))
            lo_of(6, 2)
            xn_of(7, 3, x_tile(7))
            lo_of(7, 3)
            for j in range(3, 6):
                proj_lo(0, 0, j)
            for s in range(NC):
                b_step(s, s, 0, (s + 1) // NC, False, (s + 2) * TC if s < 2 else None)
            with dve.Fori(0, 3) as i:
                for k in range(8):
                    b_step(i * 8 + (NC + k), k % NC, i * 2 + (1 + k // NC), i * 2 + (1 + (k + 1) // NC), False)
            for s in range(28, 32):
                b_step(s, s % NC, s // NC, (s + 1) // NC, s == 31, NT if s == 31 else None)

            dve.wait_ge(y_add, 128)
            dve.wait_ge(gb_in, 32)

            def y_stats(n):
                dve.wait_ge(f_y, n + 1)
                v.bn_stats(ystat[:, 0:6], yn).then_inc(y_bn, 1)
                alone(dve, y_bn, n + 1)
                v.bn_aggr(ystat[:, 6:8], ystat[:, 0:6]).then_inc(y_mv, 1)
                dve.wait_ge(y_mv, n + 1)
                v.tensor_scalar(ystat[:, 8:9], ystat[:, 7:8], EPS, None, ALU.add).then_inc(y_arg, 1)

            def y_norm(n):
                newton(dve, ystat[:, 8:14], 1, n, y_r0, y_a, y_a2, y_b, y_r)
                v.tensor_scalar(yn, yn, ystat[:, 6:7], ystat[:, 13:14], ALU.subtract, ALU.mult).then_inc(f_t, 1)
                dve.wait_ge(f_t, n + 1)
                v.tensor_tensor(yn, yn, gamb, ALU.mult).then_inc(f_g, 1)

            def y_add_to_x(n):
                dve.wait_ge(f_g, n + 1)
                v.tensor_tensor(yn, yn, betb, ALU.add).then_inc(f_b, 1)
                dve.wait_ge(f_b, n + 1)
                v.tensor_tensor(x_tile(n), x_tile(n), yn, ALU.add).then_inc(f_add, 1)

            def ffn_chunk(c, last):
                first = isinstance(c, int) and c == 0
                for q, (kind, m) in enumerate(JOBS):
                    if q in (1, 4, 5) and not first:
                        {1: y_stats, 4: y_norm, 5: y_add_to_x}[q](c * TC - 1)
                    if 7 <= q < 11 and not last:
                        v.bn_stats(cbn[:, q - 7, :], x_tile(c * TC + TC + (q - 7))).then_inc(n_bn, 1)
                    if q == 11:
                        if last:
                            norm_stats(dve, 32, 0, x_tile(0), True)
                        else:
                            chunk_var(dve, c + 5)
                    if q == 9:
                        alone(dve, g_mm, c + 1)
                        for t in range(TC):
                            mm = v.max(m8[:, t * NE:(t + 1) * NE], banks[5][:, t * NE:(t + 1) * NE])
                        mm.then_inc(g_top, 1)
                        dve.wait_ge(g_top, c + 1)
                        for t in range(TC):
                            mm = v.tensor_scalar(rsum[:, t:t + 1], m8[:, t * NE:t * NE + 1],
                                                 m8[:, t * NE + 1:t * NE + 2], UN2, ALU.add, ALU.mult)
                        mm.then_inc(g_sum, 1)
                    if q == 0:
                        w(dve, f_y, c * TC)
                    if kind == UP:
                        dve.wait_ge(u_rel, c * 8 + m + 1)
                        w(dve, u_lo, c * 12 + q)
                        v.tensor_tensor(h32, rel[:, m % 2, :], rel[:, m % 2, :], ALU.mult).then_inc(u_sq, 1)
                        dve.wait_ge(u_hi, c * 12 + q + 1)
                        v.tensor_tensor(hT[:, 1, m, :], h32, hT[:, 0, m, :], ALU.subtract).then_inc(u_lo, 1)
                    else:
                        dst = xlT if kind == FC1 else eoT
                        dve.wait_ge(u_hi, c * 12 + q + 1)
                        v.scalar_tensor_tensor(out=dst[:, 1, m, :], in0=banks[q % 2], scalar=UN,
                                               in1=dst[:, 0, m, :], op0=ALU.mult, op1=ALU.subtract).then_inc(u_lo, 1)
                m = c * TC + NT + TC

                def xnorm(t):
                    chunk_xn(dve, m + t, t, x_tile(c * TC + TC + t), rel)

                def xlo(t):
                    tile_lo(dve, m + t, t % 2, rel[:, t % 2, :])

                if last:
                    norm_apply(dve, 32, 0, x_tile(0), rel[:, 0, :])
                    tile_lo(dve, 32, 0, rel[:, 0, :])
                else:
                    chunk_newton(dve, c + 5)
                    xnorm(0)
                    xnorm(1)
                    xlo(0)
                    xlo(1)
                    xnorm(2)
                dve.wait_ge(g_sum, c + 1)
                for t in range(TC):
                    n = c * TC + t
                    bd, bf = (6, 7) if t % 2 == 0 else (2, 3)
                    dve.wait_ge(f_mm, n * 2 + 2)
                    v.tensor_scalar(h32, banks[bf], rsum[:, t:t + 1], None, ALU.mult).then_inc(f_rt, 1)
                    dve.wait_ge(f_rt, n + 1)
                    v.scalar_tensor_tensor(out=yn, in0=banks[bd], scalar=UN, in1=h32, op0=ALU.mult, op1=ALU.add).then_inc(f_y, 1)
                    if t == TC - 1:
                        break
                    y_stats(n)
                    if t == 0 and not last:
                        xlo(2)
                        xnorm(3)
                        xlo(3)
                    y_norm(n)
                    y_add_to_x(n)

            ffn_chunk(0, False)
            with dve.Fori(1, NC - 1) as c:
                ffn_chunk(c, False)
            ffn_chunk(NC - 1, True)

            def mask_of(n):
                dve.wait_ge(r_mm, n + 1)
                v.scalar_tensor_tensor(out=lgt, in0=banks[7][:, 0:NE], scalar=UN, in1=bgb,
                                       op0=ALU.mult, op1=ALU.add).then_inc(r_lg, 1)
                alone(dve, r_lg, n + 1)
                v.max(m8[:, 0:8], lgt).then_inc(r_top, 1)
                alone(dve, r_top, n + 1)
                v.max_index(idx8, m8[:, 0:8], lgt).then_inc(r_idx, 1)
                dve.wait_ge(r_idx, n + 1)
                v.tensor_copy(idxf, idx8).then_inc(r_f, 1)
                dve.wait_ge(r_f, n + 1)
                v.tensor_scalar(msk[:, 0:8], iota8, idxf[:, 0:1], 0.5, ALU.is_equal, ALU.mult).then_inc(r_m1, 1)
                v.tensor_scalar(msk[:, 8:16], iota8, idxf[:, 1:2], 0.5, ALU.is_equal, ALU.mult).then_inc(r_m2, 1)
                dve.wait_ge(r_m1, n + 1)
                dve.wait_ge(r_m2, n + 1)
                w(dve, e_rel, n * NE)
                v.tensor_tensor(msk[:, 16:24], msk[:, 0:8], msk[:, 8:16], ALU.add).then_inc(r_mask, 1)

            def expert(n, e):
                dve.wait_ge(e_mm, n * NE + e + 1)
                if e == 2:
                    dve.wait_ge(e_rel, n * NE + 1)
                elif e > 2:
                    dve.wait_ge(e_acc, n * (NE - 1) + e - 2)
                else:
                    w(dve, e_acc, n * (NE - 1))
                v.scalar_tensor_tensor(out=tmp[:, e % 2, :], in0=banks[2 + e % 2], scalar=UN, in1=beb[:, e, :],
                                       op0=ALU.mult, op1=ALU.add).then_inc(e_bias, 1)

            def q_lo(n):
                dve.wait_ge(a_qhi, n + 1)
                v.tensor_tensor(qs[:, :, 1, :], banks[0].rearrange("p (h d) -> p h d", h=32), qs[:, :, 0, :],
                                ALU.subtract).then_inc(a_qlo, 1)

            def kv_lo(n):
                dve.wait_ge(a_kvhi, n + 1)
                v.tensor_tensor(ks[:, :, 0, 2, :], banks[1][:, 0:P].rearrange("p (g d) -> p g d", g=NG),
                                ks[:, :, 0, 0, :], ALU.subtract)
                for b in range(2):
                    h = slice(64 * b, 64 * b + 64)
                    last = v.scalar_tensor_tensor(out=V1[0:64, b, 1, :], in0=banks[1][h, P:2 * P], scalar=UN,
                                                  in1=V1[h, b, 0, :], op0=ALU.mult, op1=ALU.subtract)
                last.then_inc(a_klo, 1)
                alone(dve, a_klo, n + 1)
                v.tensor_copy(ks[:, :, 1, 0:3, :], ks[:, :, 0, 0:3, :]).then_inc(a_kdup, 1)

            def wide(cols, k):
                return cols.unsqueeze(2).to_broadcast([P, cols.shape[1], k])

            def less_max(n, b):
                dve.wait_ge(b_s, n * 2 + b + 1)
                for h in range(2):
                    last = v.tensor_reduce(smx[:, 8 * h:8 * h + 8], banks[h].rearrange("p (k m) -> p k m", m=64), AX.X, ALU.max)
                last.then_inc(b_max, 1)
                dve.wait_ge(b_max, n * 2 + b + 1)
                for h in range(2):
                    last = v.tensor_tensor(E1[:, 8 * h:8 * h + 8, :], banks[h].rearrange("p (k m) -> p k m", m=64),
                                           wide(smx[:, 8 * h:8 * h + 8], 64), ALU.subtract)
                last.then_inc(b_sub, 1)

            def row_sums(n, b):
                dve.wait_ge(b_exp, n * 2 + b + 1)
                v.tensor_reduce(smx[:, 16:32], E1, AX.X, ALU.add).then_inc(b_sum, 1)

            def reciprocals(n, b):
                dve.wait_ge(b_sum, n * 2 + b + 1)
                v.reciprocal(smx[:, 32:48], smx[:, 16:32]).then_inc(b_rec, 1)

            def probs_lo(n, b):
                dve.wait_ge(b_phi, n * 2 + b + 1)
                v.scalar_tensor_tensor(out=PP1[:, :, 1, :], in0=E1, scalar=PS, in1=PP1[:, :, 0, :],
                                       op0=ALU.mult, op1=ALU.subtract).then_inc(b_plo, 1)

            def out_scale(n, b):
                dve.wait_ge(b_o, n * 2 + b + 1)
                dve.wait_ge(b_rec, n * 2 + b + 1)
                v.tensor_tensor(on32.rearrange("p (k d) -> p k d", d=16), banks[6][:, 0:256].rearrange("p (k d) -> p k d", d=16),
                                wide(smx[:, 32:48], 16), ALU.mult).then_inc(b_on, 1)

            def out_lo(n, b):
                dve.wait_ge(b_ohi, n * 2 + b + 1)
                v.tensor_tensor(onh[:, b, 1, :], on32, onh[:, b, 0, :], ALU.subtract).then_inc(b_olo, 1)

            def attn_step(n):
                one, two, more = has(n, 1), has(n, 2), has(n, -1)
                less_max(n, 0)
                if n_is_first(n):
                    y_stats(NT - 1)
                if two:
                    expert(n - 2, 5)
                if one:
                    ffn_lo(n - 1)
                if two:
                    expert(n - 2, 6)
                row_sums(n, 0)
                reciprocals(n, 0)
                probs_lo(n, 0)
                if two:
                    expert(n - 2, 7)
                less_max(n, 1)
                if n_is_first(n):
                    y_norm(NT - 1)
                if one:
                    mask_of(n - 1)
                row_sums(n, 1)
                probs_lo(n, 1)
                if one:
                    expert(n - 1, 0)
                out_scale(n, 0)
                out_lo(n, 0)
                reciprocals(n, 1)
                if n_is_first(n):
                    y_add_to_x(NT - 1)
                    norm_stats(dve, attn_stat(1), 1, x_tile(1), True)
                    norm_apply(dve, attn_stat(1), 1, x_tile(1), yn)
                    tile_lo(dve, attn_stat(1), 1, yn)
                if one:
                    expert(n - 1, 1)
                if has(n, -2):
                    norm_stats(dve, attn_stat(n + 2), 1, x_tile(n + 2), True)
                out_scale(n, 1)
                out_lo(n, 1)
                if more:
                    q_lo(n + 1)
                if one:
                    expert(n - 1, 2)
                if more:
                    kv_lo(n + 1)
                if has(n, -2):
                    norm_apply(dve, attn_stat(n + 2), 1, x_tile(n + 2), yn)
                    tile_lo(dve, attn_stat(n + 2), 1, yn, attn_turn(n + 1) + 1)
                if one:
                    expert(n - 1, 3)
                dve.wait_ge(a_y, n + 1)
                xt = x_tile(n)
                v.scalar_tensor_tensor(out=xt, in0=banks[0], scalar=UN2, in1=xt, op0=ALU.mult, op1=ALU.add).then_inc(a_add, 1)
                alone(dve, a_add, n + 1)
                norm_stats(dve, ffn_stat(n), 0, xt, False)
                if one:
                    expert(n - 1, 4)
                norm_apply(dve, ffn_stat(n), 0, xt, yn)

            def ffn_lo(n):
                tile_lo(dve, ffn_stat(n), 0, yn, ffn_turn(n - 1) + 1 if has(n, 1) else 33)

            q_lo(0)
            kv_lo(0)
            attn_step(0)
            dve.wait_ge(be_in, 16)
            attn_step(1)
            with dve.Fori(2, NT - 2) as n:
                attn_step(n)
            attn_step(NT - 2)
            attn_step(NT - 1)
            ffn_lo(NT - 1)
            for e in (5, 6, 7):
                expert(NT - 2, e)
            mask_of(NT - 1)
            for e in range(NE):
                expert(NT - 1, e)


def kernel(**inputs):
    import numpy as np
    import concourse.bacc as bacc
    from concourse.bass_utils import run_bass_kernel_spmd

    a = {k: np.asarray(v) for k, v in inputs.items()}

    def rows(m, k):
        return m.reshape(k, P, m.shape[1]).transpose(1, 0, 2).reshape(P, -1)

    ctx = a["ctx_4096"].reshape(NTOK, D)
    ctxT = np.stack([rows(ctx[c * CH:(c + 1) * CH].T, KC) for c in range(NC)])
    Wq, Wkv, Wo = a["L0_xattn_Wq"], a["L0_xattn_Wkv"], a["L0_xattn_Wo"]
    wB = np.stack([np.concatenate([
        rows(Wq[:, g * 512:(g + 1) * 512], KC),
        rows(np.concatenate([Wkv[:, g * P:(g + 1) * P], Wkv[:, 1024 + g * P:1024 + (g + 1) * P]], 1), KC),
        rows(Wo[g * 512:(g + 1) * 512], HG)], 1) for g in range(NG)])
    biasB = np.concatenate([a["L0_xattn_bq"].reshape(32, P).T, a["L0_xattn_bkv"].reshape(16, P).T], 1)
    wo1 = a["L1_xattn_wo"].T.reshape(NG, 2, 2, HD1, D)
    wo1 = wo1.transpose(0, 3, 2, 1, 4).reshape(P, 4 * D)
    arrays = {
        "x": a["x"].reshape(NTOK, D), "ctxT": ctxT, "wB": wB, "biasB": biasB,
        "bo": a["L0_xattn_bo"].reshape(1, D),
        "up": rows(a["L0_ffn_up_w"], KC), "down": rows(a["L0_ffn_down_w"], INT // P),
        "small0": np.concatenate([rows(a["L0_ffn_fc1_w"], KC), rows(a["L0_ffn_expert_w"], 2),
                                  rows(a["L0_ffn_gate_w"], KC)], 1),
        "fc2": rows(a["L0_ffn_fc2_w"], 2),
        "gam": a["L0_ffn_ln_gamma"].reshape(1, D), "bet": a["L0_ffn_ln_beta"].reshape(1, D),
        "wq1": rows(a["L1_xattn_wq"].T, KC),
        "wkv1": np.concatenate([rows(np.concatenate([a["L1_xattn_wk"], a["L1_xattn_wv"]], 0).T, KC),
                                rows(a["L1_ffn_W_gate"], KC)], 1),
        "wo1": wo1, "lnw": a["L1_xattn_ln_w"].reshape(KC, P).T,
        "we": np.stack([rows(a["L1_ffn_W_e"][e], KC) for e in range(NE)]),
        "be": a["L1_ffn_b_e"].reshape(1, NE * D), "bg": a["L1_ffn_b_gate"].reshape(1, NE),
    }
    arrays = {"in_" + k: np.ascontiguousarray(v) for k, v in arrays.items()}
    nc = bacc.Bacc("TRN2", target_bir_lowering=False, num_devices=1)
    args = [nc.dram_tensor(k, v.shape, mybir.dt.from_np(v.dtype), kind="ExternalInput").ap() for k, v in arrays.items()]
    args.append(nc.dram_tensor("out_0", (NTOK, D), F32, kind="ExternalOutput").ap())
    build(nc, *args)
    r = run_bass_kernel_spmd(nc, [arrays], core_ids=[0])
    return r.results[0]["out_0"].reshape(32, 64, D)
```
